# Optimizing a Trainium2 kernel written in Bass

```python
import numpy as np
import jax
import jax.numpy as jnp

def _softmax(x, axis=-1):
    return jax.nn.softmax(x, axis=axis)

def _gelu(x):
    return jax.nn.gelu(x, approximate=True)

def _silu(x):
    return jax.nn.silu(x)

def _sigmoid(x):
    return jax.nn.sigmoid(x)

def _layernorm(x, axis=-1, eps=1e-05):
    m = jnp.mean(x, axis=axis, keepdims=True)
    v = jnp.var(x, axis=axis, keepdims=True)
    return (x - m) / jnp.sqrt(v + eps)

def _scatter_add(tgt, idx, src, axis=0):
    return tgt.at[idx].add(src)

def _segment_sum(src, seg, n):
    return jax.ops.segment_sum(src, seg, n)
kernel_name = 'mk_gnn_preln_d4_gnn_r32_cb0b83'

def setup_inputs(seed: int=0):
    np.random.seed(seed)
    _w = jnp.asarray

    def _rec_inputs():
        import jax
        import jax.numpy as jnp
        _gk = jax.random.key(seed)
        x = -0.0002117 + 1 * jax.random.normal(jax.random.fold_in(_gk, 1), (3125, 256), jnp.float32)
        _s = jax.random.randint(jax.random.fold_in(_gk, 2), (25000,), 0, 3125, jnp.int32)
        _d = jax.random.randint(jax.random.fold_in(_gk, 3), (25000,), 0, 3125, jnp.int32)
        _loop = jnp.arange(3125, dtype=jnp.int32)
        src = jnp.concatenate([_s, _d, _loop])
        dst = jnp.concatenate([_d, _s, _loop])
        _o = jnp.argsort(dst, stable=True)
        src = src[_o]
        dst = dst[_o]
        edge_attr_16 = 0.000130101 + 1.00012 * jax.random.normal(jax.random.fold_in(_gk, 12), (53125, 16), jnp.float32)
        edge_weight = jax.random.uniform(jax.random.fold_in(_gk, 15), (53125,), jnp.float32, 0.0, 1)
        edge_weight1 = jax.random.uniform(jax.random.fold_in(_gk, 16), (53125, 1), jnp.float32, 0.0, 1)
        return (x, src, dst, edge_attr_16, edge_weight, edge_weight1)
    x, src, dst, edge_attr_16, edge_weight, edge_weight1 = _rec_inputs()

    def _L0_gnn_setup():
        import jax, jax.numpy as jnp
        import numpy as np
        N_NODES = 3125
        N_EDGES = 100000
        IN_FT = 256
        OUT_FT = 256
        key = jax.random.key(seed)
        k1, k2, k3, k4, k5 = jax.random.split(key, 5)
        seq = jax.random.normal(k1, (N_NODES, IN_FT), dtype=jnp.float32)
        edge_row = jax.random.randint(k2, (N_EDGES,), 0, N_NODES, dtype=jnp.int32)
        edge_col = jax.random.randint(k3, (N_EDGES,), 0, N_NODES, dtype=jnp.int32)
        edge_vals = jax.random.uniform(k4, (N_EDGES,), dtype=jnp.float32)
        std = 1.414 * np.sqrt(2.0 / (IN_FT + OUT_FT))
        W = jax.random.normal(k5, (OUT_FT, IN_FT), dtype=jnp.float32) * std
        bias = jnp.zeros((OUT_FT,), dtype=jnp.float32)
        return {'seq': seq, 'edge_row': edge_row, 'edge_col': edge_col, 'edge_vals': edge_vals, 'W': W, 'bias': bias}
    _L0_gnn_all = _L0_gnn_setup()
    _L0_gnn_in = {k: v for k, v in _L0_gnn_all.items() if k in ('W', 'bias')}
    del _L0_gnn_all

    def _L1_gnn_setup():
        import jax, jax.numpy as jnp
        import numpy as np
        BS = 512
        EMBED = 256
        NHEAD = 8
        HDIM = EMBED // NHEAD
        E = BS * BS

        def _xavier(key, shape):
            lim = float(np.sqrt(6.0 / (shape[0] + shape[1])))
            return jax.random.uniform(key, shape, jnp.float32, -lim, lim)
        key = jax.random.key(seed)
        ks = jax.random.split(key, 6)
        feats = jax.random.normal(ks[0], (BS, EMBED), jnp.float32)
        dst = jnp.repeat(jnp.arange(BS), BS)
        src = jnp.tile(jnp.arange(BS), BS)
        edge_index = jnp.stack([src, dst], axis=1).astype(jnp.int32)
        edge_attr = jnp.zeros((E, 1), jnp.float32)
        return {'feats': feats, 'edge_index': edge_index, 'edge_attr': edge_attr, 'Wq': _xavier(ks[1], (EMBED, EMBED)), 'bq': jnp.zeros((EMBED,), jnp.float32), 'Wk': _xavier(ks[2], (EMBED, EMBED)), 'bk': jnp.zeros((EMBED,), jnp.float32), 'Wv': _xavier(ks[3], (EMBED, EMBED)), 'bv': jnp.zeros((EMBED,), jnp.float32), 'Wo': _xavier(ks[4], (EMBED, EMBED)), 'bo': jnp.zeros((EMBED,), jnp.float32)}
    _L1_gnn_all = _L1_gnn_setup()
    _L1_gnn_in = {k: v for k, v in _L1_gnn_all.items() if k in ('Wq', 'bq', 'Wk', 'bk', 'Wv', 'bv', 'Wo', 'bo')}
    del _L1_gnn_all

    def _L2_gnn_setup():
        import jax, jax.numpy as jnp
        import numpy as np
        N, E = (50000, 25000)
        IN, H, C = (256, 8, 32)
        NEG_SLOPE = 0.2
        EPS = 1e-05
        key = jax.random.key(seed)
        ks = jax.random.split(key, 6)
        x = jax.random.normal(ks[0], (N, IN), jnp.float32)
        edge_index = jax.random.randint(ks[1], (2, E), 0, N, dtype=jnp.int32)
        W = jax.random.normal(ks[2], (IN, H * C), jnp.float32) / np.sqrt(IN).astype(np.float32)
        att_src = jax.random.normal(ks[3], (H, C), jnp.float32) * 0.1
        att_dst = jax.random.normal(ks[4], (H, C), jnp.float32) * 0.1
        bias = jnp.zeros((H * C,), jnp.float32)
        gamma = jnp.ones((H * C,), jnp.float32)
        beta = jnp.zeros((H * C,), jnp.float32)
        return {'x': x, 'edge_index': edge_index, 'W': W, 'att_src': att_src, 'att_dst': att_dst, 'bias': bias, 'gamma': gamma, 'beta': beta}
    _L2_gnn_all = _L2_gnn_setup()
    _L2_gnn_in = {k: v for k, v in _L2_gnn_all.items() if k in ('W', 'att_src', 'att_dst', 'bias', 'gamma', 'beta')}
    del _L2_gnn_all

    def _L3_gnn_setup():
        import jax, jax.numpy as jnp
        import numpy as np
        N, NODE_DIM, EDGE_DIM, HIDDEN, E = (10000, 256, 16, 512, 10000)
        key = jax.random.key(seed)
        ks = jax.random.split(key, 12)

        def lin(kw, kb, fan_in, fan_out):
            bound = 1.0 / np.sqrt(fan_in)
            W = jax.random.uniform(kw, (fan_in, fan_out), jnp.float32, -bound, bound)
            b = jax.random.uniform(kb, (fan_out,), jnp.float32, -bound, bound)
            return (W, b)
        node_features = jax.random.normal(ks[0], (N, NODE_DIM), jnp.float32)
        edge_index = jax.random.randint(ks[1], (2, E), 0, N, jnp.int32)
        edge_features = jax.random.normal(ks[2], (E, EDGE_DIM), jnp.float32)
        mW1, mb1 = lin(ks[3], ks[4], 2 * NODE_DIM + EDGE_DIM, HIDDEN)
        mW2, mb2 = lin(ks[5], ks[6], HIDDEN, NODE_DIM)
        uW1, ub1 = lin(ks[7], ks[8], 2 * NODE_DIM, HIDDEN)
        uW2, ub2 = lin(ks[9], ks[10], HIDDEN, NODE_DIM)
        return {'node_features': node_features, 'edge_index': edge_index, 'edge_features': edge_features, 'mW1': mW1, 'mb1': mb1, 'mW2': mW2, 'mb2': mb2, 'uW1': uW1, 'ub1': ub1, 'uW2': uW2, 'ub2': ub2}
    _L3_gnn_all = _L3_gnn_setup()
    _L3_gnn_in = {k: v for k, v in _L3_gnn_all.items() if k in ('mW1', 'mb1', 'mW2', 'mb2', 'uW1', 'ub1', 'uW2', 'ub2')}
    del _L3_gnn_all
    return {'x': x, 'src': src, 'dst': dst, 'edge_attr_16': edge_attr_16, 'edge_weight': edge_weight, 'edge_weight1': edge_weight1, 'L0_gnn_W': _L0_gnn_in['W'], 'L0_gnn_bias': _L0_gnn_in['bias'], 'L1_gnn_Wq': _L1_gnn_in['Wq'], 'L1_gnn_bq': _L1_gnn_in['bq'], 'L1_gnn_Wk': _L1_gnn_in['Wk'], 'L1_gnn_bk': _L1_gnn_in['bk'], 'L1_gnn_Wv': _L1_gnn_in['Wv'], 'L1_gnn_bv': _L1_gnn_in['bv'], 'L1_gnn_Wo': _L1_gnn_in['Wo'], 'L1_gnn_bo': _L1_gnn_in['bo'], 'L2_gnn_W': _L2_gnn_in['W'], 'L2_gnn_att_src': _L2_gnn_in['att_src'], 'L2_gnn_att_dst': _L2_gnn_in['att_dst'], 'L2_gnn_bias': _L2_gnn_in['bias'], 'L2_gnn_gamma': _L2_gnn_in['gamma'], 'L2_gnn_beta': _L2_gnn_in['beta'], 'L3_gnn_mW1': _L3_gnn_in['mW1'], 'L3_gnn_mb1': _L3_gnn_in['mb1'], 'L3_gnn_mW2': _L3_gnn_in['mW2'], 'L3_gnn_mb2': _L3_gnn_in['mb2'], 'L3_gnn_uW1': _L3_gnn_in['uW1'], 'L3_gnn_ub1': _L3_gnn_in['ub1'], 'L3_gnn_uW2': _L3_gnn_in['uW2'], 'L3_gnn_ub2': _L3_gnn_in['ub2']}

def reference(x, src, dst, edge_attr_16, edge_weight, edge_weight1, L0_gnn_W, L0_gnn_bias, L1_gnn_Wq, L1_gnn_bq, L1_gnn_Wk, L1_gnn_bk, L1_gnn_Wv, L1_gnn_bv, L1_gnn_Wo, L1_gnn_bo, L2_gnn_W, L2_gnn_att_src, L2_gnn_att_dst, L2_gnn_bias, L2_gnn_gamma, L2_gnn_beta, L3_gnn_mW1, L3_gnn_mb1, L3_gnn_mW2, L3_gnn_mb2, L3_gnn_uW1, L3_gnn_ub1, L3_gnn_uW2, L3_gnn_ub2):
    import jax
    import jax.numpy as jnp

    def _L0_gnn_ref(seq, edge_row, edge_col, edge_vals, W, bias):
        import jax, jax.numpy as jnp
        import numpy as np
        N_NODES = 3125
        N_EDGES = 100000
        IN_FT = 256
        OUT_FT = 256
        seq_fts = jnp.einsum('ni,oi->no', seq, W)
        messages = edge_vals[:, None] * seq_fts[edge_col]
        out = jax.ops.segment_sum(messages, edge_row, num_segments=N_NODES)
        return jax.nn.relu(out + bias)

    def _L1_gnn_ref(feats, edge_index, edge_attr, Wq, bq, Wk, bk, Wv, bv, Wo, bo):
        import jax, jax.numpy as jnp
        import numpy as np
        BS = 512
        EMBED = 256
        NHEAD = 8
        HDIM = EMBED // NHEAD
        E = BS * BS

        def _xavier(key, shape):
            lim = float(np.sqrt(6.0 / (shape[0] + shape[1])))
            return jax.random.uniform(key, shape, jnp.float32, -lim, lim)
        bs = feats.shape[0]
        scale = 1.0 / np.sqrt(HDIM)
        q = (feats @ Wq.T + bq).reshape(bs, NHEAD, HDIM).transpose(1, 0, 2)
        k = (feats @ Wk.T + bk).reshape(bs, NHEAD, HDIM).transpose(1, 0, 2)
        v = (feats @ Wv.T + bv).reshape(bs, NHEAD, HDIM).transpose(1, 0, 2)
        r, c = (edge_index[:, 0], edge_index[:, 1])
        qe = q[:, c, :]
        ke = k[:, r, :]
        ve = v[:, r, :]
        sim = jnp.einsum('hed,hed->eh', qe, ke) * scale
        m = jax.ops.segment_max(sim, c, num_segments=bs)
        p = jnp.exp(sim - m[c])
        s = jax.ops.segment_sum(p, c, num_segments=bs)
        attn = p / s[c]
        out_e = attn.T[..., None] * ve
        out_e = out_e.transpose(1, 0, 2).reshape(-1, NHEAD * HDIM)
        agg = jax.ops.segment_sum(out_e, c, num_segments=bs)
        return agg @ Wo.T + bo

    def _L2_gnn_ref(x, edge_index, W, att_src, att_dst, bias, gamma, beta):
        import jax, jax.numpy as jnp
        import numpy as np
        N, E = (50000, 25000)
        IN, H, C = (256, 8, 32)
        NEG_SLOPE = 0.2
        EPS = 1e-05
        n = x.shape[0]
        xl = (x @ W).reshape(n, H, C)
        a_src = jnp.einsum('nhc,hc->nh', xl, att_src)
        a_dst = jnp.einsum('nhc,hc->nh', xl, att_dst)
        loops = jnp.arange(n, dtype=edge_index.dtype)
        src = jnp.concatenate([edge_index[0], loops])
        dst = jnp.concatenate([edge_index[1], loops])
        logits = jax.nn.leaky_relu(a_src[src] + a_dst[dst], NEG_SLOPE)
        seg_max = jax.ops.segment_max(logits, dst, num_segments=n)
        ex = jnp.exp(logits - seg_max[dst])
        denom = jax.ops.segment_sum(ex, dst, num_segments=n)
        alpha = ex / denom[dst]
        msgs = xl[src] * alpha[:, :, None]
        out = jax.ops.segment_sum(msgs, dst, num_segments=n).reshape(n, H * C) + bias
        mu = jnp.mean(out, axis=-1, keepdims=True)
        var = jnp.var(out, axis=-1, keepdims=True)
        return (out - mu) / jnp.sqrt(var + EPS) * gamma + beta

    def _L3_gnn_ref(node_features, edge_index, edge_features, mW1, mb1, mW2, mb2, uW1, ub1, uW2, ub2):
        import jax, jax.numpy as jnp
        import numpy as np
        N, NODE_DIM, EDGE_DIM, HIDDEN, E = (10000, 256, 16, 512, 10000)
        i_idx = edge_index[0]
        j_idx = edge_index[1]
        node_i = node_features[i_idx]
        node_j = node_features[j_idx]
        msg_input = jnp.concatenate([node_i, node_j, edge_features], axis=-1)
        h = jax.nn.relu(msg_input @ mW1 + mb1)
        messages = h @ mW2 + mb2
        aggregated = jax.ops.segment_sum(messages, i_idx, num_segments=node_features.shape[0])
        update_input = jnp.concatenate([node_features, aggregated], axis=-1)
        u = jax.nn.relu(update_input @ uW1 + ub1)
        updated = u @ uW2 + ub2
        return node_features + updated
    edge_index = jnp.stack([src, dst])
    edge_index_t = jnp.stack([src, dst], axis=1)
    h = jnp.maximum(_layernorm(x, axis=-1), 0.0)
    x = x + _L0_gnn_ref(h, src, dst, edge_weight, L0_gnn_W, L0_gnn_bias)
    h = jnp.maximum(_layernorm(x, axis=-1), 0.0)
    x = x + _L1_gnn_ref(h, edge_index_t, edge_weight1, L1_gnn_Wq, L1_gnn_bq, L1_gnn_Wk, L1_gnn_bk, L1_gnn_Wv, L1_gnn_bv, L1_gnn_Wo, L1_gnn_bo)
    h = jnp.maximum(_layernorm(x, axis=-1), 0.0)
    x = x + _L2_gnn_ref(h, edge_index, L2_gnn_W, L2_gnn_att_src, L2_gnn_att_dst, L2_gnn_bias, L2_gnn_gamma, L2_gnn_beta)
    h = jnp.maximum(_layernorm(x, axis=-1), 0.0)
    x = x + _L3_gnn_ref(h, edge_index, edge_attr_16, L3_gnn_mW1, L3_gnn_mb1, L3_gnn_mW2, L3_gnn_mb2, L3_gnn_uW1, L3_gnn_ub1, L3_gnn_uW2, L3_gnn_ub2)
    return x

_drawn_inputs = setup_inputs


def setup_inputs(seed=0):
    import zlib

    import numpy as np

    out = dict(_drawn_inputs(seed))
    spreads = {'L0_gnn_bias': (0.0, 0.433),
     'L1_gnn_bq': (0.0, 2.0),
     'L1_gnn_bk': (0.0, 2.0),
     'L1_gnn_bv': (0.0, 0.398),
     'L1_gnn_bo': (0.0, 0.391),
     'L2_gnn_bias': (0.0, 0.1),
     'L2_gnn_gamma': (1.0, 0.2),
     'L2_gnn_beta': (0.0, 0.353)}
    factors = {'edge_attr_16': 8.0,
     'L1_gnn_Wq': 8.0,
     'L1_gnn_Wk': 8.0,
     'L2_gnn_att_src': 8.0,
     'L2_gnn_att_dst': 30.613,
     'L3_gnn_mb1': 8.0,
     'L3_gnn_mb2': 3.994,
     'L3_gnn_ub1': 29.895,
     'L3_gnn_ub2': 8.0}
    for name, (base, spread) in spreads.items():
        noise = np.random.default_rng([zlib.crc32(name.encode()), seed]).standard_normal(out[name].shape)
        drawn = base * np.exp(spread * noise) if base else spread * noise
        out[name] = jnp.asarray(drawn.astype(out[name].dtype))
    for name, factor in factors.items():
        out[name] = (out[name] * factor).astype(out[name].dtype)
    return out
```

```python
from contextlib import ExitStack

import concourse.bass as bass
from concourse import mybir

ALU = mybir.AluOpType
ACT = mybir.ActivationFunctionType
AX_X = mybir.AxisListType.X
F32 = mybir.dt.float32
BF16 = mybir.dt.bfloat16
I32 = mybir.dt.int32

P = 128
N = 3125
D = 256
H = 8
C = D // H
E = 53125
EA = 16
HID = 512
EP = 125
EC = E // EP
T = 26
TR = (N + P - 1) // P
NP = T * P
LAST = N - (TR - 1) * P
G = 4
NC = -(-(E + TR * (P - 1)) // P)
NC = -(-NC // (2 * G)) * 2 * G
IT = NC // (2 * G)
NB = 16
BC = 28
NCB = NB * BC
assert E == EP * EC and NCB >= NC
RA = 2
RB = EA + 3
BIG = 1e30
EPS = 1e-5
KC = D // P
SC = 5


class Chain:

    def __init__(self, eng, sem):
        self.eng, self.sem, self.n = eng, sem, 0

    def __call__(self, instruction):
        self.n += 1
        instruction.then_inc(self.sem, 1)
        self.eng.wait_ge(self.sem, self.n)


def rounds(eng, n, body):
    body(0, True)
    with eng.Fori(1, n) as i:
        body(i, False)


def at(start, size):
    return bass.ds(start, size)


def phase(build):
    def run(nc, *args, **settings):
        mine = []

        def new_semaphore(name):
            mine.append(nc.alloc_semaphore(name=name))
            return mine[-1]
        build(nc, new_semaphore, *args, **settings)
        while resting:
            nc.release_semaphore(resting.pop())
        numbers = [s.num for s in mine]
        nc.clear_and_free_semaphores(mine)
        resting.extend(nc.alloc_semaphore(name=f"resting{n}", num=n) for n in numbers)
    return run


resting = []


@phase
def setup_phase(nc, new_semaphore, k):
    with ExitStack() as tmp:
        def sb(name, shape, dt):
            return tmp.enter_context(nc.sbuf_tensor(name, shape, dt))

        src_i = sb("src_i", [EP, EC], I32)
        dst_i = sb("dst_i", [EP, EC], I32)
        weight_f = sb("weight_f", [EP, EC], F32)
        tile_i = sb("tile_i", [EP, EC], I32)
        tile_f = sb("tile_f", [EP, EC], F32)
        is_tile = sb("is_tile", [EP, TR, EC], BF16)
        running = sb("running", [EP, TR, EC], F32)
        attr_f = running[:, :, :].rearrange("p t c -> p (t c)")[:, 0:EC * EA].rearrange("p (c a) -> p c a", a=EA)
        go_on = sb("go_on", [EP, TR, EC], BF16)
        tile_ids = sb("tile_ids", [P, TR], F32)
        counts = sb("counts", [EP, TR], F32)
        before = sb("before", [P, P], F32)
        ones = sb("ones_pp", [P, P], F32)
        total_i = sb("total_i", [P, TR], I32)
        chunks_f = sb("chunks_f", [P, TR], F32)
        ends_f = sb("ends_f", [P, TR], F32)
        base_f = sb("base_f", [P, TR], F32)
        zeros_t = sb("zeros_t", [P, TR], F32)
        first_f = sb("first_f", [EP, TR], F32)
        pos_f = sb("pos_f", [EP, EC], F32)
        chunk_ids = sb("chunk_ids", [P, NC], F32)
        past = sb("past", [P, NC // 4, TR - 1], F32)
        pad_a = sb("pad_a", [P, NC, RA], F32)
        pad_b = sb("pad_b", [P, NC // 8, RB], F32)
        ps_before = tmp.enter_context(nc.psum_tensor("ps_before", [EP, 2, TR], F32))
        ps_total = tmp.enter_context(nc.psum_tensor("ps_total", [P, 2, TR], F32))

        def sem(name):
            return new_semaphore(name)

        s_edges = sem("s_edges")
        s_x = sem("s_x")
        s_pool = sem("s_pool")
        s_dve = sem("s_dve")
        s_mask = sem("s_mask")
        s_counts = sem("s_counts")
        s_totals = sem("s_totals")
        s_is = sem("s_is")
        s_copied = sem("s_copied")
        s_fields = sem("s_fields")
        s_rec = sem("s_rec")
        s_pad = sem("s_pad")
        s_filled = sem("s_filled")

        with nc.Block() as block:
            @block.sync
            def _(sp):
                sp.dma_start(dst_i[:, :], k.dst.rearrange("(p c) -> p c", p=EP)).then_inc(s_edges, 16)
                sp.dma_start(src_i[:, :], k.src.rearrange("(p c) -> p c", p=EP)).then_inc(s_edges, 16)
                sp.dma_start(weight_f[:, :], k.edge_weight.rearrange("(p c) -> p c", p=EP)).then_inc(s_edges, 16)
                sp.dma_start(attr_f, k.edge_attr.rearrange("(p c) a -> p c a", p=EP)).then_inc(s_edges, 16)
                sp.wait_ge(s_pool, 1)
                sp.dma_start(k.x[:, 0:TR - 1, :], k.x_in[0:(TR - 1) * P, :].rearrange("(t p) d -> p t d", p=P)).then_inc(s_x, 16)
                sp.dma_start(k.x[0:LAST, TR - 1, :], k.x_in[(TR - 1) * P:N, :]).then_inc(s_x, 16)
                sp.wait_ge(s_x, 32)

            @block.gpsimd
            def _(pool):
                nc.gpsimd.memset(k.x[:, TR - 1:T, :], 0.0).then_inc(s_pool, 1)
                nc.gpsimd.memset(ones[:, :], 1.0).then_inc(s_pool, 1)
                nc.gpsimd.iota(tile_ids[:, :], [[1, TR]], base=0, channel_multiplier=0,
                               allow_small_or_imprecise_dtypes=True).then_inc(s_pool, 1)
                nc.gpsimd.iota(chunk_ids[:, :], [[1, NC]], base=0, channel_multiplier=0,
                               allow_small_or_imprecise_dtypes=True).then_inc(s_pool, 1)
                nc.gpsimd.iota(k.lane[:, :], [[1, P]], base=0, channel_multiplier=0,
                               allow_small_or_imprecise_dtypes=True).then_inc(s_pool, 1)
                pool.wait_ge(s_pool, 2)
                nc.gpsimd.affine_select(out=before[:, :], in_=ones[:, :], compare_op=ALU.is_gt, fill=0.0, base=0,
                                        pattern=[[1, P]], channel_multiplier=-1).then_inc(s_pool, 1)
                nc.gpsimd.affine_select(out=k.ident[:, :], in_=ones[:, :], compare_op=ALU.is_equal, fill=0.0, base=0,
                                        pattern=[[1, P]], channel_multiplier=-1).then_inc(s_pool, 1)
                nc.gpsimd.memset(pad_a[:, :, :], 0.0).then_inc(s_pad, 1)
                nc.gpsimd.memset(pad_b[:, :, :], 0.0).then_inc(s_pad, 1)
                pool.wait_ge(s_pad, 2)
                nc.gpsimd.memset(pad_a[:, :, 1:2], -1.0).then_inc(s_pad, 1)
                nc.gpsimd.memset(pad_b[:, :, EA + 1:EA + 2], -1.0).then_inc(s_pad, 1)

            @block.scalar
            def _(act):
                act.wait_ge(s_pad, 4)
                act.dma_start(k.rec_a.rearrange("(p c) r -> p c r", p=P), pad_a[:, :, :]).then_inc(s_filled, 16)
                for n in range(8):
                    rows = NC // 8 * P
                    act.dma_start(k.rec_b[n * rows:(n + 1) * rows, :].rearrange("(p c) r -> p c r", p=P),
                                  pad_b[:, :, :]).then_inc(s_filled, 16)
                act.dma_start(k.rec_b[NC * P:, :].rearrange("(p c) r -> p c r", p=P),
                              pad_b[:, 0:G, :]).then_inc(s_filled, 16)
                act.wait_ge(s_edges, 64)
                nc.scalar.copy(k.fields_b[:, :, EA + 2], weight_f[:, :]).then_inc(s_rec, 1)
                nc.scalar.copy(k.fields_b[:, :, 0:EA], attr_f).then_inc(s_rec, 1)
                act.wait_ge(s_rec, 2)
                for n in range(2):
                    act.wait_ge(s_is, n + 1)
                    nc.scalar.copy(running[:, :, :], is_tile[:, :, :]).then_inc(s_copied, 1)
                act.wait_ge(s_pool, 7)
                nc.scalar.copy(k.ident_b[:, :], k.ident[:, :]).then_inc(s_rec, 1)
                act.wait_ge(s_filled, 160)

            @block.tensor
            def _(pe):
                pe.wait_ge(s_pool, 6)
                for n in range(2):
                    pe.wait_ge(s_counts, n + 1)
                    nc.tensor.matmul(ps_before[:, n, :], before[0:EP, 0:EP], counts[:, :], start=True, stop=True)
                    nc.tensor.matmul(ps_total[:, n, :], ones[0:EP, :], counts[:, :], start=True,
                                     stop=True).then_inc(s_totals, 1)

            @block.vector
            def _(dve):
                step = Chain(dve, s_dve)
                step(nc.vector.memset(go_on[:, :, :], 1.0))
                step(nc.vector.memset(go_on[:, :, 0:1], 0.0))
                step(nc.vector.memset(zeros_t[:, :], 0.0))
                dve.wait_ge(s_edges, 64)
                dve.wait_ge(s_pool, 5)
                step(nc.vector.tensor_copy(k.fields_a[:, :, 0], src_i[:, :]))
                step(nc.vector.tensor_copy(k.fields_a[:, :, 1], dst_i[:, :]))
                step(nc.vector.tensor_copy(k.fields_b[:, :, EA], dst_i[:, :]))
                step(nc.vector.tensor_copy(k.fields_b[:, :, EA + 1], src_i[:, :]))
                for n, (key, pos, tile_of) in enumerate(((dst_i, k.pos_a, k.tile_a), (src_i, k.pos_b, k.tile_b))):
                    step(nc.vector.tensor_single_scalar(tile_i[:, :], key[:, :], 7, ALU.arith_shift_right))
                    step(nc.vector.tensor_copy(tile_f[:, :], tile_i[:, :]))
                    nc.vector.tensor_tensor(is_tile[:, :, :], tile_f[:, :].unsqueeze(1).to_broadcast([EP, TR, EC]),
                                            tile_ids[0:EP, :].unsqueeze(2).to_broadcast([EP, TR, EC]),
                                            ALU.is_equal).then_inc(s_is, 1)
                    dve.wait_ge(s_is, n + 1)
                    nc.vector.tensor_reduce(counts[:, :], is_tile[:, :, :], AX_X, ALU.add).then_inc(s_counts, 1)
                    dve.wait_ge(s_totals, n + 1)
                    step(nc.vector.tensor_scalar(chunks_f[:, :], ps_total[:, n, :], float(P - 1), None, ALU.add))
                    step(nc.vector.tensor_copy(total_i[:, :], chunks_f[:, :]))
                    step(nc.vector.tensor_single_scalar(total_i[:, :], total_i[:, :], 7, ALU.arith_shift_right))
                    step(nc.vector.tensor_copy(chunks_f[:, :], total_i[:, :]))
                    step(nc.vector.tensor_tensor_scan(ends_f[:, :], chunks_f[:, :], zeros_t[:, :], 0.0, ALU.add, ALU.add))
                    step(nc.vector.tensor_tensor(base_f[:, :], ends_f[:, :], chunks_f[:, :], ALU.subtract))
                    step(nc.vector.scalar_tensor_tensor(first_f[:, :], base_f[0:EP, :], float(P), ps_before[:, n, :],
                                                        ALU.mult, ALU.add))
                    dve.wait_ge(s_copied, n + 1)
                    step(nc.vector.tensor_tensor(running[:, :, 0], is_tile[:, :, 0], first_f[:, :], ALU.add))
                    step(nc.vector.tensor_tensor_scan(running[:, :, :].rearrange("p t c -> p (t c)"),
                                                      go_on[:, :, :].rearrange("p t c -> p (t c)"),
                                                      running[:, :, :].rearrange("p t c -> p (t c)"),
                                                      0.0, ALU.mult, ALU.add))
                    step(nc.vector.tensor_tensor(running[:, :, :], running[:, :, :], is_tile[:, :, :], ALU.mult))
                    step(nc.vector.tensor_reduce(pos_f[:, :], running[:, :, :].rearrange("p t c -> p c t"), AX_X, ALU.add))
                    step(nc.vector.tensor_scalar(pos[:, :], pos_f[:, :], -1.0, None, ALU.add))
                    for q in range(4):
                        part = slice(q * NC // 4, (q + 1) * NC // 4)
                        step(nc.vector.tensor_tensor(past[:, :, :],
                                                     chunk_ids[:, part].unsqueeze(2).to_broadcast([P, NC // 4, TR - 1]),
                                                     ends_f[:, 0:TR - 1].unsqueeze(1).to_broadcast([P, NC // 4, TR - 1]),
                                                     ALU.is_ge))
                        step(nc.vector.tensor_reduce(tile_of[:, part], past[:, :, :], AX_X, ALU.add))
                step(nc.vector.tensor_copy(k.tile_ia[:, :], k.tile_a[0:1, :]))
                step(nc.vector.tensor_copy(k.tile_ib[:, :], k.tile_b[0:1, :]))


@phase
def scatter_phase(nc, new_semaphore, k):
    def sem(name):
        return new_semaphore(name)

    with ExitStack() as tmp:
        def sb(name, shape, dt):
            return tmp.enter_context(nc.sbuf_tensor(name, shape, dt))

        at_a = sb("at_a", [EP, SC], I32)
        at_b = sb("at_b", [EP, SC], I32)
        row_a = sb("row_a", [EP, SC, RA], F32)
        row_b = sb("row_b", [EP, SC, RB], F32)
        s_at = sem("s_at")
        s_row = sem("s_row")
        s_go = sem("s_go")
        s_done = [sem(f"s_scattered{j}") for j in range(SC)]

        with nc.Block() as block:
            @block.vector
            def _(dve):
                def columns(i, first):
                    for j in range(SC):
                        if not first:
                            dve.wait_ge(s_done[j], 32 * i)
                        nc.vector.tensor_copy(at_a[:, j:j + 1], k.pos_a[:, at(i * SC + j, 1)])
                        nc.vector.tensor_copy(at_b[:, j:j + 1], k.pos_b[:, at(i * SC + j, 1)]).then_inc(s_at, 1)
                rounds(dve, EC // SC, columns)

            @block.scalar
            def _(act):
                def columns(i, first):
                    for j in range(SC):
                        if not first:
                            act.wait_ge(s_done[j], 32 * i)
                        nc.scalar.copy(row_a[:, j:j + 1, :], k.fields_a[:, at(i * SC + j, 1), :])
                        nc.scalar.copy(row_b[:, j:j + 1, :], k.fields_b[:, at(i * SC + j, 1), :]).then_inc(s_row, 1)
                rounds(act, EC // SC, columns)

            @block.gpsimd
            def _(pool):
                def columns(i, first):
                    for j in range(SC):
                        pool.wait_ge(s_at, i * SC + j + 1)
                        pool.wait_ge(s_row, i * SC + j + 1)
                        pool.sem_inc(s_go, 1)
                        pool.indirect_dma_start(k.rec_a, bass.IndirectOffsetOnAxis(at_a[:, j:j + 1], 0),
                                                row_a[:, j, :], None).then_inc(s_done[j], 16)
                        pool.indirect_dma_start(k.rec_b, bass.IndirectOffsetOnAxis(at_b[:, j:j + 1], 0),
                                                row_b[:, j, :], None).then_inc(s_done[j], 16)
                rounds(pool, EC // SC, columns)
                for j in range(SC):
                    pool.wait_ge(s_done[j], 32 * (EC // SC))



@phase
def load_order_phase(nc, new_semaphore, k):
    def sem(name):
        return new_semaphore(name)

    with ExitStack() as tmp:
        def sb(name, shape, dt):
            return tmp.enter_context(nc.sbuf_tensor(name, shape, dt))

        rec = sb("rec_sb", [P, NC, RA], F32)
        rec_b = sb("rec_b_sb", [P, NC, RB - EA], F32)
        key = sb("key", [P, NCB], F32)
        key_turn = sb("key_turn", [P, 2, P], F32)
        key_rows = sb("key_rows", [P, 1 + BC * P], F32)
        ps_turn = tmp.enter_context(nc.psum_tensor("ps_key_turn", [P, 2, 512], F32))
        s_rec = sem("s_rec_sb")
        s_rec_b = sem("s_rec_b_sb")
        s_step = sem("s_order_step")
        s_key = sem("s_key")
        s_staged = sem("s_key_staged")
        s_turned = sem("s_key_turned")
        s_row = sem("s_key_row")
        s_shift = sem("s_key_shift")
        s_flag = sem("s_flag")
        s_ahead = sem("s_ahead")

        with nc.Block() as block:
            @block.sync
            def _(sp):
                sp.dma_start(rec[:, :, :], k.rec_a.rearrange("(c p) r -> p c r", p=P)).then_inc(s_rec, 16)
                sp.dma_start(rec_b[:, :, :], k.rec_b[0:NC * P, EA:RB].rearrange("(c p) r -> p c r", p=P)).then_inc(s_rec_b, 16)
                sp.wait_ge(s_row, BC + 1)
                sp.dma_start(key_rows[1:P, 0:1], key_rows[0:P - 1, BC * P:BC * P + 1]).then_inc(s_shift, 16)
                sp.wait_ge(s_flag, 2)
                sp.dma_start(k.new_node[0:P - 1, BC * P:BC * P + 1], k.new_node[1:P, 0:1]).then_inc(s_ahead, 16)
                sp.wait_ge(s_ahead, 16)

            @block.scalar
            def _(act):
                act.wait_ge(s_key, 1)

                def turn(i, first):
                    for u in range(2):
                        g = 2 * i + u
                        if not first:
                            act.wait_ge(s_turned, g - 1)
                        nc.scalar.copy(key_turn[:, u, :].rearrange("p (h b) -> p h b", h=H),
                                       key[:, :].rearrange("p (b g) -> p g b", g=BC)[:, at(g, 1), :]
                                       .to_broadcast([P, H, NB])).then_inc(s_staged, 1)
                rounds(act, BC // 2, turn)

            @block.tensor
            def _(pe):
                def turn(i, first):
                    for u in range(2):
                        g = 2 * i + u
                        pe.wait_ge(s_staged, g + 1)
                        if not first:
                            pe.wait_ge(s_row, g)
                        nc.tensor.transpose(ps_turn[:, u, 0:P], key_turn[:, u, :], k.ident[:, :]).then_inc(s_turned, 1)
                rounds(pe, BC // 2, turn)

            @block.vector
            def _(dve):
                step = Chain(dve, s_step)
                step(nc.vector.memset(key[:, NC:NCB], -1.0))
                step(nc.vector.memset(k.scores[:, NC:NCB, :], 0.0))
                for column in (k.src_at, k.dst_at, k.lane_a, k.lane_b):
                    step(nc.vector.memset(column[:, NC:NC + G], 0))
                nc.vector.memset(key_rows[:, 0:1], -2.0).then_inc(s_row, 1)
                step(nc.vector.memset(k.new_node[:, BC * P:BC * P + 1], -BIG))
                dve.wait_ge(s_rec, 16)
                nc.vector.tensor_copy(key[:, 0:NC], rec[:, :, 1]).then_inc(s_key, 1)
                step(nc.vector.tensor_copy(k.src_at[:, 0:NC], rec[:, :, 0]))
                step(nc.vector.scalar_tensor_tensor(k.lane_a[:, 0:NC], k.tile_a[:, :], -float(P), rec[:, :, 1],
                                                    ALU.mult, ALU.add))
                dve.wait_ge(s_rec_b, 16)
                step(nc.vector.tensor_copy(k.dst_at[:, 0:NC], rec_b[:, :, 0]))
                step(nc.vector.tensor_copy(k.weight[:, :], rec_b[:, :, 2]))
                step(nc.vector.scalar_tensor_tensor(k.lane_b[:, 0:NC], k.tile_b[:, :], -float(P), rec_b[:, :, 1],
                                                    ALU.mult, ALU.add))

                def turn(i, first):
                    for u in range(2):
                        g = 2 * i + u
                        dve.wait_ge(s_turned, g + 1)
                        nc.vector.tensor_copy(key_rows[:, at(g * P + 1, P)], ps_turn[:, u, 0:P]).then_inc(s_row, 1)
                rounds(dve, BC // 2, turn)
                dve.wait_ge(s_shift, 16)
                dve.wait_ge(s_row, BC + 1)
                nc.vector.tensor_tensor(k.new_node[:, 0:BC * P], key_rows[:, 1:], key_rows[:, 0:BC * P],
                                        ALU.not_equal).then_inc(s_flag, 1)
                dve.wait_ge(s_flag, 1)
                nc.vector.tensor_scalar(k.new_node[:, 0:BC * P], k.new_node[:, 0:BC * P], -BIG, None,
                                        ALU.mult).then_inc(s_flag, 1)


@phase
def weights_phase(nc, new_semaphore, k, a):
    def sem(name):
        return new_semaphore(name)

    turned = [(a['L0_gnn_W'], k.w0), (a['L1_gnn_Wq'], k.wqkv[:, :, 0:D]), (a['L1_gnn_Wk'], k.wqkv[:, :, D:2 * D]),
              (a['L1_gnn_Wv'], k.wqkv[:, :, 2 * D:3 * D]), (a['L1_gnn_Wo'], k.wo)]
    rows = [(a['L0_gnn_bias'], k.b0), (a['L1_gnn_bq'], k.bqkv[:, 0:D]), (a['L1_gnn_bk'], k.bqkv[:, D:2 * D]),
            (a['L1_gnn_bv'], k.bqkv[:, 2 * D:3 * D]), (a['L1_gnn_bo'], k.bo), (a['L2_gnn_bias'], k.b2),
            (a['L2_gnn_gamma'], k.gamma), (a['L2_gnn_beta'], k.beta),
            (a['L2_gnn_att_src'].rearrange("h c -> (h c)"), k.att_src),
            (a['L2_gnn_att_dst'].rearrange("h c -> (h c)"), k.att_dst)]
    with ExitStack() as tmp:
        w = tmp.enter_context(nc.sbuf_tensor("w_raw", [P, len(turned), KC, D], F32))
        ps = tmp.enter_context(nc.psum_tensor("ps_w", [P, KC, KC, P], F32))
        s_w = sem("s_w_raw")
        s_rows = sem("s_w_rows")
        s_turn = sem("s_w_turned")
        s_kept = sem("s_w_kept")
        with nc.Block() as block:
            @block.sync
            def _(sp):
                for n, (source, _) in enumerate(turned):
                    sp.dma_start(w[:, n, :, :], source.rearrange("(o p) i -> p o i", p=P)).then_inc(s_w, 16)
                sp.dma_start(k.w2[:, :, :], a['L2_gnn_W'].rearrange("(o p) i -> p o i", p=P)).then_inc(s_rows, 16)
                for source, row in rows:
                    sp.dma_start(row[:, :], source.partition_broadcast(P)).then_inc(s_rows, 16)
                sp.wait_ge(s_rows, 16 * (1 + len(rows)))

            @block.tensor
            def _(pe):
                pe.wait_ge(s_w, 16 * len(turned))
                for n in range(len(turned)):
                    if n:
                        pe.wait_ge(s_kept, n)
                    for o in range(KC):
                        for i in range(KC):
                            ins = nc.tensor.transpose(ps[:, i, o, :], w[:, n, o, i * P:(i + 1) * P], k.ident[:, :])
                    ins.then_inc(s_turn, 1)

            @block.vector
            def _(dve):
                for n, (_, kept) in enumerate(turned):
                    dve.wait_ge(s_turn, n + 1)
                    nc.vector.tensor_copy(kept[:, :, :], ps[:, :, :, :].rearrange("p i o q -> p i (o q)")).then_inc(s_kept, 1)


class RoundChain:

    def __init__(self, eng, sem):
        self.eng, self.sem, self.per = eng, sem, 0

    def start(self, i, first):
        self.base, self.n = (0 if first else i * self.per), 0

    def __call__(self, instruction):
        self.n += 1
        self.per = max(self.per, self.n)
        instruction.then_inc(self.sem, 1)
        self.eng.wait_ge(self.sem, self.base + self.n)


@phase
def norm_stats(nc, new_semaphore, k, name, rows):
    def sem(what):
        return new_semaphore(f"{name}_{what}")

    with ExitStack() as tmp:
        stats = tmp.enter_context(nc.sbuf_tensor(f"{name}_stats", [P, 2, 6], F32))
        mv1 = tmp.enter_context(nc.sbuf_tensor(f"{name}_mv1", [P, 2, 2], F32))
        mv = tmp.enter_context(nc.sbuf_tensor(f"{name}_mv", [P, T, 2], F32))
        var = tmp.enter_context(nc.sbuf_tensor(f"{name}_var", [P, T], F32))
        dev = tmp.enter_context(nc.sbuf_tensor(f"{name}_dev", [P, T], F32))
        s_stats = sem("stats")
        s_aggr = sem("aggr")
        s_hold = sem("hold")
        s_mv = sem("mv")
        s_step = sem("step")
        s_var = sem("var")
        s_dev = sem("dev")
        with nc.Block() as block:
            @block.vector
            def _(dve):
                def tiles(i, first):
                    for u in range(2):
                        nc.vector.bn_stats(stats[:, u, :], rows[:, at(2 * i + u, 1), :]
                                           .rearrange("p o d -> p (o d)")).then_inc(s_stats, 1)
                    for u in range(2):
                        dve.wait_ge(s_stats, 2 * i + u + 1)
                        dve.sem_inc(s_hold, 1)
                        nc.vector.bn_aggr(mv1[:, u, :], stats[:, u, :]).then_inc(s_aggr, 1)
                    for u in range(2):
                        dve.wait_ge(s_aggr, 2 * i + u + 1)
                        nc.vector.tensor_copy(mv[:, at(2 * i + u, 1), :], mv1[:, u:u + 1, :]).then_inc(s_mv, 1)
                    dve.wait_ge(s_mv, 2 * i + 2)
                rounds(dve, T // 2, tiles)
                step = Chain(dve, s_step)
                nc.vector.tensor_scalar(var[:, :], mv[:, :, 1], EPS, None, ALU.add).then_inc(s_var, 1)
                dve.wait_ge(s_dev, 1)
                step(nc.vector.reciprocal(k.rstd[:, :], dev[:, :]))
                step(nc.vector.scalar_tensor_tensor(k.shift[:, :], mv[:, :, 0], -1.0, k.rstd[:, :], ALU.mult, ALU.mult))

            @block.scalar
            def _(act):
                act.wait_ge(s_var, 1)
                nc.scalar.activation(dev[:, :], var[:, :], ACT.Sqrt).then_inc(s_dev, 1)


def tile_ap(rows, t):
    return rows[:, at(t, 1), :].rearrange("p o d -> p (o d)")


@phase
def project_phase(nc, new_semaphore, k, name, blocks, width, weights, prepare, finish, prepare_on="act", keep=None, store=None,
                  setup=None):
    def sem(what):
        return new_semaphore(f"{name}_{what}")

    banks = -(-width // 512)
    with ExitStack() as tmp:
        rows = tmp.enter_context(nc.sbuf_tensor(f"{name}_rows", [P, 2, blocks * P], F32))
        cols = tmp.enter_context(nc.sbuf_tensor(f"{name}_cols", [P, 2, blocks, P], F32))
        slots = tmp.enter_context(nc.sbuf_tensor(f"{name}_slots", [P, 2, 3 * D], F32))
        spare = tmp.enter_context(nc.sbuf_tensor(f"{name}_spare", [P, 2, 2, 2 * D], F32))
        ps_turn = tmp.enter_context(nc.psum_tensor(f"{name}_ps_turn", [P, 2, 4, P], F32))
        ps_out = tmp.enter_context(nc.psum_tensor(f"{name}_ps_out", [P, 2, banks * 512], F32))
        s_setup = sem("setup")
        s_rows = sem("rows")
        s_turned = sem("turned")
        s_cols = sem("cols")
        s_out = sem("out")
        s_done = sem("done")
        s_prep = sem("prep_step")
        s_step = sem("step")
        s_kept = [sem(f"kept{u}") for u in range(2)]
        s_stored = [sem(f"stored{u}") for u in range(2)]
        stores = len(store(0, slots[:, 0, :])) if store else 0

        def prepare_rows(eng, chain, i, first):
            for u in range(2):
                t = 2 * i + u
                if not first:
                    eng.wait_ge(s_turned, t - 1)
                    if keep:
                        eng.wait_ge(s_kept[u], 16 * i)
                prepare(chain, t, u, rows[:, u, :]).then_inc(s_rows, 1)

        with nc.Block() as block:
            @block.scalar
            def _(act):
                if prepare_on == "act":
                    chain = RoundChain(act, s_prep)

                    def tiles(i, first):
                        chain.start(i, first)
                        prepare_rows(act, chain, i, first)
                    rounds(act, T // 2, tiles)

            @block.vector
            def _(dve):
                if setup:
                    setup(Chain(dve, s_setup))
                chain = RoundChain(dve, s_step)

                def tiles(i, first):
                    chain.start(i, first)
                    if prepare_on == "dve":
                        prepare_rows(dve, chain, i, first)
                    for u in range(2):
                        dve.wait_ge(s_turned, 2 * i + u + 1)
                        if not first:
                            dve.wait_ge(s_out, 2 * i + u - 1)
                        nc.vector.tensor_copy(cols[:, u, :, :], ps_turn[:, u, 0:blocks, :]).then_inc(s_cols, 1)
                    for u in range(2):
                        dve.wait_ge(s_out, 2 * i + u + 1)
                        if stores and not first:
                            dve.wait_ge(s_stored[u], 16 * stores * i)
                        finish(chain, 2 * i + u, ps_out[:, u, 0:width], slots[:, u, :], spare[:, u, :, :])\
                            .then_inc(s_done, 1)
                rounds(dve, T // 2, tiles)

            @block.tensor
            def _(pe):
                def tiles(i, first):
                    for u in range(2):
                        pe.wait_ge(s_rows, 2 * i + u + 1)
                        if not first:
                            pe.wait_ge(s_cols, 2 * i + u - 1)
                        for b in range(blocks):
                            ins = nc.tensor.transpose(ps_turn[:, u, b, :], rows[:, u, b * P:(b + 1) * P], k.ident[:, :])
                        ins.then_inc(s_turned, 1)
                    for u in range(2):
                        pe.wait_ge(s_cols, 2 * i + u + 1)
                        if not first:
                            pe.wait_ge(s_done, 2 * i + u - 1)
                        for w0 in range(0, width, 512):
                            w1 = min(width, w0 + 512)
                            for b in range(blocks):
                                ins = nc.tensor.matmul(ps_out[:, u, w0:w1], cols[:, u, b, :], weights[:, b, w0:w1],
                                                       start=(b == 0), stop=(b == blocks - 1))
                        ins.then_inc(s_out, 1)
                rounds(pe, T // 2, tiles)

            @block.sync
            def _(sp):
                if keep:
                    def keeps(i, first):
                        for u in range(2):
                            sp.wait_ge(s_rows, 2 * i + u + 1)
                            sp.dma_start(keep(2 * i + u), rows[:, u, 0:D]).then_inc(s_kept[u], 16)
                        if store:
                            put(i)

                if store:
                    def put(i):
                        for u in range(2):
                            sp.wait_ge(s_done, 2 * i + u + 1)
                            for to, what in store(2 * i + u, slots[:, u, :]):
                                sp.dma_start(to, what).then_inc(s_stored[u], 16)
                if keep:
                    rounds(sp, T // 2, keeps)
                elif store:
                    rounds(sp, T // 2, lambda i, first: put(i))
                for u in range(2):
                    if keep:
                        sp.wait_ge(s_kept[u], 16 * (T // 2))
                    if store:
                        sp.wait_ge(s_stored[u], 16 * stores * (T // 2))


def rows_of(dram, t):
    return dram[at(t * P, P), :]


@phase
def store_norm_phase(nc, new_semaphore, k, table):
    def sem(name):
        return new_semaphore(name)

    with ExitStack() as tmp:
        h = tmp.enter_context(nc.sbuf_tensor("h0", [P, T, D], F32))
        s_h = sem("s_h0")
        s_out = sem("s_h0_out")
        with nc.Block() as block:
            @block.scalar
            def _(act):
                def tiles(i, first):
                    for u in range(2):
                        t = 2 * i + u
                        nc.scalar.activation(tile_ap(h, t), tile_ap(k.x, t), ACT.Relu, bias=k.shift[:, at(t, 1)],
                                             scale=k.rstd[:, at(t, 1)]).then_inc(s_h, 1)
                rounds(act, T // 2, tiles)

            @block.sync
            def _(sp):
                sp.wait_ge(s_h, T // 2)
                sp.dma_start(table[0:T // 2 * P, :].rearrange("(t p) d -> p t d", p=P), h[:, 0:T // 2, :]).then_inc(s_out, 16)
                sp.wait_ge(s_h, T)
                sp.dma_start(table[T // 2 * P:, :].rearrange("(t p) d -> p t d", p=P), h[:, T // 2:, :]).then_inc(s_out, 16)
                sp.wait_ge(s_out, 32)


def tile_registers(nc, eng, tiles, c, size):
    return nc.values_load_multi_w_load_instructions(
        tiles[0:1, at(c, size)], [eng], min_val=0, max_val=T - 1,
        skip_runtime_bounds_check_because="a count of at most TR - 1 tiles")[1]


def gather_rounds(pool, k, s_idx, s_go, s_landed, idx, gathered, table, free):
    def groups(i, first):
        for u in range(2):
            g = 2 * i + u
            if not first:
                free(u, g)
            pool.wait_ge(s_idx, g + 1)
            pool.sem_inc(s_go, 1)
            for j in range(G):
                pool.indirect_dma_start(gathered[:, u, j, :], None, table,
                                        bass.IndirectOffsetOnAxis(idx[:, u, j:j + 1], 0)).then_inc(s_landed[u], 16)
    rounds(pool, IT, groups)


def stage_index(nc, act, i, first, u, idx, source, s_landed, s_idx):
    g = 2 * i + u
    if first and u == 0:
        nc.scalar.copy(idx[:, 0, :], source[:, at(0, G)]).then_inc(s_idx, 1)
    else:
        act.wait_ge(s_landed[1 - u], 16 * G * (i + u))
    nc.scalar.copy(idx[:, 1 - u, :], source[:, at((g + 1) * G, G)]).then_inc(s_idx, 1)


@phase
def score_phase(nc, new_semaphore, k, name, table, width, parts):
    def sem(what):
        return new_semaphore(f"{name}_{what}")

    dots = width == D
    with ExitStack() as tmp:
        def sb(what, shape, dt):
            return tmp.enter_context(nc.sbuf_tensor(f"{name}_{what}", shape, dt))

        idx = sb("idx", [P, 2, G], I32)
        gathered = sb("gathered", [P, 2, G, width], F32)
        is_lane = sb("is_lane", [P, 2, G, P], BF16)
        lane_is = sb("lane_is", [P, 2, G, P], BF16)
        products = sb("products", [P, 2, G, width], F32)
        ps_turn = tmp.enter_context(nc.psum_tensor(f"{name}_ps_turn", [P, 2, 2 * G, P], BF16))
        ps_rows = tmp.enter_context(nc.psum_tensor(f"{name}_ps_rows", [P, 2, G, max(width, D)], F32))
        s_idx = sem("idx")
        s_go = sem("go")
        s_landed = [sem(f"landed{u}") for u in range(2)]
        s_lane = sem("lane")
        s_turned = sem("turned")
        s_cols = sem("cols")
        s_rows = sem("rows")
        s_prod = sem("prod")
        s_score = sem("score")

        with nc.Block() as block:
            @block.scalar
            def _(act):
                def columns(g, u, n):
                    act.wait_ge(s_turned, g + 1)
                    if n >= 2:
                        act.wait_ge(s_rows, g - 1)
                    nc.scalar.copy(lane_is[:, u, :, :], ps_turn[:, u, 0:G, :]).then_inc(s_cols, 1)

                def groups(i, first):
                    if first:
                        columns(0, 0, 0)
                    for u in range(2):
                        stage_index(nc, act, i, first, u, idx, k.src_at, s_landed, s_idx)
                        columns(2 * i + u + 1, 1 - u, u + 1 if first else 2)
                rounds(act, IT, groups)

            @block.gpsimd
            def _(pool):
                gather_rounds(pool, k, s_idx, s_go, s_landed, idx, gathered, table,
                              lambda u, g: pool.wait_ge(s_prod, g - 1))

            @block.tensor
            def _(pe):
                def turn(g, u, n):
                    pe.wait_ge(s_lane, g + 1)
                    if n >= 2:
                        pe.wait_ge(s_cols, g - 1)
                    for j in range(G):
                        ins = nc.tensor.transpose(ps_turn[:, u, j, :], is_lane[:, u, j, :], k.ident_b[:, :])
                    ins.then_inc(s_turned, 1)

                def groups(i, first):
                    if first:
                        turn(0, 0, 0)
                    for u in range(2):
                        g = 2 * i + u
                        turn(g + 1, 1 - u, u + 1 if first else 2)
                        tiles = tile_registers(nc, mybir.EngineType.PE, k.tile_ia, g * G, G)
                        pe.wait_ge(s_cols, g + 1)
                        if not first:
                            pe.wait_ge(s_prod, g - 1)
                        for j in range(G):
                            for part in range(3):
                                ins = nc.tensor.matmul(ps_rows[:, u, j, 0:width], lane_is[:, u, j, :],
                                                       parts[:, at(tiles[j], 1), part, :],
                                                       start=(part == 0), stop=(part == 2))
                        ins.then_inc(s_rows, 1)
                rounds(pe, IT, groups)

            @block.vector
            def _(dve):
                def lanes(g, u, n):
                    if n >= 2:
                        dve.wait_ge(s_turned, g - 1)
                    nc.vector.tensor_tensor(is_lane[:, u, :, :], k.lane[:, :].unsqueeze(1).to_broadcast([P, G, P]),
                                            k.lane_a[:, at(g * G, G)].unsqueeze(2).to_broadcast([P, G, P]),
                                            ALU.is_equal).then_inc(s_lane, 1)

                def groups(i, first):
                    if first:
                        lanes(0, 0, 0)
                    for u in range(2):
                        g = 2 * i + u
                        lanes(g + 1, 1 - u, u + 1 if first else 2)
                        dve.wait_ge(s_landed[u], 16 * G * (i + 1))
                        dve.wait_ge(s_rows, g + 1)
                        if not first:
                            dve.wait_ge(s_score, g - 1)
                        nc.vector.tensor_tensor(products[:, u, :, :], gathered[:, u, :, :], ps_rows[:, u, :, 0:width],
                                                ALU.mult if dots else ALU.add).then_inc(s_prod, 1)
                        dve.wait_ge(s_prod, g + 1)
                        scores = k.scores[:, at(g * G, G), :]
                        if dots:
                            nc.vector.tensor_reduce(scores, products[:, u, :, :].rearrange("p j (h c) -> p j h c", h=H),
                                                    AX_X, ALU.add).then_inc(s_score, 1)
                        else:
                            nc.vector.scalar_tensor_tensor(scores, products[:, u, :, :], 0.2, products[:, u, :, :],
                                                           ALU.mult, ALU.max).then_inc(s_score, 1)
                rounds(dve, IT, groups)


@phase
def weights_of_edges_phase(nc, new_semaphore, k, name, scale, last=None):
    def sem(what):
        return new_semaphore(f"{name}_{what}")

    L = BC * P
    with ExitStack() as tmp:
        def sb(what, shape, dt):
            return tmp.enter_context(nc.sbuf_tensor(f"{name}_{what}", shape, dt))

        stage = sb("stage", [P, 2, P], F32)
        line = sb("line", [P, BC, P], F32)
        run = sb("run", [P, L], F32)
        only_last = sb("only_last", [P, BC, P], F32) if last is not None else None
        kill = sb("kill", [P, 2], F32)
        end = sb("end", [P, 1], F32)
        row = sb("row", [1, 2, P], F32)
        chain_row = sb("chain_row", [1, P + 2], F32)
        carry = sb("carry", [P, 1], F32)
        ps_turn = tmp.enter_context(nc.psum_tensor(f"{name}_ps_turn", [P, 2, 512], F32))
        ps_row = tmp.enter_context(nc.psum_tensor(f"{name}_ps_row", [1, 2, P], F32))
        ps_carry = tmp.enter_context(nc.psum_tensor(f"{name}_ps_carry", [P, 2], F32))
        s_stage = sem("stage")
        s_turned = sem("turned")
        s_line = sem("line")
        s_step = sem("step")
        s_ends = sem("ends")
        s_endrow = sem("endrow")
        s_chain = sem("chain")
        s_carry = sem("carry")
        s_max = sem("max")
        s_bstage = sem("bstage")
        s_bturned = sem("bturned")
        s_less = sem("less")
        whole = line[:, :, :].rearrange("p g e -> p (g e)")
        by_block = k.scores[:, :, :].rearrange("p (b g) h -> p g b h", g=BC)
        backs = 2 if last is not None else 1
        flag = k.new_node

        with nc.Block() as block:
            @block.scalar
            def _(act):
                def there(i, first):
                    for u in range(2):
                        g = 2 * i + u
                        if not first:
                            act.wait_ge(s_turned, g - 1)
                        nc.scalar.copy(stage[:, u, :].rearrange("p (h b) -> p h b", h=H),
                                       by_block[:, at(g, 1), :, :].rearrange("p o b h -> p (o h) b")).then_inc(s_stage, 1)
                rounds(act, BC // 2, there)
                act.wait_ge(s_max, 1)
                for back, source in enumerate([line, only_last][:backs]):
                    def here(i, first):
                        for u in range(2):
                            n = back * BC + 2 * i + u
                            if not first or back:
                                act.wait_ge(s_bturned, n - 1)
                            nc.scalar.copy(stage[:, u, :], tile_ap(source, 2 * i + u)).then_inc(s_bstage, 1)
                    act.wait_ge(s_turned, BC)
                    rounds(act, BC // 2, here)
                act.wait_ge(s_less, backs * BC)
                nc.scalar.activation(k.scores[:, :, :], k.scores[:, :, :], ACT.Exp, scale=scale)

            @block.tensor
            def _(pe):
                def there(i, first):
                    for u in range(2):
                        g = 2 * i + u
                        pe.wait_ge(s_stage, g + 1)
                        if not first:
                            pe.wait_ge(s_line, g - 1)
                        nc.tensor.transpose(ps_turn[:, u, 0:P], stage[:, u, :], k.ident[:, :]).then_inc(s_turned, 1)
                rounds(pe, BC // 2, there)
                for n in range(2):
                    pe.wait_ge(s_ends, n + 1)
                    nc.tensor.transpose(ps_row[:, 0, :], kill[:, n:n + 1], k.ident[:, :])
                    nc.tensor.transpose(ps_row[:, 1, :], end[:, :], k.ident[:, :]).then_inc(s_endrow, 1)
                    pe.wait_ge(s_chain, n + 1)
                    nc.tensor.transpose(ps_carry[:, n:n + 1], chain_row[0:1, 2 * n:2 * n + P],
                                        k.ident[0:1, 0:1]).then_inc(s_carry, 1)
                for back in range(backs):
                    def here(i, first):
                        for u in range(2):
                            n = back * BC + 2 * i + u
                            pe.wait_ge(s_bstage, n + 1)
                            if not first or back:
                                pe.wait_ge(s_less, n - 1)
                            nc.tensor.transpose(ps_turn[:, u, 0:P], stage[:, u, :], k.ident[:, :]).then_inc(s_bturned, 1)
                    pe.wait_ge(s_line, BC)
                    rounds(pe, BC // 2, here)

            @block.vector
            def _(dve):
                def there(i, first):
                    for u in range(2):
                        g = 2 * i + u
                        dve.wait_ge(s_turned, g + 1)
                        nc.vector.tensor_copy(tile_ap(line, g), ps_turn[:, u, 0:P]).then_inc(s_line, 1)
                rounds(dve, BC // 2, there)
                step = Chain(dve, s_step)
                dve.wait_ge(s_line, BC)
                for n, (flags, source, target, way, last_at) in enumerate((
                        (flag[:, 0:L], whole, run[:, :], slice(None, None, 1), L - 1),
                        (flag[:, 1:L + 1], run[:, :], whole, slice(None, None, -1), 0))):
                    step(nc.vector.tensor_reduce(kill[:, n:n + 1], flags, AX_X, ALU.min))
                    step(nc.vector.tensor_tensor_scan(target[:, way], flags[:, way], source[:, way], -BIG, ALU.add, ALU.max))
                    nc.vector.tensor_copy(end[:, :], target[:, last_at:last_at + 1]).then_inc(s_ends, 1)
                    step(nc.vector.memset(chain_row[:, :], -BIG))
                    dve.wait_ge(s_endrow, n + 1)
                    step(nc.vector.tensor_copy(row[:, :, :], ps_row[:, :, :]))
                    nc.vector.tensor_tensor_scan(chain_row[:, 1:P + 1][:, way], row[:, 0, :][:, way], row[:, 1, :][:, way],
                                                 -BIG, ALU.add, ALU.max).then_inc(s_chain, 1)
                    dve.wait_ge(s_carry, n + 1)
                    step(nc.vector.tensor_copy(carry[:, :], ps_carry[:, n:n + 1]))
                    step(nc.vector.tensor_tensor_scan(target[:, way], flags[:, way], source[:, way], carry[:, :],
                                                      ALU.add, ALU.max))
                if last is not None:
                    step(nc.vector.scalar_tensor_tensor(only_last[:, :, :].rearrange("p g e -> p (g e)"),
                                                        flag[:, 1:L + 1], -1.0, whole, ALU.is_lt, ALU.mult))
                dve.sem_inc(s_max, 1)
                for back in range(backs):
                    def here(i, first):
                        for u in range(2):
                            g = 2 * i + u
                            dve.wait_ge(s_bturned, back * BC + g + 1)
                            turned = ps_turn[:, u, 0:P].rearrange("p (h b) -> p b h", h=H)
                            mine = by_block[:, at(g, 1), :, :].rearrange("p o b h -> p (o b) h")
                            if back == 0:
                                nc.vector.tensor_tensor(mine, mine, turned, ALU.subtract).then_inc(s_less, 1)
                            else:
                                nc.vector.tensor_copy(last[:, :, :].rearrange("p (b g) h -> p g b h", g=BC)[:, at(g, 1), :, :]
                                                      .rearrange("p o b h -> p (o b) h"), turned).then_inc(s_less, 1)
                    rounds(dve, BC // 2, here)


@phase
def sum_phase(nc, new_semaphore, k, name, table, sums, heads, last=None):
    row_at, lane_of, tile_ids = ((k.src_at, k.lane_a, k.tile_ia) if heads else (k.dst_at, k.lane_b, k.tile_ib))

    def sem(what):
        return new_semaphore(f"{name}_{what}")

    width = sums.shape[2]
    with ExitStack() as tmp:
        def sb(what, shape, dt):
            return tmp.enter_context(nc.sbuf_tensor(f"{name}_{what}", shape, dt))

        idx = sb("idx", [P, 2, G], I32)
        gathered = sb("gathered", [P, 2, G, D], F32)
        is_lane = sb("is_lane", [P, 2, G, P], F32)
        values = sb("values", [P, 2, G, width], F32)
        ps_sums = tmp.enter_context(nc.psum_tensor(f"{name}_ps_sums", [P, 2 * G, 512], F32))
        s_idx = sem("idx")
        s_go = sem("go")
        s_landed = [sem(f"landed{u}") for u in range(2)]
        s_zero = sem("zero")
        s_extra = sem("extra")
        s_values = sem("values")
        s_lane = sem("lane")
        s_sums = sem("sums")
        s_added = sem("added")

        with nc.Block() as block:
            @block.scalar
            def _(act):
                def groups(i, first):
                    for u in range(2):
                        g = 2 * i + u
                        stage_index(nc, act, i, first, u, idx, row_at, s_landed, s_idx)
                        if heads:
                            if not first:
                                act.wait_ge(s_sums, G * (g - 1))
                            ins = nc.scalar.copy(values[:, u, :, D:D + H], k.scores[:, at(g * G, G), :])
                            if last is not None:
                                ins = nc.scalar.copy(values[:, u, :, D + H:D + 2 * H], last[:, at(g * G, G), :])
                            ins.then_inc(s_extra, 1)
                        else:
                            act.wait_ge(s_landed[u], 16 * G * (i + 1))
                            if not first:
                                act.wait_ge(s_sums, G * (g - 1))
                            for j in range(G):
                                ins = nc.scalar.activation(values[:, u, j, 0:D], gathered[:, u, j, :], ACT.Copy,
                                                           scale=k.weight[:, at(g * G + j, 1)])
                            ins.then_inc(s_values, 1)
                act.wait_ge(s_zero, 2)
                rounds(act, IT, groups)

            @block.gpsimd
            def _(pool):
                gather_rounds(pool, k, s_idx, s_go, s_landed, idx, gathered, table,
                              lambda u, g: pool.wait_ge(s_values, g - 1))

            @block.tensor
            def _(pe):
                def groups(i, first):
                    for u in range(2):
                        g = 2 * i + u
                        pe.wait_ge(s_lane, g + 1)
                        pe.wait_ge(s_values, g + 1)
                        if heads:
                            pe.wait_ge(s_extra, g + 1)
                        for j in range(G):
                            if not first:
                                pe.wait_ge(s_added, G * (g - 2) + j + 1)
                            nc.tensor.matmul(ps_sums[:, G * u + j, 0:width], is_lane[:, u, j, :], values[:, u, j, :],
                                             start=True, stop=True).then_inc(s_sums, 1)
                pe.wait_ge(s_zero, 2)
                rounds(pe, IT, groups)

            @block.vector
            def _(dve):
                nc.vector.memset(sums[:, :, :], 0.0).then_inc(s_zero, 1)
                nc.vector.memset(values[:, :, :, width - 1:width], 1.0).then_inc(s_zero, 1)
                dve.wait_ge(s_zero, 2)

                def make(i, first, u):
                    g = 2 * i + u
                    if not first:
                        dve.wait_ge(s_sums, G * (g - 1))
                    for j in range(G):
                        ins = nc.vector.tensor_scalar(is_lane[:, u, j, :], k.lane[:, :], lane_of[:, at(g * G + j, 1)],
                                                      None, ALU.is_equal)
                    ins.then_inc(s_lane, 1)
                    if heads:
                        dve.wait_ge(s_landed[u], 16 * G * (i + 1))
                        nc.vector.tensor_tensor(
                            values[:, u, :, 0:D].rearrange("p j (h c) -> p j h c", h=H),
                            gathered[:, u, :, :].rearrange("p j (h c) -> p j h c", h=H),
                            k.scores[:, at(g * G, G), :].unsqueeze(3).to_broadcast([P, G, H, C]),
                            ALU.mult).then_inc(s_values, 1)

                def add(i, u, first):
                    g = 2 * i + u
                    tiles = tile_registers(nc, mybir.EngineType.DVE, tile_ids, g * G, G)
                    for j in range(G):
                        dve.wait_ge(s_sums, g * G + j + 1)
                        if not (first and j == 0):
                            dve.wait_ge(s_added, g * G + j)
                        to = tile_ap(sums, tiles[j])
                        nc.vector.tensor_tensor(to, to, ps_sums[:, G * u + j, 0:width], ALU.add).then_inc(s_added, 1)

                def groups(i, first):
                    make(i, first, 0)
                    if not first:
                        add(i - 1, 1, False)
                    make(i, first, 1)
                    add(i, 0, first)
                rounds(dve, IT, groups)
                add(IT - 1, 1, False)



@phase
def combine_loops_phase(nc, new_semaphore, k, sums):
    def sem(name):
        return new_semaphore(name)

    with ExitStack() as tmp:
        def sb(name, shape):
            return tmp.enter_context(nc.sbuf_tensor(name, shape, F32))

        own = sb("own_logit", [P, T, H])
        z = sb("own_z", [P, T, H])
        top = sb("top_logit", [P, T, H])
        old = sb("old_part", [P, T, H])
        new = sb("new_part", [P, T, H])
        s_step = sem("s_loop_step")
        s_less = sem("s_loop_less")
        s_exp = sem("s_loop_exp")
        weight, largest = sums[:, :, D:D + H], sums[:, :, D + H:D + 2 * H]
        rows = sums[:, :, 0:D].rearrange("p t (h c) -> p t h c", h=H)
        xl = k.xl[:, :, :].rearrange("p t (h c) -> p t h c", h=H)

        with nc.Block() as block:
            @block.vector
            def _(dve):
                step = Chain(dve, s_step)
                step(nc.vector.tensor_tensor(z[:, :, :], k.of_src[:, :, :], k.of_dst[:, :, :], ALU.add))
                step(nc.vector.scalar_tensor_tensor(own[:, :, :], z[:, :, :], 0.2, z[:, :, :], ALU.mult, ALU.max))
                step(nc.vector.tensor_scalar(z[:, :, :], weight, 0.5, -BIG, ALU.is_lt, ALU.mult))
                step(nc.vector.tensor_tensor(old[:, :, :], z[:, :, :], largest, ALU.add))
                step(nc.vector.tensor_tensor(top[:, :, :], old[:, :, :], own[:, :, :], ALU.max))
                step(nc.vector.tensor_tensor(old[:, :, :], old[:, :, :], top[:, :, :], ALU.subtract))
                step(nc.vector.tensor_tensor(new[:, :, :], own[:, :, :], top[:, :, :], ALU.subtract))
                dve.sem_inc(s_less, 1)
                dve.wait_ge(s_exp, 2)
                step(nc.vector.tensor_tensor(z[:, :, :], weight, old[:, :, :], ALU.mult))
                step(nc.vector.tensor_tensor(z[:, :, :], z[:, :, :], new[:, :, :], ALU.add))
                step(nc.vector.reciprocal(top[:, :, :], z[:, :, :]))
                step(nc.vector.tensor_tensor(old[:, :, :], old[:, :, :], top[:, :, :], ALU.mult))
                step(nc.vector.tensor_tensor(new[:, :, :], new[:, :, :], top[:, :, :], ALU.mult))
                step(nc.vector.tensor_tensor(xl, xl, new[:, :, :].unsqueeze(3).to_broadcast([P, T, H, C]), ALU.mult))
                step(nc.vector.tensor_tensor(rows, rows, old[:, :, :].unsqueeze(3).to_broadcast([P, T, H, C]), ALU.mult))
                step(nc.vector.tensor_tensor(k.xl[:, :, :], k.xl[:, :, :], sums[:, :, 0:D], ALU.add))
                step(nc.vector.tensor_tensor(k.xl[:, :, :], k.xl[:, :, :], k.b2[:, :].unsqueeze(1).to_broadcast([P, T, D]),
                                             ALU.add))

            @block.scalar
            def _(act):
                act.wait_ge(s_less, 1)
                nc.scalar.activation(old[:, :, :], old[:, :, :], ACT.Exp).then_inc(s_exp, 1)
                nc.scalar.activation(new[:, :, :], new[:, :, :], ACT.Exp).then_inc(s_exp, 1)


@phase
def norm_of_layer_phase(nc, new_semaphore, k):
    s_step = new_semaphore("s_norm2_step")
    s_scaled = new_semaphore("s_norm2_scaled")
    with nc.Block() as block:
        @block.scalar
        def _(act):
            def tiles(i, first):
                for u in range(2):
                    t = 2 * i + u
                    nc.scalar.activation(tile_ap(k.xl, t), tile_ap(k.xl, t), ACT.Identity, bias=k.shift[:, at(t, 1)],
                                         scale=k.rstd[:, at(t, 1)]).then_inc(s_scaled, 1)
            rounds(act, T // 2, tiles)

        @block.vector
        def _(dve):
            step = Chain(dve, s_step)
            step(nc.vector.tensor_tensor(k.x[:, :, :], k.x[:, :, :], k.beta[:, :].unsqueeze(1).to_broadcast([P, T, D]),
                                         ALU.add))
            dve.wait_ge(s_scaled, T)
            step(nc.vector.tensor_tensor(k.xl[:, :, :], k.xl[:, :, :], k.gamma[:, :].unsqueeze(1).to_broadcast([P, T, D]),
                                         ALU.mult))
            step(nc.vector.tensor_tensor(k.x[:, :, :], k.x[:, :, :], k.xl[:, :, :], ALU.add))


@phase
def logit_parts_phase(nc, new_semaphore, k):
    s_step = new_semaphore("s_parts_step")
    s_out = new_semaphore("s_of_src_out")
    with ExitStack() as tmp:
        left = tmp.enter_context(nc.sbuf_tensor("parts_left", [P, T, H], F32))
        with nc.Block() as block:
            @block.sync
            def _(sp):
                sp.dma_start(k.of_src_table.rearrange("(t p) h -> p t h", p=P), k.of_src[:, :, :]).then_inc(s_out, 16)
                sp.wait_ge(s_out, 16)

            @block.vector
            def _(dve):
                step = Chain(dve, s_step)
                step(nc.vector.tensor_copy(k.of_dst_parts[:, :, 0, :], k.of_dst[:, :, :]))
                step(nc.vector.tensor_tensor(left[:, :, :], k.of_dst[:, :, :], k.of_dst_parts[:, :, 0, :], ALU.subtract))
                step(nc.vector.tensor_copy(k.of_dst_parts[:, :, 1, :], left[:, :, :]))
                step(nc.vector.tensor_tensor(k.of_dst_parts[:, :, 2, :], left[:, :, :], k.of_dst_parts[:, :, 1, :],
                                             ALU.subtract))


def split_parts(nc, step, parts, t, value, left):
    def part(n):
        return parts[:, at(t, 1), n, :].rearrange("p o d -> p (o d)")
    step(nc.vector.tensor_copy(part(0), value))
    step(nc.vector.tensor_tensor(left, value, part(0), ALU.subtract))
    step(nc.vector.tensor_copy(part(1), left))
    return nc.vector.tensor_tensor(part(2), left, part(1), ALU.subtract)


A_PARTS = (0, 0, 0, 1, 1, 1, 2, 2)
W_PARTS = (0, 1, 2, 0, 1, 2, 0, 1)


@phase
def attribute_weights_phase(nc, new_semaphore, k, a):
    def sem(name):
        return new_semaphore(name)

    with ExitStack() as tmp:
        w = tmp.enter_context(nc.sbuf_tensor("w_attr_raw", [EA, HID], F32))
        left = tmp.enter_context(nc.sbuf_tensor("w_attr_left", [EA, HID], F32))
        parts = tmp.enter_context(nc.sbuf_tensor("w_attr_parts", [EA, 3, HID], BF16))
        s_w = sem("s_w_attr")
        s_step = sem("s_w_attr_step")
        s_split = sem("s_w_attr_split")
        s_stacked = sem("s_w_attr_stacked")
        s_rows = sem("s_w3")
        with nc.Block() as block:
            @block.sync
            def _(sp):
                sp.dma_start(w[:, :], a['L3_gnn_mW1'][2 * D:2 * D + EA, :]).then_inc(s_w, 16)
                for half in range(2):
                    sp.dma_start(k.w_node[:, :, half * HID:(half + 1) * HID],
                                 a['L3_gnn_mW1'][half * D:(half + 1) * D, :].rearrange("(b p) n -> p b n", p=P))\
                        .then_inc(s_rows, 16)
                sp.dma_start(k.b_m1[:, :], a['L3_gnn_mb1'].partition_broadcast(P)).then_inc(s_rows, 16)
                sp.wait_ge(s_split, 1)
                for n, part in enumerate(W_PARTS):
                    sp.dma_start(k.w_attr[n * EA:(n + 1) * EA, :], parts[:, part, :]).then_inc(s_stacked, 16)
                sp.wait_ge(s_stacked, 16 * len(W_PARTS))
                sp.wait_ge(s_rows, 48)

            @block.vector
            def _(dve):
                step = Chain(dve, s_step)
                dve.wait_ge(s_w, 16)
                step(nc.vector.tensor_copy(parts[:, 0, :], w[:, :]))
                step(nc.vector.tensor_tensor(left[:, :], w[:, :], parts[:, 0, :], ALU.subtract))
                step(nc.vector.tensor_copy(parts[:, 1, :], left[:, :]))
                step(nc.vector.tensor_tensor(parts[:, 2, :], left[:, :], parts[:, 1, :], ALU.subtract))
                dve.sem_inc(s_split, 1)


@phase
def message_phase(nc, new_semaphore, k, table, parts, sums):
    def sem(name):
        return new_semaphore(f"m_{name}")

    PAIRS = len(A_PARTS)
    with ExitStack() as tmp:
        def sb(name, shape, dt):
            return tmp.enter_context(nc.sbuf_tensor(f"m_{name}", shape, dt))

        raw = sb("raw", [P, 2, G, EA], F32)
        idx = sb("idx", [P, 2, G], I32)
        gathered = sb("gathered", [P, 2, G, HID], F32)
        hidden = k.x[:, 0:2 * G * HID // D, :].rearrange("p t d -> p (t d)")\
            .rearrange("p (u j f) -> p u j f", u=2, j=G)
        is_lane = sb("is_lane", [P, 2, G, P], F32)
        is_lane_b = sb("is_lane_b", [P, 2, G, P], BF16)
        lane_is = sb("lane_is", [P, 2, G, P], BF16)
        attr = sb("attr", [P, 2, G, PAIRS, EA], BF16)
        attr_turned = sb("attr_turned", [P, 2, G, P], BF16)
        left = sb("left", [P, 2, 2, G, EA], F32)
        ps_turn = tmp.enter_context(nc.psum_tensor("m_ps_turn", [P, 2, 2, G, P], BF16))
        ps_lane, ps_attr = ps_turn[:, :, 0, :, :], ps_turn[:, :, 1, :, :]
        ps_hidden = tmp.enter_context(nc.psum_tensor("m_ps_hidden", [P, 2, HID], F32))
        ps_sums = tmp.enter_context(nc.psum_tensor("m_ps_sums", [P, 2, HID], F32))
        s_raw = [sem(f"raw{u}") for u in range(2)]
        s_idx = sem("idx")
        s_go = sem("go")
        s_landed = [sem(f"landed{u}") for u in range(2)]
        s_zero = sem("zero")
        s_lane = sem("lane")
        s_lane_b = sem("lane_b")
        s_split = sem("split")
        s_split0 = sem("split_first")
        s_attr = sem("attr")
        s_turned = sem("turned")
        s_cols = sem("cols")
        s_ps_hidden = sem("ps_hidden")
        s_added = sem("hidden_added")
        s_hidden = sem("hidden")
        s_ps_sums = sem("ps_sums")
        s_sums = sem("sums")

        with nc.Block() as block:
            @block.sync
            def _(sp):
                def load(g, u, n):
                    if n >= 2:
                        sp.wait_ge(s_attr, g - 1)
                    sp.dma_start(raw[:, u, :, :], k.rec_b[at(g * G * P, G * P), 0:EA]
                                 .rearrange("(j p) r -> p j r", p=P)).then_inc(s_raw[u], 16)

                def groups(i, first):
                    if first:
                        load(0, 0, 0)
                    for u in range(2):
                        load(2 * i + u + 1, 1 - u, u + 1 if first else 2)
                rounds(sp, IT, groups)

            @block.gpsimd
            def _(pool):
                split = RoundChain(pool, s_split)

                def attributes(split, g, u, landed, n):
                    value = raw[:, u, :, :]
                    pool.wait_ge(s_raw[u], 16 * landed)
                    if n >= 2:
                        pool.wait_ge(s_turned, g - 1)
                    pool.sem_inc(s_go, 1)
                    for part in range(3):
                        pairs = [m for m in range(PAIRS) if A_PARTS[m] == part]
                        ins = nc.gpsimd.tensor_copy(attr[:, u, :, pairs[0]:pairs[-1] + 1, :],
                                                    value.unsqueeze(2).to_broadcast([P, G, len(pairs), EA]))
                        if part == 2:
                            ins.then_inc(s_attr, 1)
                            break
                        split(ins)
                        pool.sem_inc(s_go, 1)
                        split(nc.gpsimd.tensor_tensor(left[:, u, part, :, :], value, attr[:, u, :, pairs[0], :],
                                                      ALU.subtract))
                        pool.sem_inc(s_go, 1)
                        value = left[:, u, part, :, :]

                def groups(i, first):
                    split.start(i, first)
                    for u in range(2):
                        g = 2 * i + u
                        pool.wait_ge(s_idx, g + 1)
                        if not first:
                            pool.wait_ge(s_hidden, G * (g - 1))
                        pool.sem_inc(s_go, 1)
                        for j in range(G):
                            pool.indirect_dma_start(gathered[:, u, j, :], None, table,
                                                    bass.IndirectOffsetOnAxis(idx[:, u, j:j + 1], 0))\
                                .then_inc(s_landed[u], 16)
                        attributes(split, g + 1, 1 - u, i + 1 + u, u + 1 if first else 2)

                attributes(Chain(pool, s_split0), 0, 0, 1, 0)
                rounds(pool, IT, groups)

            @block.scalar
            def _(act):
                def narrow(g, u, n):
                    act.wait_ge(s_lane, g + 1)
                    if n >= 2:
                        act.wait_ge(s_turned, g - 1)
                    nc.scalar.copy(is_lane_b[:, u, :, :], is_lane[:, u, :, :]).then_inc(s_lane_b, 1)

                def columns(g, u, n):
                    act.wait_ge(s_turned, g + 1)
                    if n >= 2:
                        act.wait_ge(s_ps_hidden, G * (g - 1))
                    nc.scalar.copy(lane_is[:, u, :, :], ps_lane[:, u, :, :])
                    nc.scalar.copy(attr_turned[:, u, :, :], ps_attr[:, u, :, :]).then_inc(s_cols, 1)

                def groups(i, first):
                    if first:
                        narrow(0, 0, 0)
                        columns(0, 0, 0)
                    for u in range(2):
                        g = 2 * i + u
                        n = u + 1 if first else 2
                        stage_index(nc, act, i, first, u, idx, k.dst_at, s_landed, s_idx)
                        for j in range(G):
                            act.wait_ge(s_added, G * g + j + 1)
                            if not first:
                                act.wait_ge(s_ps_sums, G * (g - 2) + j + 1)
                            nc.scalar.activation(hidden[:, u, j, :], gathered[:, u, j, :], ACT.Relu).then_inc(s_hidden, 1)
                            if j == 1:
                                narrow(g + 1, 1 - u, n)
                            if j == 2:
                                columns(g + 1, 1 - u, n)
                rounds(act, IT, groups)

            @block.tensor
            def _(pe):
                def turn(g, u, n):
                    pe.wait_ge(s_lane_b, g + 1)
                    pe.wait_ge(s_attr, g + 1)
                    if n >= 2:
                        pe.wait_ge(s_cols, g - 1)
                    for j in range(G):
                        nc.tensor.transpose(ps_lane[:, u, j, :], is_lane_b[:, u, j, :], k.ident_b[:, :])
                        ins = nc.tensor.transpose(ps_attr[:, u, j, :], attr[:, u, j, :, :].rearrange("p n a -> p (n a)"),
                                                  k.ident_b[:, :])
                    ins.then_inc(s_turned, 1)

                def product(g, u, j, tile, first):
                    if not (first and u == 0 and j < 2):
                        pe.wait_ge(s_added, g * G + j - 1)
                    for part in range(3):
                        nc.tensor.matmul(ps_hidden[:, j % 2, :], lane_is[:, u, j, :], parts[:, at(tile, 1), part, :],
                                         start=(part == 0), stop=False)
                    nc.tensor.matmul(ps_hidden[:, j % 2, :], attr_turned[:, u, j, :], k.w_attr[:, :],
                                     start=False, stop=True).then_inc(s_ps_hidden, 1)

                def add(g, u, j, begin):
                    c = g * G + j
                    pe.wait_ge(s_hidden, c + 1)
                    if not (begin and j < 2):
                        pe.wait_ge(s_sums, c - 1)
                    nc.tensor.matmul(ps_sums[:, j % 2, :], is_lane[:, u, j, :], hidden[:, u, j, :], start=True,
                                     stop=True).then_inc(s_ps_sums, 1)

                def groups(i, first):
                    if first:
                        turn(0, 0, 0)
                    for u in range(2):
                        g = 2 * i + u
                        tiles = tile_registers(nc, mybir.EngineType.PE, k.tile_ib, g * G, G)
                        pe.wait_ge(s_cols, g + 1)
                        for j in range(G):
                            product(g, u, j, tiles[j], first)
                            if j >= 2:
                                add(g, u, j - 2, first and u == 0)
                            elif not (first and u == 0):
                                add(g - 1, 1 - u, j + 2, False)
                            if j == 2:
                                turn(g + 1, 1 - u, u + 1 if first else 2)
                rounds(pe, IT, groups)
                for j in range(2, G):
                    add(2 * IT - 1, 1, j, False)

            @block.vector
            def _(dve):
                nc.vector.memset(sums[:, :, :], 0.0).then_inc(s_zero, 1)
                dve.wait_ge(s_zero, 1)

                def lanes(g, u, n):
                    if n >= 2:
                        dve.wait_ge(s_ps_sums, G * (g - 1))
                        dve.wait_ge(s_lane_b, g - 1)
                    nc.vector.tensor_tensor(is_lane[:, u, :, :], k.lane[:, :].unsqueeze(1).to_broadcast([P, G, P]),
                                            k.lane_b[:, at(g * G, G)].unsqueeze(2).to_broadcast([P, G, P]),
                                            ALU.is_equal).then_inc(s_lane, 1)

                def add(g, j, tile, begin):
                    c = g * G + j
                    dve.wait_ge(s_ps_sums, c + 1)
                    if not (begin and j == 0):
                        dve.wait_ge(s_sums, c)
                    to = tile_ap(sums, tile)
                    nc.vector.tensor_tensor(to, to, ps_sums[:, j % 2, :], ALU.add).then_inc(s_sums, 1)

                def groups(i, first):
                    if first:
                        lanes(0, 0, 0)
                    for u in range(2):
                        g = 2 * i + u
                        begin = first and u == 0
                        if not begin:
                            before = tile_registers(nc, mybir.EngineType.DVE, k.tile_ib, g * G - 2, 2)
                        tiles = tile_registers(nc, mybir.EngineType.DVE, k.tile_ib, g * G, 2)
                        dve.wait_ge(s_landed[u], 16 * G * (i + 1))
                        for j in range(G):
                            dve.wait_ge(s_ps_hidden, G * g + j + 1)
                            nc.vector.tensor_tensor(gathered[:, u, j, :], gathered[:, u, j, :], ps_hidden[:, j % 2, :],
                                                    ALU.add).then_inc(s_added, 1)
                            if j >= 2:
                                add(g, j - 2, tiles[j - 2], begin)
                            elif not begin:
                                add(g - 1, j + 2, before[j], False)
                            if j == 1:
                                lanes(g + 1, 1 - u, u + 1 if first else 2)
                rounds(dve, IT, groups)
                tiles = tile_registers(nc, mybir.EngineType.DVE, k.tile_ib, NC - 2, 2)
                for j in range(2, G):
                    add(2 * IT - 1, j, tiles[j - 2], False)


@phase
def load_phase(nc, new_semaphore, name, pairs):
    s = new_semaphore(name)
    with nc.Block() as block:
        @block.sync
        def _(sp):
            for to, source in pairs:
                sp.dma_start(to, source).then_inc(s, 16)
            sp.wait_ge(s, 16 * len(pairs))


class Names:
    pass


_IN = ['x', 'src', 'dst', 'edge_attr_16', 'edge_weight', 'edge_weight1', 'L0_gnn_W', 'L0_gnn_bias', 'L1_gnn_Wq',
       'L1_gnn_bq', 'L1_gnn_Wk', 'L1_gnn_bk', 'L1_gnn_Wv', 'L1_gnn_bv', 'L1_gnn_Wo', 'L1_gnn_bo', 'L2_gnn_W',
       'L2_gnn_att_src', 'L2_gnn_att_dst', 'L2_gnn_bias', 'L2_gnn_gamma', 'L2_gnn_beta', 'L3_gnn_mW1', 'L3_gnn_mb1',
       'L3_gnn_mW2', 'L3_gnn_mb2', 'L3_gnn_uW1', 'L3_gnn_ub1', 'L3_gnn_uW2', 'L3_gnn_ub2']


def gnn_layers_kernel(nc, a, out):
    resting.clear()
    with ExitStack() as ctx:
        k = Names()
        k.x_in, k.src, k.dst = a['x'], a['src'], a['dst']
        k.edge_attr, k.edge_weight = a['edge_attr_16'], a['edge_weight']

        def table(name, width):
            return nc.dram_tensor(name, (NP, width), F32).ap()

        k.rec_a = nc.dram_tensor("rec_a", (NC * P, RA), F32).ap()
        k.rec_b = nc.dram_tensor("rec_b", ((NC + G) * P, RB), F32).ap()
        h_table, key_table, value_table = table("h_table", D), table("key_table", D), table("value_table", D)
        xl_table, h3_table, dst_table = table("xl_table", D), table("h3_table", D), table("dst_table", HID)
        k.of_src_table, x_table = table("of_src_table", H), table("x_table", D)

        def sb(name, shape, dt=F32, to=ctx):
            return to.enter_context(nc.sbuf_tensor(name, shape, dt))

        k.x = sb("x_nodes", [P, T, D])
        k.ident = sb("ident", [P, P])
        k.ident_b = sb("ident_b", [P, P], BF16)
        k.lane = sb("lane", [P, P])
        k.tile_a = sb("tile_a", [P, NC])
        k.tile_b = sb("tile_b", [P, NC])
        k.tile_ia = sb("tile_ia", [1, NC], I32)
        k.tile_ib = sb("tile_ib", [1, NC], I32)
        k.dst_at = sb("dst_at", [P, NC + G], I32)
        k.lane_b = sb("lane_b", [P, NC + G])
        k.weight = sb("weight", [P, NC])
        degree = sb("degree", [P, T])
        k.rstd = sb("rstd", [P, T])
        k.shift = sb("shift", [P, T])

        def normed(eng_step, t, u, rows):
            return nc.scalar.activation(rows[:, 0:D], tile_ap(k.x, t), ACT.Relu, bias=k.shift[:, at(t, 1)],
                                        scale=k.rstd[:, at(t, 1)])

        with ExitStack() as edges:
            k.pos_a, k.pos_b = sb("pos_a", [EP, EC], I32, edges), sb("pos_b", [EP, EC], I32, edges)
            k.fields_a, k.fields_b = sb("fields_a", [EP, EC, RA], F32, edges), sb("fields_b", [EP, EC, RB], F32, edges)
            setup_phase(nc, k)
            scatter_phase(nc, k)

        with ExitStack() as mid:
            k.scores = sb("scores", [P, NCB, H], F32, mid)
            k.new_node = sb("new_node", [P, BC * P + 1], F32, mid)
            k.src_at = sb("src_at", [P, NC + G], I32, mid)
            k.lane_a = sb("lane_a", [P, NC + G], F32, mid)
            k.w0, k.wo, k.w2 = (sb(n, [P, KC, D], F32, mid) for n in ("w0", "wo", "w2"))
            k.wqkv = sb("wqkv", [P, KC, 3 * D], F32, mid)
            k.b0, k.bo, k.b2, k.gamma, k.beta, k.att_src, k.att_dst = (
                sb(n, [P, D], F32, mid) for n in ("b0", "bo", "b2", "gamma", "beta", "att_src", "att_dst"))
            k.bqkv = sb("bqkv", [P, 3 * D], F32, mid)
            load_order_phase(nc, k)
            weights_phase(nc, k, a)

            norm_stats(nc, k, "n0", k.x)
            store_norm_phase(nc, k, h_table)
            with ExitStack() as layer:
                sums = sb("sums0", [P, T, D + 1], F32, layer)
                sum_phase(nc, k, "l0", h_table, sums, heads=False)

                def copy_rows(step, t, u, rows):
                    return nc.scalar.copy(rows, sums[:, at(t, 1), 0:D].rearrange("p o d -> p (o d)"))

                def keep_degree(step):
                    step(nc.vector.tensor_copy(degree[:, :], sums[:, :, D]))

                def add_relu(step, t, ps, slot, spare):
                    step(nc.vector.tensor_tensor(spare[:, 0, 0:D], ps, k.b0[:, :], ALU.add))
                    return nc.vector.scalar_tensor_tensor(tile_ap(k.x, t), spare[:, 0, 0:D], 0.0, tile_ap(k.x, t),
                                                          ALU.max, ALU.add)
                project_phase(nc, k, "p0", KC, D, k.w0, copy_rows, add_relu, setup=keep_degree)

            norm_stats(nc, k, "n1", k.x)
            with ExitStack() as layer:
                query = sb("query_parts", [P, T, 3, D], BF16, layer)

                def query_key_value(step, t, ps, slot, spare):
                    step(nc.vector.tensor_tensor(slot, ps, k.bqkv[:, :], ALU.add))
                    return split_parts(nc, step, query, t, slot[:, 0:D], spare[:, 0, 0:D])
                project_phase(nc, k, "p1", KC, 3 * D, k.wqkv, normed, query_key_value,
                              store=lambda t, slot: [(rows_of(key_table, t), slot[:, D:2 * D]),
                                                     (rows_of(value_table, t), slot[:, 2 * D:3 * D])])
                score_phase(nc, k, "s1", key_table, D, query)
            weights_of_edges_phase(nc, k, "m1", C ** -0.5)
            with ExitStack() as layer:
                sums1 = sb("sums1", [P, T, D + H], F32, layer)
                inverse = sb("inverse1", [P, T, H], F32, layer)
                sum_phase(nc, k, "l1", value_table, sums1, heads=True)

                def inverses(step):
                    step(nc.vector.tensor_scalar(inverse[:, :, :], sums1[:, :, D:D + H], 0.0, None, ALU.is_equal))
                    step(nc.vector.tensor_tensor(inverse[:, :, :], inverse[:, :, :], sums1[:, :, D:D + H], ALU.add))
                    step(nc.vector.reciprocal(inverse[:, :, :], inverse[:, :, :]))

                def divide(step, t, u, rows):
                    return nc.vector.tensor_tensor(
                        rows.rearrange("p (h c) -> p h c", h=H),
                        sums1[:, at(t, 1), 0:D].rearrange("p o (h c) -> p (o h) c", h=H),
                        inverse[:, at(t, 1), :].rearrange("p o h -> p (o h)").unsqueeze(2).to_broadcast([P, H, C]),
                        ALU.mult)

                def add_to_x(step, t, ps, slot, spare):
                    step(nc.vector.tensor_tensor(spare[:, 0, 0:D], ps, k.bo[:, :], ALU.add))
                    return nc.vector.tensor_tensor(tile_ap(k.x, t), tile_ap(k.x, t), spare[:, 0, 0:D], ALU.add)
                project_phase(nc, k, "p2", KC, D, k.wo, divide, add_to_x, prepare_on="dve", setup=inverses)

            norm_stats(nc, k, "n2", k.x)
            with ExitStack() as layer:
                k.xl = sb("xl", [P, T, D], F32, layer)
                k.of_src, k.of_dst = sb("of_src", [P, T, H], F32, layer), sb("of_dst", [P, T, H], F32, layer)
                k.of_dst_parts = sb("of_dst_parts", [P, T, 3, H], BF16, layer)

                def rows_and_logits(step, t, ps, slot, spare):
                    step(nc.vector.tensor_copy(slot[:, 0:D], ps))
                    step(nc.vector.tensor_copy(tile_ap(k.xl, t), ps))
                    step(nc.vector.tensor_tensor(spare[:, 0, 0:D], slot[:, 0:D], k.att_src[:, :], ALU.mult))
                    step(nc.vector.tensor_tensor(spare[:, 1, 0:D], slot[:, 0:D], k.att_dst[:, :], ALU.mult))
                    step(nc.vector.tensor_reduce(tile_ap(k.of_src, t), spare[:, 0, 0:D].rearrange("p (h c) -> p h c", h=H),
                                                 AX_X, ALU.add))
                    return nc.vector.tensor_reduce(tile_ap(k.of_dst, t),
                                                   spare[:, 1, 0:D].rearrange("p (h c) -> p h c", h=H), AX_X, ALU.add)
                project_phase(nc, k, "p3", KC, D, k.w2, normed, rows_and_logits,
                              store=lambda t, slot: [(rows_of(xl_table, t), slot[:, 0:D])])
                logit_parts_phase(nc, k)
                score_phase(nc, k, "s2", k.of_src_table, H, k.of_dst_parts)
                largest = sb("largest2", [P, NCB, H], F32, layer)
                weights_of_edges_phase(nc, k, "m2", 1.0, last=largest)
                sums2 = sb("sums2", [P, T, D + 2 * H], F32, layer)
                sum_phase(nc, k, "l2", xl_table, sums2, heads=True, last=largest)
                combine_loops_phase(nc, k, sums2)
                norm_stats(nc, k, "n3", k.xl)
                norm_of_layer_phase(nc, k)

        norm_stats(nc, k, "n4", k.x)
        with ExitStack() as layer:
            sums3 = sb("sums3", [P, T, HID], F32, layer)
            with ExitStack() as message:
                k.w_attr = sb("w_attr", [P, HID], BF16, message)
                parts = sb("src_parts", [P, T, 3, HID], BF16, message)
                with ExitStack() as weights:
                    k.w_node = sb("w_node", [P, KC, 2 * HID], F32, weights)
                    k.b_m1 = sb("b_m1", [P, HID], F32, weights)
                    attribute_weights_phase(nc, k, a)

                    def hidden_parts(step, t, ps, slot, spare):
                        step(nc.vector.tensor_copy(slot[:, 0:HID], ps[:, HID:2 * HID]))
                        step(nc.vector.tensor_tensor(spare[:, 0, :], ps[:, 0:HID], k.b_m1[:, :], ALU.add))
                        return split_parts(nc, step, parts, t, spare[:, 0, :], spare[:, 1, :])
                    project_phase(nc, k, "p4", KC, 2 * HID, k.w_node, normed, hidden_parts,
                                  keep=lambda t: rows_of(h3_table, t),
                                  store=lambda t, slot: [(rows_of(dst_table, t), slot[:, 0:HID])])
                load_phase(nc, "s_x_out", [(x_table.rearrange("(t p) d -> p t d", p=P), k.x[:, :, :])])
                message_phase(nc, k, dst_table, parts, sums3)

            h3 = sb("h3", [P, T, D], F32, layer)
            received = sb("received", [P, T, D], F32, layer)
            w_m2, w_u1 = sb("w_m2", [P, HID // P, D], F32, layer), sb("w_u1", [P, HID // P, HID], F32, layer)
            w_u2 = sb("w_u2", [P, HID // P, D], F32, layer)
            b_m2, b_u1, b_u2 = (sb(n, [P, w], F32, layer) for n, w in (("b_m2", D), ("b_u1", HID), ("b_u2", D)))
            load_phase(nc, "s_update_loads", [
                (k.x[:, :, :], x_table.rearrange("(t p) d -> p t d", p=P)),
                (h3[:, :, :], h3_table.rearrange("(t p) d -> p t d", p=P)),
                (w_m2[:, :, :], a['L3_gnn_mW2'].rearrange("(b p) n -> p b n", p=P)),
                (w_u1[:, :, :], a['L3_gnn_uW1'].rearrange("(b p) n -> p b n", p=P)),
                (w_u2[:, :, :], a['L3_gnn_uW2'].rearrange("(b p) n -> p b n", p=P)),
                (b_m2[:, :], a['L3_gnn_mb2'].partition_broadcast(P)), (b_u1[:, :], a['L3_gnn_ub1'].partition_broadcast(P)),
                (b_u2[:, :], a['L3_gnn_ub2'].partition_broadcast(P))])

            def copy_sums(step, t, u, rows):
                return nc.scalar.copy(rows, tile_ap(sums3, t))

            def messages(step, t, ps, slot, spare):
                return nc.vector.scalar_tensor_tensor(tile_ap(received, t), b_m2[:, :], degree[:, at(t, 1)], ps,
                                                      ALU.mult, ALU.add)
            project_phase(nc, k, "p5", HID // P, D, w_m2, copy_sums, messages)

            def node_and_received(step, t, u, rows):
                step(nc.scalar.copy(rows[:, 0:D], tile_ap(h3, t)))
                return nc.scalar.copy(rows[:, D:2 * D], tile_ap(received, t))

            def update_hidden(step, t, ps, slot, spare):
                step(nc.vector.tensor_tensor(spare[:, 0, :], ps, b_u1[:, :], ALU.add))
                return nc.vector.tensor_scalar(tile_ap(sums3, t), spare[:, 0, :], 0.0, None, ALU.max)
            project_phase(nc, k, "p6", HID // P, HID, w_u1, node_and_received, update_hidden)

            def update(step, t, ps, slot, spare):
                step(nc.vector.tensor_tensor(spare[:, 0, 0:D], ps, b_u2[:, :], ALU.add))
                step(nc.vector.tensor_tensor(spare[:, 1, 0:D], spare[:, 0, 0:D], tile_ap(h3, t), ALU.add))
                return nc.vector.tensor_tensor(tile_ap(k.x, t), tile_ap(k.x, t), spare[:, 1, 0:D], ALU.add)
            project_phase(nc, k, "p7", HID // P, D, w_u2, copy_sums, update)
            finish_x(nc, k, out)


def finish_x(nc, k, out):
    load_phase(nc, "s_out", [
        (out[0:(TR - 1) * P, :].rearrange("(t p) d -> p t d", p=P), k.x[:, 0:TR - 1, :]),
        (out[(TR - 1) * P:N, :], k.x[0:LAST, TR - 1, :])])


def kernel(**inputs):
    import numpy as _np
    import concourse.bacc as _bacc
    from concourse import mybir as _mybir
    from concourse.bass_utils import run_bass_kernel_spmd as _run

    nc = _bacc.Bacc("TRN2", target_bir_lowering=False, num_devices=1)
    arrays, args = {}, {}
    for name in _IN:
        v = _np.ascontiguousarray(inputs[name])
        arrays[f"in_{name}"] = v
        args[name] = nc.dram_tensor(f"in_{name}", v.shape, _mybir.dt.from_np(v.dtype), kind="ExternalInput").ap()
    out = nc.dram_tensor("x_out", (N, D), F32, kind="ExternalOutput").ap()
    gnn_layers_kernel(nc, args, out)
    r = _run(nc, [arrays], core_ids=[0])
    return r.results[0]["x_out"]
```

```python
from contextlib import ExitStack

import concourse.bass as bass
from concourse import mybir

ALU = mybir.AluOpType
ACT = mybir.ActivationFunctionType
AX_X = mybir.AxisListType.X
F32 = mybir.dt.float32
BF16 = mybir.dt.bfloat16
I32 = mybir.dt.int32

P = 128
N = 3125
D = 256
H = 8
C = D // H
E = 53125
EA = 16
HID = 512
EP = 125
EC = E // EP
T = 26
TR = (N + P - 1) // P
NP = T * P
LAST = N - (TR - 1) * P
G = 4
NC = -(-(E + TR * (P - 1)) // P)
NC = -(-NC // (2 * G)) * 2 * G
IT = NC // (2 * G)
NB = 16
BC = 28
NCB = NB * BC
CQ = 4
CR = NC // CQ
RB = EA + 3
BUCKETS, DIGITS = 16, 3
BIG = 1e30
EPS = 1e-5
assert E == EP * EC and NCB >= NC and NC == CQ * CR and CR <= P and N <= BUCKETS ** DIGITS and BUCKETS <= TR
KC = D // P
SC = 5


class Chain:

    def __init__(self, eng, sem):
        self.eng, self.sem, self.n = eng, sem, 0

    def __call__(self, instruction):
        self.n += 1
        instruction.then_inc(self.sem, 1)
        self.eng.wait_ge(self.sem, self.n)


def rounds(eng, n, body):
    body(0, True)
    with eng.Fori(1, n) as i:
        body(i, False)


def at(start, size):
    return bass.ds(start, size)


def phase(build):
    def run(nc, *args, **settings):
        mine = []

        def new_semaphore(name):
            mine.append(nc.alloc_semaphore(name=name))
            return mine[-1]
        build(nc, new_semaphore, *args, **settings)
        while resting:
            nc.release_semaphore(resting.pop())
        numbers = [s.num for s in mine]
        nc.clear_and_free_semaphores(mine)
        resting.extend(nc.alloc_semaphore(name=f"resting{n}", num=n) for n in numbers)
    return run


resting = []


def totals_to_chunks(nc, step, total, chunks, ends, whole, zeros):
    step(nc.vector.tensor_scalar(chunks, total, float(P - 1), None, ALU.add))
    step(nc.vector.tensor_copy(whole, chunks))
    step(nc.vector.tensor_single_scalar(whole, whole, 7, ALU.arith_shift_right))
    step(nc.vector.tensor_copy(chunks, whole))
    step(nc.vector.tensor_tensor_scan(ends, chunks, zeros, 0.0, ALU.add, ALU.add))


def places_in_buckets(nc, step, is_in, running, first, zeros, place_f, place):
    buckets = is_in.shape[1]
    for t in range(buckets):
        ins = nc.vector.tensor_tensor_scan(running[:, t, :], zeros, is_in[:, t, :], first[:, t:t + 1], ALU.add, ALU.add)
    step(ins)
    step(nc.vector.tensor_tensor(running, running, is_in, ALU.mult))
    step(nc.vector.tensor_reduce(place_f, running.rearrange("p t c -> p c t"), AX_X, ALU.add))
    step(nc.vector.tensor_scalar(place, place_f, -1.0, None, ALU.add))


@phase
def setup_phase(nc, new_semaphore, k):
    with ExitStack() as tmp:
        def sb(name, shape, dt):
            return tmp.enter_context(nc.sbuf_tensor(name, shape, dt))

        weight_f = sb("weight_f", [EP, EC], F32)
        tile_i = sb("tile_i", [EP, EC], I32)
        tile_f = sb("tile_f", [EP, EC], F32)
        is_tile = sb("is_tile", [EP, TR, EC], BF16)
        running = sb("running", [EP, TR, EC], F32)
        attr_f = running[:, :, :].rearrange("p t c -> p (t c)")[:, 0:EC * EA].rearrange("p (c a) -> p c a", a=EA)
        zeros_c = sb("zeros_c", [EP, EC], F32)
        counts = sb("counts", [EP, TR], F32)
        total_i = sb("total_i", [P, TR], I32)
        chunks_f = sb("chunks_f", [P, TR], F32)
        base_f = sb("base_f", [P, TR], F32)
        first_f = sb("first_f", [EP, TR], F32)
        pos_f = sb("pos_f", [EP, EC], F32)
        pad_b = sb("pad_b", [P, NC // 8, RB], F32)
        tail = sb("tail", [2, P], I32)
        ps_before = tmp.enter_context(nc.psum_tensor("ps_before", [EP, TR], F32))
        ps_total = tmp.enter_context(nc.psum_tensor("ps_total", [P, TR], F32))
        s_keys = new_semaphore("s_keys")
        s_dst = new_semaphore("s_dst")
        s_attr = new_semaphore("s_attr")
        s_x = new_semaphore("s_x")
        s_pool = new_semaphore("s_pool")
        s_next = new_semaphore("s_next")
        s_dve = new_semaphore("s_dve")
        s_counts = new_semaphore("s_counts")
        s_totals = new_semaphore("s_totals")
        s_is = new_semaphore("s_is")
        s_rec = new_semaphore("s_rec")
        s_pad = new_semaphore("s_pad")
        s_filled = new_semaphore("s_filled")
        s_tail = new_semaphore("s_tail")

        with nc.Block() as block:
            @block.sync
            def _(sp):
                sp.dma_start(k.src_i[:, :], k.src.rearrange("(p c) -> p c", p=EP)).then_inc(s_keys, 16)
                sp.dma_start(weight_f[:, :], k.edge_weight.rearrange("(p c) -> p c", p=EP)).then_inc(s_attr, 16)
                sp.dma_start(attr_f, k.edge_attr.rearrange("(p c) a -> p c a", p=EP)).then_inc(s_attr, 16)
                sp.dma_start(k.dst_i[:, :], k.dst.rearrange("(p c) -> p c", p=EP)).then_inc(s_dst, 16)
                sp.wait_ge(s_next, 1)
                sp.dma_start(k.next_i[0:EP - 1, :], k.dst[1:(EP - 1) * EC + 1].rearrange("(p c) -> p c", c=EC)).then_inc(s_dst, 16)
                sp.dma_start(k.next_i[EP - 1:EP, 0:EC - 1], k.dst[(EP - 1) * EC + 1:E].rearrange("(p c) -> p c", p=1))\
                    .then_inc(s_dst, 16)
                sp.wait_ge(s_pool, 1)
                sp.dma_start(k.x[:, 0:TR - 1, :], k.x_in[0:(TR - 1) * P, :].rearrange("(t p) d -> p t d", p=P)).then_inc(s_x, 16)
                sp.dma_start(k.x[0:LAST, TR - 1, :], k.x_in[(TR - 1) * P:N, :]).then_inc(s_x, 16)
                sp.dma_start(k.by_dst_src[0:E, :].rearrange("(p c) o -> p (c o)", p=EP), k.src.rearrange("(p c) -> p c", p=EP))\
                    .then_inc(s_tail, 16)
                sp.dma_start(k.by_dst_dst[0:E, :].rearrange("(p c) o -> p (c o)", p=EP), k.dst.rearrange("(p c) -> p c", p=EP))\
                    .then_inc(s_tail, 16)
                sp.wait_ge(s_pad, 4)
                sp.dma_start(k.by_dst_src[E:E + P, :].rearrange("(o p) q -> o (p q)", o=1), tail[0:1, :]).then_inc(s_tail, 16)
                sp.dma_start(k.by_dst_dst[E:E + P, :].rearrange("(o p) q -> o (p q)", o=1), k.minus[0:1, :]).then_inc(s_tail, 16)
                sp.wait_ge(s_dst, 48)
                sp.wait_ge(s_x, 32)
                sp.wait_ge(s_tail, 64)

            @block.gpsimd
            def _(pool):
                nc.gpsimd.memset(k.x[:, TR - 1:T, :], 0.0).then_inc(s_pool, 1)
                nc.gpsimd.memset(k.ones[:, :], 1.0).then_inc(s_pool, 1)
                nc.gpsimd.iota(k.tile_ids[:, :], [[1, TR]], base=0, channel_multiplier=0,
                               allow_small_or_imprecise_dtypes=True).then_inc(s_pool, 1)
                nc.gpsimd.iota(k.chunk_ids[:, :], [[1, NC]], base=0, channel_multiplier=0,
                               allow_small_or_imprecise_dtypes=True).then_inc(s_pool, 1)
                nc.gpsimd.iota(k.chunk_of_row[:, :], [[CR, CQ]], base=0, channel_multiplier=1,
                               allow_small_or_imprecise_dtypes=True).then_inc(s_pool, 1)
                nc.gpsimd.iota(k.lane[:, :], [[1, P]], base=0, channel_multiplier=0,
                               allow_small_or_imprecise_dtypes=True).then_inc(s_pool, 1)
                pool.wait_ge(s_pool, 2)
                nc.gpsimd.affine_select(out=k.before[:, :], in_=k.ones[:, :], compare_op=ALU.is_gt, fill=0.0, base=0,
                                        pattern=[[1, P]], channel_multiplier=-1).then_inc(s_pool, 1)
                nc.gpsimd.affine_select(out=k.ident[:, :], in_=k.ones[:, :], compare_op=ALU.is_equal, fill=0.0, base=0,
                                        pattern=[[1, P]], channel_multiplier=-1).then_inc(s_pool, 1)
                nc.gpsimd.memset(pad_b[:, :, :], 0.0).then_inc(s_pad, 1)
                nc.gpsimd.memset(tail[:, :], 0).then_inc(s_pad, 1)
                nc.gpsimd.memset(k.minus[:, :], -1).then_inc(s_pad, 1)
                pool.wait_ge(s_pad, 3)
                nc.gpsimd.memset(pad_b[:, :, EA + 1:EA + 2], -1.0).then_inc(s_pad, 1)

            @block.scalar
            def _(act):
                act.wait_ge(s_attr, 32)
                nc.scalar.copy(k.fields_b[:, :, EA + 2], weight_f[:, :]).then_inc(s_rec, 1)
                nc.scalar.copy(k.fields_b[:, :, 0:EA], attr_f).then_inc(s_rec, 1)
                act.wait_ge(s_dst, 48)
                nc.scalar.copy(k.fields_b[:, :, EA], k.dst_i[:, :]).then_inc(s_rec, 1)
                act.wait_ge(s_pool, 8)
                nc.scalar.copy(k.ident_b[:, :], k.ident[:, :]).then_inc(s_rec, 1)
                act.wait_ge(s_pad, 4)
                for n in range(8):
                    rows = NC // 8 * P
                    act.dma_start(k.rec_b[n * rows:(n + 1) * rows, :].rearrange("(p c) r -> p c r", p=P),
                                  pad_b[:, :, :]).then_inc(s_filled, 16)
                act.dma_start(k.rec_b[NC * P:, :].rearrange("(p c) r -> p c r", p=P),
                              pad_b[:, 0:G, :]).then_inc(s_filled, 16)
                act.wait_ge(s_filled, 144)

            @block.tensor
            def _(pe):
                pe.wait_ge(s_pool, 7)
                pe.wait_ge(s_counts, 1)
                nc.tensor.matmul(ps_before[:, :], k.before[0:EP, 0:EP], counts[:, :], start=True, stop=True)
                nc.tensor.matmul(ps_total[:, :], k.ones[0:EP, :], counts[:, :], start=True, stop=True).then_inc(s_totals, 1)

            @block.vector
            def _(dve):
                step = Chain(dve, s_dve)
                nc.vector.memset(k.next_i[:, :], N).then_inc(s_next, 1)
                step(nc.vector.memset(zeros_c[:, :], 0.0))
                step(nc.vector.memset(k.zeros_t[:, :], 0.0))
                dve.wait_ge(s_keys, 16)
                dve.wait_ge(s_pool, 6)
                step(nc.vector.tensor_single_scalar(tile_i[:, :], k.src_i[:, :], 7, ALU.arith_shift_right))
                step(nc.vector.tensor_copy(tile_f[:, :], tile_i[:, :]))
                nc.vector.tensor_tensor(is_tile[:, :, :], tile_f[:, :].unsqueeze(1).to_broadcast([EP, TR, EC]),
                                        k.tile_ids[0:EP, :].unsqueeze(2).to_broadcast([EP, TR, EC]),
                                        ALU.is_equal).then_inc(s_is, 1)
                dve.wait_ge(s_is, 1)
                nc.vector.tensor_reduce(counts[:, :], is_tile[:, :, :], AX_X, ALU.add).then_inc(s_counts, 1)
                step(nc.vector.tensor_single_scalar(tile_i[:, :], k.src_i[:, :], P - 1, ALU.bitwise_and))
                step(nc.vector.tensor_copy(k.fields_b[:, :, EA + 1], tile_i[:, :]))
                dve.wait_ge(s_totals, 1)
                totals_to_chunks(nc, step, ps_total[:, :], chunks_f[:, :], k.ends_b[:, :], total_i[:, :], k.zeros_t[:, :])
                step(nc.vector.tensor_tensor(base_f[:, :], k.ends_b[:, :], chunks_f[:, :], ALU.subtract))
                step(nc.vector.scalar_tensor_tensor(first_f[:, :], base_f[0:EP, :], float(P), ps_before[:, :],
                                                    ALU.mult, ALU.add))
                dve.wait_ge(s_rec, 2)
                places_in_buckets(nc, step, is_tile[:, :, :], running[:, :, :], first_f[:, :], zeros_c[:, :],
                                  pos_f[:, :], k.pos_b[:, :])


def load_weights(sp, w, turned, rows, k, a, s_w, s_rows):
    for n, (source, _) in enumerate(turned):
        sp.dma_start(w[:, n, :, :], source.rearrange("(o p) i -> p o i", p=P)).then_inc(s_w, 16)
    sp.dma_start(k.w2[:, :, :], a['L2_gnn_W'].rearrange("(o p) i -> p o i", p=P)).then_inc(s_rows, 16)
    for source, row in rows:
        sp.dma_start(row[:, :], source.partition_broadcast(P)).then_inc(s_rows, 16)
    sp.wait_ge(s_rows, 16 * (1 + len(rows)))


@phase
def scatter_phase(nc, new_semaphore, k, a):
    turned = [(a['L0_gnn_W'], k.w0), (a['L1_gnn_Wq'], k.wqkv[:, :, 0:D]), (a['L1_gnn_Wk'], k.wqkv[:, :, D:2 * D]),
              (a['L1_gnn_Wv'], k.wqkv[:, :, 2 * D:3 * D]), (a['L1_gnn_Wo'], k.wo)]
    rows = [(a['L0_gnn_bias'], k.b0), (a['L1_gnn_bq'], k.bqkv[:, 0:D]), (a['L1_gnn_bk'], k.bqkv[:, D:2 * D]),
            (a['L1_gnn_bv'], k.bqkv[:, 2 * D:3 * D]), (a['L1_gnn_bo'], k.bo), (a['L2_gnn_bias'], k.b2),
            (a['L2_gnn_gamma'], k.gamma), (a['L2_gnn_beta'], k.beta),
            (a['L2_gnn_att_src'].rearrange("h c -> (h c)"), k.att_src),
            (a['L2_gnn_att_dst'].rearrange("h c -> (h c)"), k.att_dst)]

    with ExitStack() as tmp:
        def sb(name, shape, dt):
            return tmp.enter_context(nc.sbuf_tensor(name, shape, dt))

        at_b = sb("at_b", [EP, SC], I32)
        row_b = sb("row_b", [EP, SC, RB], F32)
        w = sb("w_raw", [P, len(turned), KC, D], F32)
        stats = sb("stats0", [P, 2, 6], F32)
        mv1 = sb("mv1_0", [P, 2, 2], F32)
        mv = sb("mv0", [P, T, 2], F32)
        var = sb("var0", [P, T], F32)
        dev = sb("dev0", [P, T], F32)
        dst_tile_i = sb("dst_tile_i", [EP, EC], I32)
        dst_tile = sb("dst_tile", [EP, EC], F32)
        behind = sb("behind", [EP, EC], F32)
        is_tile = sb("is_dst_tile", [EP, TR, EC], BF16)
        counts = sb("dst_counts", [EP, TR + 1], F32)
        total_i = sb("dst_total_i", [P, TR], I32)
        chunks_f = sb("dst_chunks_f", [P, TR], F32)
        ends_a = sb("ends_a", [P, TR], F32)
        spare_places = sb("spare_places", [P, TR], F32)
        past = sb("past", [1, NC // 4, TR - 1], F32)
        tile_f = sb("chunk_tile_f", [1, NC], F32)
        row_past = sb("row_past", [CR, CQ, TR - 1], F32)
        row_start = sb("row_start", [CR, CQ], F32)
        row_spare = sb("row_spare", [CR, CQ], F32)
        ps = tmp.enter_context(nc.psum_tensor("ps_w", [P, KC, KC, P], F32))
        ps_total = tmp.enter_context(nc.psum_tensor("ps_dst_total", [P, TR + 1], F32))
        s_staged = new_semaphore("s_staged")
        s_go = new_semaphore("s_go")
        s_done = [new_semaphore(f"s_scattered{j}") for j in range(SC)]
        s_w = new_semaphore("s_w_raw")
        s_rows = new_semaphore("s_w_rows")
        s_turn = new_semaphore("s_w_turned")
        s_kept = new_semaphore("s_w_kept")
        s_counts = new_semaphore("s_dst_counts")
        s_totals = new_semaphore("s_dst_totals")
        s_step = new_semaphore("s_tables_step")
        s_stats, s_aggr, s_hold, s_mv, s_var, s_dev = (new_semaphore(f"s_norm0_{n}") for n in
                                                       ("stats", "aggr", "hold", "mv", "var", "dev"))

        with nc.Block() as block:
            @block.sync
            def _(sp):
                load_weights(sp, w, turned, rows, k, a, s_w, s_rows)

            @block.scalar
            def _(act):
                def columns(i, first):
                    for j in range(SC):
                        if not first:
                            act.wait_ge(s_done[j], 16 * i)
                        nc.scalar.copy(at_b[:, j:j + 1], k.pos_b[:, at(i * SC + j, 1)])
                        nc.scalar.copy(row_b[:, j:j + 1, :], k.fields_b[:, at(i * SC + j, 1), :]).then_inc(s_staged, 1)
                rounds(act, EC // SC, columns)
                act.wait_ge(s_var, 1)
                nc.scalar.activation(dev[:, :], var[:, :], ACT.Sqrt).then_inc(s_dev, 1)

            @block.gpsimd
            def _(pool):
                def columns(i, first):
                    for j in range(SC):
                        pool.wait_ge(s_staged, i * SC + j + 1)
                        pool.sem_inc(s_go, 1)
                        pool.indirect_dma_start(k.rec_b, bass.IndirectOffsetOnAxis(at_b[:, j:j + 1], 0),
                                                row_b[:, j, :], None).then_inc(s_done[j], 16)
                rounds(pool, EC // SC, columns)
                for j in range(SC):
                    pool.wait_ge(s_done[j], 16 * (EC // SC))

            @block.tensor
            def _(pe):
                pe.wait_ge(s_w, 16 * len(turned))
                for n in range(len(turned)):
                    if n:
                        pe.wait_ge(s_kept, n)
                    for o in range(KC):
                        for i in range(KC):
                            ins = nc.tensor.transpose(ps[:, i, o, :], w[:, n, o, i * P:(i + 1) * P], k.ident[:, :])
                    ins.then_inc(s_turn, 1)
                pe.wait_ge(s_counts, 2)
                nc.tensor.matmul(ps_total[:, :], k.ones[0:EP, :], counts[:, :], start=True, stop=True).then_inc(s_totals, 1)

            @block.vector
            def _(dve):
                step = Chain(dve, s_step)
                for n, (_, kept) in enumerate(turned):
                    dve.wait_ge(s_turn, n + 1)
                    nc.vector.tensor_copy(kept[:, :, :], ps[:, :, :, :].rearrange("p i o q -> p i (o q)")).then_inc(s_kept, 1)
                tile_statistics(nc, dve, k.x, stats, mv1, mv, s_stats, s_aggr, s_hold, s_mv)
                nc.vector.tensor_scalar(var[:, :], mv[:, :, 1], EPS, None, ALU.add).then_inc(s_var, 1)

                step(nc.vector.tensor_single_scalar(dst_tile_i[:, :], k.dst_i[:, :], 7, ALU.arith_shift_right))
                step(nc.vector.tensor_copy(dst_tile[:, :], dst_tile_i[:, :]))
                step(nc.vector.tensor_tensor(is_tile[:, :, :], dst_tile[:, :].unsqueeze(1).to_broadcast([EP, TR, EC]),
                                             k.tile_ids[0:EP, :].unsqueeze(2).to_broadcast([EP, TR, EC]), ALU.is_equal))
                nc.vector.tensor_reduce(counts[:, 0:TR], is_tile[:, :, :], AX_X, ALU.add).then_inc(s_counts, 1)
                step(nc.vector.tensor_copy(dst_tile[:, :], k.dst_i[:, :]))
                step(nc.vector.tensor_copy(behind[:, :], k.next_i[:, :]))
                step(nc.vector.tensor_tensor(behind[:, :], behind[:, :], dst_tile[:, :], ALU.is_lt))
                nc.vector.tensor_reduce(counts[:, TR:TR + 1], behind[:, :], AX_X, ALU.add).then_inc(s_counts, 1)
                dve.wait_ge(s_totals, 1)
                step(nc.vector.tensor_copy(k.disorder[:, :], ps_total[0:1, TR:TR + 1]))
                totals_to_chunks(nc, step, ps_total[:, 0:TR], chunks_f[:, :], ends_a[:, :], total_i[:, :], k.zeros_t[:, :])
                step(nc.vector.scalar_tensor_tensor(spare_places[:, :], chunks_f[:, :], float(P), ps_total[:, 0:TR],
                                                    ALU.mult, ALU.subtract))
                for ends, tile_of in ((k.ends_b, k.tile_ib), (ends_a, k.tile_ia)):
                    for q in range(4):
                        part = slice(q * NC // 4, (q + 1) * NC // 4)
                        step(nc.vector.tensor_tensor(past[:, :, :],
                                                     k.chunk_ids[:, part].unsqueeze(2).to_broadcast([1, NC // 4, TR - 1]),
                                                     ends[0:1, 0:TR - 1].unsqueeze(1).to_broadcast([1, NC // 4, TR - 1]),
                                                     ALU.is_ge))
                        step(nc.vector.tensor_reduce(tile_f[:, part], past[:, :, :], AX_X, ALU.add))
                    step(nc.vector.tensor_copy(tile_of[:, :], tile_f[:, :]))
                step(nc.vector.tensor_tensor(row_past[:, :, :], k.chunk_of_row[:, :].unsqueeze(2).to_broadcast([CR, CQ, TR - 1]),
                                             ends_a[0:CR, 0:TR - 1].unsqueeze(1).to_broadcast([CR, CQ, TR - 1]), ALU.is_ge))
                step(nc.vector.tensor_reduce(row_spare[:, :], row_past[:, :, :], AX_X, ALU.add))
                step(nc.vector.tensor_scalar(k.node_of_row[:, :], row_spare[:, :], float(P), None, ALU.mult))
                step(nc.vector.tensor_tensor(row_past[:, :, :], row_past[:, :, :],
                                             spare_places[0:CR, 0:TR - 1].unsqueeze(1).to_broadcast([CR, CQ, TR - 1]), ALU.mult))
                step(nc.vector.tensor_reduce(row_spare[:, :], row_past[:, :, :], AX_X, ALU.add))
                step(nc.vector.scalar_tensor_tensor(row_start[:, :], k.chunk_of_row[:, :], float(P), row_spare[:, :],
                                                    ALU.mult, ALU.subtract))
                step(nc.vector.tensor_scalar(k.start_of_row[:, :], row_start[:, :], float(E), None, ALU.min))
                dve.wait_ge(s_dev, 1)
                step(nc.vector.reciprocal(k.rstd[:, :], dev[:, :]))
                step(nc.vector.scalar_tensor_tensor(k.shift[:, :], mv[:, :, 0], -1.0, k.rstd[:, :], ALU.mult, ALU.mult))


def if_disorder(nc, eng, which, k):
    disorder = nc.values_load(k.disorder[:, :], [which], min_val=0, max_val=E,
                              skip_runtime_bounds_check_because="a count of edges")
    return eng.If(disorder != 0)


@phase
def sort_by_dst_phase(nc, new_semaphore, k):
    with ExitStack() as tmp:
        def sb(name, shape, dt):
            return tmp.enter_context(nc.sbuf_tensor(name, shape, dt))

        pairs = sb("pairs", [EP, EC, 2], I32)
        digit_i = sb("digit_i", [EP, EC], I32)
        digit_f = sb("digit_f", [EP, EC], F32)
        is_digit = sb("is_digit", [EP, BUCKETS, EC], BF16)
        running = sb("running_digit", [EP, BUCKETS, EC], F32)
        zeros_c = sb("digit_zeros_c", [EP, EC], F32)
        counts = sb("digit_counts", [EP, BUCKETS], F32)
        totals = sb("digit_totals", [EP, BUCKETS], F32)
        ends = sb("digit_ends", [EP, BUCKETS], F32)
        first_f = sb("digit_first", [EP, BUCKETS], F32)
        zeros = sb("digit_zeros", [EP, BUCKETS], F32)
        place_f = sb("digit_place_f", [EP, EC], F32)
        place = sb("digit_place", [EP, EC], I32)
        at_p = sb("at_p", [EP, SC], I32)
        row_p = sb("row_p", [EP, SC, 2], I32)
        ps_before = tmp.enter_context(nc.psum_tensor("ps_digit_before", [EP, BUCKETS], F32))
        ps_total = tmp.enter_context(nc.psum_tensor("ps_digit_total", [EP, BUCKETS], F32))
        s_step = new_semaphore("s_digit_step")
        s_counts = new_semaphore("s_digit_counts")
        s_totals = new_semaphore("s_digit_totals")
        s_placed = new_semaphore("s_digit_placed")
        s_staged = new_semaphore("s_digit_staged")
        s_go = new_semaphore("s_digit_go")
        s_done = [new_semaphore(f"s_digit_scattered{j}") for j in range(SC)]
        s_all = new_semaphore("s_digit_all")
        s_loaded = new_semaphore("s_digit_loaded")
        s_columns = new_semaphore("s_digit_columns")
        s_out = new_semaphore("s_digit_out")

        with nc.Block() as block:
            @block.vector
            def _(dve):
                with if_disorder(nc, dve, mybir.EngineType.DVE, k):
                    step = Chain(dve, s_step)
                    step(nc.vector.memset(zeros_c[:, :], 0.0))
                    step(nc.vector.memset(zeros[:, :], 0.0))
                    step(nc.vector.tensor_copy(pairs[:, :, 0], k.src_i[:, :]))
                    step(nc.vector.tensor_copy(pairs[:, :, 1], k.dst_i[:, :]))
                    for n in range(DIGITS):
                        if n:
                            dve.wait_ge(s_loaded, 16 * n)
                        step(nc.vector.tensor_copy(digit_i[:, :], pairs[:, :, 1]))
                        step(nc.vector.tensor_single_scalar(digit_i[:, :], digit_i[:, :], 4 * n, ALU.arith_shift_right))
                        step(nc.vector.tensor_single_scalar(digit_i[:, :], digit_i[:, :], BUCKETS - 1, ALU.bitwise_and))
                        step(nc.vector.tensor_copy(digit_f[:, :], digit_i[:, :]))
                        step(nc.vector.tensor_tensor(is_digit[:, :, :], digit_f[:, :].unsqueeze(1).to_broadcast([EP, BUCKETS, EC]),
                                                     k.tile_ids[0:EP, 0:BUCKETS].unsqueeze(2).to_broadcast([EP, BUCKETS, EC]),
                                                     ALU.is_equal))
                        nc.vector.tensor_reduce(counts[:, :], is_digit[:, :, :], AX_X, ALU.add).then_inc(s_counts, 1)
                        dve.wait_ge(s_totals, n + 1)
                        step(nc.vector.tensor_copy(totals[:, :], ps_total[:, :]))
                        step(nc.vector.tensor_tensor_scan(ends[:, :], totals[:, :], zeros[:, :], 0.0, ALU.add, ALU.add))
                        step(nc.vector.tensor_tensor(ends[:, :], ends[:, :], totals[:, :], ALU.subtract))
                        step(nc.vector.tensor_tensor(first_f[:, :], ends[:, :], ps_before[:, :], ALU.add))
                        places_in_buckets(nc, step, is_digit[:, :, :], running[:, :, :], first_f[:, :], zeros_c[:, :],
                                          place_f[:, :], place[:, :])
                        dve.sem_inc(s_placed, 1)
                    dve.wait_ge(s_loaded, 16 * DIGITS)
                    step(nc.vector.tensor_copy(digit_i[:, :], pairs[:, :, 0]))
                    step(nc.vector.tensor_copy(place[:, :], pairs[:, :, 1]))
                    dve.sem_inc(s_columns, 1)

            @block.tensor
            def _(pe):
                with if_disorder(nc, pe, mybir.EngineType.PE, k):
                    for n in range(DIGITS):
                        pe.wait_ge(s_counts, n + 1)
                        nc.tensor.matmul(ps_before[:, :], k.before[0:EP, 0:EP], counts[:, :], start=True, stop=True)
                        nc.tensor.matmul(ps_total[:, :], k.ones[0:EP, 0:EP], counts[:, :], start=True,
                                         stop=True).then_inc(s_totals, 1)

            @block.scalar
            def _(act):
                with if_disorder(nc, act, mybir.EngineType.Activation, k):
                    for n in range(DIGITS):
                        act.wait_ge(s_placed, n + 1)

                        def columns(i, first):
                            for j in range(SC):
                                if not first:
                                    act.wait_ge(s_done[j], 16 * (n * (EC // SC) + i))
                                nc.scalar.copy(at_p[:, j:j + 1], place[:, at(i * SC + j, 1)])
                                nc.scalar.copy(row_p[:, j:j + 1, :], pairs[:, at(i * SC + j, 1), :]).then_inc(s_staged, 1)
                        if n:
                            act.wait_ge(s_all, n)
                        rounds(act, EC // SC, columns)

            @block.gpsimd
            def _(pool):
                with if_disorder(nc, pool, mybir.EngineType.Pool, k):
                    for n in range(DIGITS):
                        def columns(i, first):
                            for j in range(SC):
                                pool.wait_ge(s_staged, n * EC + i * SC + j + 1)
                                pool.sem_inc(s_go, 1)
                                pool.indirect_dma_start(k.pairs, bass.IndirectOffsetOnAxis(at_p[:, j:j + 1], 0),
                                                        row_p[:, j, :], None).then_inc(s_done[j], 16)
                        rounds(pool, EC // SC, columns)
                        for j in range(SC):
                            pool.wait_ge(s_done[j], 16 * (n + 1) * (EC // SC))
                        pool.sem_inc(s_all, 1)

            @block.sync
            def _(sp):
                with if_disorder(nc, sp, mybir.EngineType.SP, k):
                    for n in range(DIGITS):
                        sp.wait_ge(s_all, n + 1)
                        sp.dma_start(pairs[:, :, :], k.pairs.rearrange("(p c) r -> p c r", p=EP)).then_inc(s_loaded, 16)
                    sp.wait_ge(s_columns, 1)
                    for column, target in ((digit_i, k.by_dst_src), (place, k.by_dst_dst)):
                        sp.dma_start(target[0:E, :].rearrange("(p c) o -> p (c o)", p=EP), column[:, :]).then_inc(s_out, 16)
                    sp.wait_ge(s_out, 32)


@phase
def load_orders_phase(nc, new_semaphore, k, table):
    with ExitStack() as tmp:
        def sb(name, shape, dt):
            return tmp.enter_context(nc.sbuf_tensor(name, shape, dt))

        h = sb("h0", [P, T, D], F32)
        rec_b = sb("rec_b_sb", [P, NC, RB - EA], F32)
        src_rows = sb("src_rows", [CR, CQ, P], I32)
        dst_rows = sb("dst_rows", [CR, CQ, P], I32)
        start = sb("start_slots", [CR, CQ], I32)
        src_f = sb("src_rows_f", [CR, CQ, P], F32)
        dst_f = sb("dst_rows_f", [CR, CQ, P], F32)
        lane_f = sb("lane_rows_f", [CR, CQ, P], F32)
        own = sb("own_rows", [CR, CQ, P], F32)
        keys = sb("key_of_rows", [CR, CQ, P], F32)
        no_key = sb("no_key", [1, (NCB - NC) * P + 2], F32)
        key_rows = sb("key_rows", [P, BC * P + 2], F32)
        ps_turn = tmp.enter_context(nc.psum_tensor("ps_order_turn", [P, 2, CQ, P], F32))
        s_rec_b = new_semaphore("s_rec_b_sb")
        s_step = new_semaphore("s_order_step")
        s_start = new_semaphore("s_start")
        s_src = new_semaphore("s_src_rows")
        s_dst = new_semaphore("s_dst_rows")
        s_keyed = new_semaphore("s_keyed")
        s_no_key = new_semaphore("s_no_key")
        s_key_out = new_semaphore("s_key_out")
        s_key_rows = new_semaphore("s_key_rows")
        s_ready = new_semaphore("s_rows_ready")
        s_turned = new_semaphore("s_order_turned")
        s_h = new_semaphore("s_h0")
        s_out = new_semaphore("s_h0_out")

        with nc.Block() as block:
            @block.gpsimd
            def _(pool):
                nc.gpsimd.tensor_copy(start[:, :], k.start_of_row[:, :]).then_inc(s_start, 1)
                pool.wait_ge(s_start, 1)
                for q in range(CQ):
                    pool.indirect_dma_start(dst_rows[:, q, :], None, k.by_dst_dst,
                                            bass.IndirectOffsetOnAxis(start[:, q:q + 1], 0)).then_inc(s_dst, 16)
                for q in range(CQ):
                    pool.indirect_dma_start(src_rows[:, q, :], None, k.by_dst_src,
                                            bass.IndirectOffsetOnAxis(start[:, q:q + 1], 0)).then_inc(s_src, 16)

            @block.sync
            def _(sp):
                sp.dma_start(rec_b[:, :, :], k.rec_b[0:NC * P, EA:RB].rearrange("(c p) r -> p c r", p=P)).then_inc(s_rec_b, 16)
                sp.wait_ge(s_keyed, 1)
                sp.dma_start(k.keys[1:1 + NC * P].rearrange("(q p e) -> p q e", q=CQ, e=P), keys[:, :, :]).then_inc(s_key_out, 16)
                sp.wait_ge(s_no_key, 2)
                sp.dma_start(k.keys[0:1].rearrange("(o e) -> o e", o=1), no_key[:, 0:1]).then_inc(s_key_out, 16)
                sp.dma_start(k.keys[1 + NC * P:].rearrange("(o e) -> o e", o=1), no_key[:, 1:]).then_inc(s_key_out, 16)
                sp.wait_ge(s_key_out, 48)
                for head in range(H):
                    sp.dma_start(key_rows[head * NB:(head + 1) * NB, :],
                                 bass.AP(tensor=k.keys.tensor, offset=0, ap=[[BC * P, NB], [1, BC * P + 2]])).then_inc(s_key_rows, 16)
                sp.wait_ge(s_h, T)
                sp.dma_start(table.rearrange("(t p) d -> p t d", p=P), h[:, :, :]).then_inc(s_out, 16)
                sp.wait_ge(s_out, 16)

            @block.scalar
            def _(act):
                def tiles(i, first):
                    for u in range(2):
                        t = 2 * i + u
                        nc.scalar.activation(tile_ap(h, t), tile_ap(k.x, t), ACT.Relu, bias=k.shift[:, at(t, 1)],
                                             scale=k.rstd[:, at(t, 1)]).then_inc(s_h, 1)
                rounds(act, T // 2, tiles)

            @block.tensor
            def _(pe):
                for n, rows in enumerate((lane_f, src_f)):
                    pe.wait_ge(s_ready, n + 1)
                    for q in range(CQ):
                        ins = nc.tensor.transpose(ps_turn[:, n, q, 0:CR], rows[:, q, :], k.ident[0:CR, 0:CR])
                    ins.then_inc(s_turned, 1)

            @block.vector
            def _(dve):
                step = Chain(dve, s_step)
                nc.vector.memset(no_key[:, :], 0.0).then_inc(s_no_key, 1)
                for column in (k.src_at, k.dst_at, k.lane_a, k.lane_b):
                    step(nc.vector.memset(column[:, NC:NC + G], 0))
                step(nc.vector.memset(k.scores[:, NC:NCB, :], 0.0))
                dve.wait_ge(s_no_key, 1)
                step(nc.vector.memset(no_key[:, 0:1], -2.0))
                nc.vector.memset(no_key[:, (NCB - NC) * P + 1:], -2.0).then_inc(s_no_key, 1)
                dve.wait_ge(s_dst, 16 * CQ)
                step(nc.vector.tensor_copy(dst_f[:, :, :], dst_rows[:, :, :]))
                for q in range(CQ):
                    ins = nc.vector.tensor_scalar(lane_f[:, q, :], dst_f[:, q, :], k.node_of_row[:, q:q + 1], None, ALU.subtract)
                ins.then_inc(s_ready, 1)
                dve.wait_ge(s_ready, 1)
                step(nc.vector.tensor_scalar(own[:, :, :], lane_f[:, :, :], float(P), None, ALU.is_lt))
                nc.vector.scalar_tensor_tensor(keys[:, :, :], dst_f[:, :, :], 1.0, own[:, :, :], ALU.add,
                                               ALU.mult).then_inc(s_keyed, 1)
                dve.wait_ge(s_src, 16 * CQ)
                nc.vector.tensor_copy(src_f[:, :, :], src_rows[:, :, :]).then_inc(s_ready, 1)
                dve.wait_ge(s_rec_b, 16)
                step(nc.vector.tensor_copy(k.dst_at[:, 0:NC], rec_b[:, :, 0]))
                step(nc.vector.tensor_copy(k.lane_b[:, 0:NC], rec_b[:, :, 1]))
                step(nc.vector.tensor_copy(k.weight[:, :], rec_b[:, :, 2]))
                dve.wait_ge(s_turned, 2)
                step(nc.vector.tensor_copy(k.lane_a[:, 0:NC].rearrange("p (q c) -> p q c", q=CQ), ps_turn[:, 0, :, 0:CR]))
                step(nc.vector.tensor_copy(k.src_at[:, 0:NC].rearrange("p (q c) -> p q c", q=CQ), ps_turn[:, 1, :, 0:CR]))
                dve.wait_ge(s_key_rows, 16 * H)
                step(nc.vector.tensor_tensor(k.new_node[:, :], key_rows[:, 1:], key_rows[:, 0:BC * P + 1], ALU.not_equal))
                step(nc.vector.tensor_scalar(k.new_node[:, :], k.new_node[:, :], -BIG, None, ALU.mult))


def tile_statistics(nc, dve, rows, stats, mv1, mv, s_stats, s_aggr, s_hold, s_mv):
    def tiles(i, first):
        for u in range(2):
            nc.vector.bn_stats(stats[:, u, :], rows[:, at(2 * i + u, 1), :]
                               .rearrange("p o d -> p (o d)")).then_inc(s_stats, 1)
        for u in range(2):
            dve.wait_ge(s_stats, 2 * i + u + 1)
            dve.sem_inc(s_hold, 1)
            nc.vector.bn_aggr(mv1[:, u, :], stats[:, u, :]).then_inc(s_aggr, 1)
        for u in range(2):
            dve.wait_ge(s_aggr, 2 * i + u + 1)
            nc.vector.tensor_copy(mv[:, at(2 * i + u, 1), :], mv1[:, u:u + 1, :]).then_inc(s_mv, 1)
        dve.wait_ge(s_mv, 2 * i + 2)
    rounds(dve, T // 2, tiles)


class RoundChain:

    def __init__(self, eng, sem):
        self.eng, self.sem, self.per = eng, sem, 0

    def start(self, i, first):
        self.base, self.n = (0 if first else i * self.per), 0

    def __call__(self, instruction):
        self.n += 1
        self.per = max(self.per, self.n)
        instruction.then_inc(self.sem, 1)
        self.eng.wait_ge(self.sem, self.base + self.n)


@phase
def norm_stats(nc, new_semaphore, k, name, rows):
    def sem(what):
        return new_semaphore(f"{name}_{what}")

    with ExitStack() as tmp:
        stats = tmp.enter_context(nc.sbuf_tensor(f"{name}_stats", [P, 2, 6], F32))
        mv1 = tmp.enter_context(nc.sbuf_tensor(f"{name}_mv1", [P, 2, 2], F32))
        mv = tmp.enter_context(nc.sbuf_tensor(f"{name}_mv", [P, T, 2], F32))
        var = tmp.enter_context(nc.sbuf_tensor(f"{name}_var", [P, T], F32))
        dev = tmp.enter_context(nc.sbuf_tensor(f"{name}_dev", [P, T], F32))
        s_stats = sem("stats")
        s_aggr = sem("aggr")
        s_hold = sem("hold")
        s_mv = sem("mv")
        s_step = sem("step")
        s_var = sem("var")
        s_dev = sem("dev")
        with nc.Block() as block:
            @block.vector
            def _(dve):
                tile_statistics(nc, dve, rows, stats, mv1, mv, s_stats, s_aggr, s_hold, s_mv)
                step = Chain(dve, s_step)
                nc.vector.tensor_scalar(var[:, :], mv[:, :, 1], EPS, None, ALU.add).then_inc(s_var, 1)
                dve.wait_ge(s_dev, 1)
                step(nc.vector.reciprocal(k.rstd[:, :], dev[:, :]))
                step(nc.vector.scalar_tensor_tensor(k.shift[:, :], mv[:, :, 0], -1.0, k.rstd[:, :], ALU.mult, ALU.mult))

            @block.scalar
            def _(act):
                act.wait_ge(s_var, 1)
                nc.scalar.activation(dev[:, :], var[:, :], ACT.Sqrt).then_inc(s_dev, 1)


def tile_ap(rows, t):
    return rows[:, at(t, 1), :].rearrange("p o d -> p (o d)")


@phase
def project_phase(nc, new_semaphore, k, name, blocks, width, weights, prepare, finish, prepare_on="act", keep=None, store=None,
                  setup=None):
    def sem(what):
        return new_semaphore(f"{name}_{what}")

    banks = -(-width // 512)
    with ExitStack() as tmp:
        rows = tmp.enter_context(nc.sbuf_tensor(f"{name}_rows", [P, 2, blocks * P], F32))
        cols = tmp.enter_context(nc.sbuf_tensor(f"{name}_cols", [P, 2, blocks, P], F32))
        slots = tmp.enter_context(nc.sbuf_tensor(f"{name}_slots", [P, 2, 3 * D], F32))
        spare = tmp.enter_context(nc.sbuf_tensor(f"{name}_spare", [P, 2, 2, 2 * D], F32))
        ps_turn = tmp.enter_context(nc.psum_tensor(f"{name}_ps_turn", [P, 2, 4, P], F32))
        ps_out = tmp.enter_context(nc.psum_tensor(f"{name}_ps_out", [P, 2, banks * 512], F32))
        s_setup = sem("setup")
        s_rows = sem("rows")
        s_turned = sem("turned")
        s_cols = sem("cols")
        s_out = sem("out")
        s_done = sem("done")
        s_prep = sem("prep_step")
        s_step = sem("step")
        s_kept = [sem(f"kept{u}") for u in range(2)]
        s_stored = [sem(f"stored{u}") for u in range(2)]
        stores = len(store(0, slots[:, 0, :])) if store else 0

        def prepare_rows(eng, chain, i, first):
            for u in range(2):
                t = 2 * i + u
                if not first:
                    eng.wait_ge(s_turned, t - 1)
                    if keep:
                        eng.wait_ge(s_kept[u], 16 * i)
                prepare(chain, t, u, rows[:, u, :]).then_inc(s_rows, 1)

        with nc.Block() as block:
            @block.scalar
            def _(act):
                if prepare_on == "act":
                    chain = RoundChain(act, s_prep)

                    def tiles(i, first):
                        chain.start(i, first)
                        prepare_rows(act, chain, i, first)
                    rounds(act, T // 2, tiles)

            @block.vector
            def _(dve):
                if setup:
                    setup(Chain(dve, s_setup))
                chain = RoundChain(dve, s_step)

                def tiles(i, first):
                    chain.start(i, first)
                    if prepare_on == "dve":
                        prepare_rows(dve, chain, i, first)
                    for u in range(2):
                        dve.wait_ge(s_turned, 2 * i + u + 1)
                        if not first:
                            dve.wait_ge(s_out, 2 * i + u - 1)
                        nc.vector.tensor_copy(cols[:, u, :, :], ps_turn[:, u, 0:blocks, :]).then_inc(s_cols, 1)
                    for u in range(2):
                        dve.wait_ge(s_out, 2 * i + u + 1)
                        if stores and not first:
                            dve.wait_ge(s_stored[u], 16 * stores * i)
                        finish(chain, 2 * i + u, ps_out[:, u, 0:width], slots[:, u, :], spare[:, u, :, :])\
                            .then_inc(s_done, 1)
                rounds(dve, T // 2, tiles)

            @block.tensor
            def _(pe):
                def tiles(i, first):
                    for u in range(2):
                        pe.wait_ge(s_rows, 2 * i + u + 1)
                        if not first:
                            pe.wait_ge(s_cols, 2 * i + u - 1)
                        for b in range(blocks):
                            ins = nc.tensor.transpose(ps_turn[:, u, b, :], rows[:, u, b * P:(b + 1) * P], k.ident[:, :])
                        ins.then_inc(s_turned, 1)
                    for u in range(2):
                        pe.wait_ge(s_cols, 2 * i + u + 1)
                        if not first:
                            pe.wait_ge(s_done, 2 * i + u - 1)
                        for w0 in range(0, width, 512):
                            w1 = min(width, w0 + 512)
                            for b in range(blocks):
                                ins = nc.tensor.matmul(ps_out[:, u, w0:w1], cols[:, u, b, :], weights[:, b, w0:w1],
                                                       start=(b == 0), stop=(b == blocks - 1))
                        ins.then_inc(s_out, 1)
                rounds(pe, T // 2, tiles)

            @block.sync
            def _(sp):
                if keep:
                    def keeps(i, first):
                        for u in range(2):
                            sp.wait_ge(s_rows, 2 * i + u + 1)
                            sp.dma_start(keep(2 * i + u), rows[:, u, 0:D]).then_inc(s_kept[u], 16)
                        if store:
                            put(i)

                if store:
                    def put(i):
                        for u in range(2):
                            sp.wait_ge(s_done, 2 * i + u + 1)
                            for to, what in store(2 * i + u, slots[:, u, :]):
                                sp.dma_start(to, what).then_inc(s_stored[u], 16)
                if keep:
                    rounds(sp, T // 2, keeps)
                elif store:
                    rounds(sp, T // 2, lambda i, first: put(i))
                for u in range(2):
                    if keep:
                        sp.wait_ge(s_kept[u], 16 * (T // 2))
                    if store:
                        sp.wait_ge(s_stored[u], 16 * stores * (T // 2))


def rows_of(dram, t):
    return dram[at(t * P, P), :]


def tile_registers(nc, eng, tiles, c, size):
    return nc.values_load_multi_w_load_instructions(
        tiles[0:1, at(c, size)], [eng], min_val=0, max_val=T - 1,
        skip_runtime_bounds_check_because="a count of at most TR - 1 tiles")[1]


def gather_rounds(pool, k, s_idx, s_go, s_landed, idx, gathered, table, free):
    def groups(i, first):
        for u in range(2):
            g = 2 * i + u
            if not first:
                free(u, g)
            pool.wait_ge(s_idx, g + 1)
            pool.sem_inc(s_go, 1)
            for j in range(G):
                pool.indirect_dma_start(gathered[:, u, j, :], None, table,
                                        bass.IndirectOffsetOnAxis(idx[:, u, j:j + 1], 0)).then_inc(s_landed[u], 16)
    rounds(pool, IT, groups)


def stage_index(nc, act, i, first, u, idx, source, s_landed, s_idx):
    g = 2 * i + u
    if first and u == 0:
        nc.scalar.copy(idx[:, 0, :], source[:, at(0, G)]).then_inc(s_idx, 1)
    else:
        act.wait_ge(s_landed[1 - u], 16 * G * (i + u))
    nc.scalar.copy(idx[:, 1 - u, :], source[:, at((g + 1) * G, G)]).then_inc(s_idx, 1)


@phase
def score_phase(nc, new_semaphore, k, name, table, width, parts):
    def sem(what):
        return new_semaphore(f"{name}_{what}")

    dots = width == D
    with ExitStack() as tmp:
        def sb(what, shape, dt):
            return tmp.enter_context(nc.sbuf_tensor(f"{name}_{what}", shape, dt))

        idx = sb("idx", [P, 2, G], I32)
        gathered = sb("gathered", [P, 2, G, width], F32)
        is_lane = sb("is_lane", [P, 2, G, P], BF16)
        lane_is = sb("lane_is", [P, 2, G, P], BF16)
        products = sb("products", [P, 2, G, width], F32)
        ps_turn = tmp.enter_context(nc.psum_tensor(f"{name}_ps_turn", [P, 2, 2 * G, P], BF16))
        ps_rows = tmp.enter_context(nc.psum_tensor(f"{name}_ps_rows", [P, 2, G, max(width, D)], F32))
        s_idx = sem("idx")
        s_go = sem("go")
        s_landed = [sem(f"landed{u}") for u in range(2)]
        s_lane = sem("lane")
        s_turned = sem("turned")
        s_cols = sem("cols")
        s_rows = sem("rows")
        s_prod = sem("prod")
        s_score = sem("score")

        with nc.Block() as block:
            @block.scalar
            def _(act):
                def columns(g, u, n):
                    act.wait_ge(s_turned, g + 1)
                    if n >= 2:
                        act.wait_ge(s_rows, g - 1)
                    nc.scalar.copy(lane_is[:, u, :, :], ps_turn[:, u, 0:G, :]).then_inc(s_cols, 1)

                def groups(i, first):
                    if first:
                        columns(0, 0, 0)
                    for u in range(2):
                        stage_index(nc, act, i, first, u, idx, k.src_at, s_landed, s_idx)
                        columns(2 * i + u + 1, 1 - u, u + 1 if first else 2)
                rounds(act, IT, groups)

            @block.gpsimd
            def _(pool):
                gather_rounds(pool, k, s_idx, s_go, s_landed, idx, gathered, table,
                              lambda u, g: pool.wait_ge(s_prod, g - 1))

            @block.tensor
            def _(pe):
                def turn(g, u, n):
                    pe.wait_ge(s_lane, g + 1)
                    if n >= 2:
                        pe.wait_ge(s_cols, g - 1)
                    for j in range(G):
                        ins = nc.tensor.transpose(ps_turn[:, u, j, :], is_lane[:, u, j, :], k.ident_b[:, :])
                    ins.then_inc(s_turned, 1)

                def groups(i, first):
                    if first:
                        turn(0, 0, 0)
                    for u in range(2):
                        g = 2 * i + u
                        tiles = tile_registers(nc, mybir.EngineType.PE, k.tile_ia, g * G, G)
                        pe.wait_ge(s_cols, g + 1)
                        if not first:
                            pe.wait_ge(s_prod, g - 1)
                        for j in range(G):
                            for part in range(3):
                                ins = nc.tensor.matmul(ps_rows[:, u, j, 0:width], lane_is[:, u, j, :],
                                                       parts[:, at(tiles[j], 1), part, :],
                                                       start=(part == 0), stop=(part == 2))
                        ins.then_inc(s_rows, 1)
                        turn(g + 1, 1 - u, u + 1 if first else 2)
                rounds(pe, IT, groups)

            @block.vector
            def _(dve):
                def lanes(g, u, n):
                    if n >= 2:
                        dve.wait_ge(s_turned, g - 1)
                    nc.vector.tensor_tensor(is_lane[:, u, :, :], k.lane[:, :].unsqueeze(1).to_broadcast([P, G, P]),
                                            k.lane_a[:, at(g * G, G)].unsqueeze(2).to_broadcast([P, G, P]),
                                            ALU.is_equal).then_inc(s_lane, 1)

                def groups(i, first):
                    if first:
                        lanes(0, 0, 0)
                    for u in range(2):
                        g = 2 * i + u
                        lanes(g + 1, 1 - u, u + 1 if first else 2)
                        dve.wait_ge(s_landed[u], 16 * G * (i + 1))
                        dve.wait_ge(s_rows, g + 1)
                        if not first:
                            dve.wait_ge(s_score, g - 1)
                        nc.vector.tensor_tensor(products[:, u, :, :], gathered[:, u, :, :], ps_rows[:, u, :, 0:width],
                                                ALU.mult if dots else ALU.add).then_inc(s_prod, 1)
                        dve.wait_ge(s_prod, g + 1)
                        scores = k.scores[:, at(g * G, G), :]
                        if dots:
                            nc.vector.tensor_reduce(scores, products[:, u, :, :].rearrange("p j (h c) -> p j h c", h=H),
                                                    AX_X, ALU.add).then_inc(s_score, 1)
                        else:
                            nc.vector.scalar_tensor_tensor(scores, products[:, u, :, :], 0.2, products[:, u, :, :],
                                                           ALU.mult, ALU.max).then_inc(s_score, 1)
                rounds(dve, IT, groups)


@phase
def weights_of_edges_phase(nc, new_semaphore, k, name, scale, last=None):
    def sem(what):
        return new_semaphore(f"{name}_{what}")

    L = BC * P
    with ExitStack() as tmp:
        def sb(what, shape, dt):
            return tmp.enter_context(nc.sbuf_tensor(f"{name}_{what}", shape, dt))

        stage = sb("stage", [P, 2, P], F32)
        line = sb("line", [P, BC, P], F32)
        run = sb("run", [P, L], F32)
        only_last = sb("only_last", [P, BC, P], F32) if last is not None else None
        kill = sb("kill", [P, 2], F32)
        end = sb("end", [P, 1], F32)
        row = sb("row", [1, 2, P], F32)
        chain_row = sb("chain_row", [1, P + 2], F32)
        carry = sb("carry", [P, 1], F32)
        ps_turn = tmp.enter_context(nc.psum_tensor(f"{name}_ps_turn", [P, 2, 512], F32))
        ps_row = tmp.enter_context(nc.psum_tensor(f"{name}_ps_row", [1, 2, P], F32))
        ps_carry = tmp.enter_context(nc.psum_tensor(f"{name}_ps_carry", [P, 2], F32))
        s_stage = sem("stage")
        s_turned = sem("turned")
        s_line = sem("line")
        s_step = sem("step")
        s_ends = sem("ends")
        s_endrow = sem("endrow")
        s_chain = sem("chain")
        s_carry = sem("carry")
        s_max = sem("max")
        s_bstage = sem("bstage")
        s_bturned = sem("bturned")
        s_less = sem("less")
        whole = line[:, :, :].rearrange("p g e -> p (g e)")
        by_block = k.scores[:, :, :].rearrange("p (b g) h -> p g b h", g=BC)
        backs = 2 if last is not None else 1
        flag = k.new_node

        with nc.Block() as block:
            @block.scalar
            def _(act):
                def there(i, first):
                    for u in range(2):
                        g = 2 * i + u
                        if not first:
                            act.wait_ge(s_turned, g - 1)
                        nc.scalar.copy(stage[:, u, :].rearrange("p (h b) -> p h b", h=H),
                                       by_block[:, at(g, 1), :, :].rearrange("p o b h -> p (o h) b")).then_inc(s_stage, 1)
                rounds(act, BC // 2, there)
                act.wait_ge(s_max, 1)
                for back, source in enumerate([line, only_last][:backs]):
                    def here(i, first):
                        for u in range(2):
                            n = back * BC + 2 * i + u
                            if not first or back:
                                act.wait_ge(s_bturned, n - 1)
                            nc.scalar.copy(stage[:, u, :], tile_ap(source, 2 * i + u)).then_inc(s_bstage, 1)
                    act.wait_ge(s_turned, BC)
                    rounds(act, BC // 2, here)
                act.wait_ge(s_less, backs * BC)
                nc.scalar.activation(k.scores[:, :, :], k.scores[:, :, :], ACT.Exp, scale=scale)

            @block.tensor
            def _(pe):
                def there(i, first):
                    for u in range(2):
                        g = 2 * i + u
                        pe.wait_ge(s_stage, g + 1)
                        if not first:
                            pe.wait_ge(s_line, g - 1)
                        nc.tensor.transpose(ps_turn[:, u, 0:P], stage[:, u, :], k.ident[:, :]).then_inc(s_turned, 1)
                rounds(pe, BC // 2, there)
                for n in range(2):
                    pe.wait_ge(s_ends, n + 1)
                    nc.tensor.transpose(ps_row[:, 0, :], kill[:, n:n + 1], k.ident[:, :])
                    nc.tensor.transpose(ps_row[:, 1, :], end[:, :], k.ident[:, :]).then_inc(s_endrow, 1)
                    pe.wait_ge(s_chain, n + 1)
                    nc.tensor.transpose(ps_carry[:, n:n + 1], chain_row[0:1, 2 * n:2 * n + P],
                                        k.ident[0:1, 0:1]).then_inc(s_carry, 1)
                for back in range(backs):
                    def here(i, first):
                        for u in range(2):
                            n = back * BC + 2 * i + u
                            pe.wait_ge(s_bstage, n + 1)
                            if not first or back:
                                pe.wait_ge(s_less, n - 1)
                            nc.tensor.transpose(ps_turn[:, u, 0:P], stage[:, u, :], k.ident[:, :]).then_inc(s_bturned, 1)
                    pe.wait_ge(s_line, BC)
                    rounds(pe, BC // 2, here)

            @block.vector
            def _(dve):
                def there(i, first):
                    for u in range(2):
                        g = 2 * i + u
                        dve.wait_ge(s_turned, g + 1)
                        nc.vector.tensor_copy(tile_ap(line, g), ps_turn[:, u, 0:P]).then_inc(s_line, 1)
                rounds(dve, BC // 2, there)
                step = Chain(dve, s_step)
                dve.wait_ge(s_line, BC)
                for n, (flags, source, target, way, last_at) in enumerate((
                        (flag[:, 0:L], whole, run[:, :], slice(None, None, 1), L - 1),
                        (flag[:, 1:L + 1], run[:, :], whole, slice(None, None, -1), 0))):
                    step(nc.vector.tensor_reduce(kill[:, n:n + 1], flags, AX_X, ALU.min))
                    step(nc.vector.tensor_tensor_scan(target[:, way], flags[:, way], source[:, way], -BIG, ALU.add, ALU.max))
                    nc.vector.tensor_copy(end[:, :], target[:, last_at:last_at + 1]).then_inc(s_ends, 1)
                    step(nc.vector.memset(chain_row[:, :], -BIG))
                    dve.wait_ge(s_endrow, n + 1)
                    step(nc.vector.tensor_copy(row[:, :, :], ps_row[:, :, :]))
                    nc.vector.tensor_tensor_scan(chain_row[:, 1:P + 1][:, way], row[:, 0, :][:, way], row[:, 1, :][:, way],
                                                 -BIG, ALU.add, ALU.max).then_inc(s_chain, 1)
                    dve.wait_ge(s_carry, n + 1)
                    step(nc.vector.tensor_copy(carry[:, :], ps_carry[:, n:n + 1]))
                    step(nc.vector.tensor_tensor_scan(target[:, way], flags[:, way], source[:, way], carry[:, :],
                                                      ALU.add, ALU.max))
                if last is not None:
                    step(nc.vector.scalar_tensor_tensor(only_last[:, :, :].rearrange("p g e -> p (g e)"),
                                                        flag[:, 1:L + 1], -1.0, whole, ALU.is_lt, ALU.mult))
                dve.sem_inc(s_max, 1)
                for back in range(backs):
                    def here(i, first):
                        for u in range(2):
                            g = 2 * i + u
                            dve.wait_ge(s_bturned, back * BC + g + 1)
                            turned = ps_turn[:, u, 0:P].rearrange("p (h b) -> p b h", h=H)
                            mine = by_block[:, at(g, 1), :, :].rearrange("p o b h -> p (o b) h")
                            if back == 0:
                                nc.vector.tensor_tensor(mine, mine, turned, ALU.subtract).then_inc(s_less, 1)
                            else:
                                nc.vector.tensor_copy(last[:, :, :].rearrange("p (b g) h -> p g b h", g=BC)[:, at(g, 1), :, :]
                                                      .rearrange("p o b h -> p (o b) h"), turned).then_inc(s_less, 1)
                    rounds(dve, BC // 2, here)


@phase
def sum_phase(nc, new_semaphore, k, name, table, sums, heads, last=None):
    row_at, lane_of, tile_ids = ((k.src_at, k.lane_a, k.tile_ia) if heads else (k.dst_at, k.lane_b, k.tile_ib))

    def sem(what):
        return new_semaphore(f"{name}_{what}")

    width = sums.shape[2]
    with ExitStack() as tmp:
        def sb(what, shape, dt):
            return tmp.enter_context(nc.sbuf_tensor(f"{name}_{what}", shape, dt))

        idx = sb("idx", [P, 2, G], I32)
        gathered = sb("gathered", [P, 2, G, D], F32)
        is_lane = sb("is_lane", [P, 2, G, P], F32)
        values = sb("values", [P, 2, G, width], F32)
        ps_sums = tmp.enter_context(nc.psum_tensor(f"{name}_ps_sums", [P, 2 * G, 512], F32))
        s_idx = sem("idx")
        s_go = sem("go")
        s_landed = [sem(f"landed{u}") for u in range(2)]
        s_zero = sem("zero")
        s_extra = sem("extra")
        s_values = sem("values")
        s_lane = sem("lane")
        s_sums = sem("sums")
        s_added = sem("added")

        with nc.Block() as block:
            @block.scalar
            def _(act):
                def groups(i, first):
                    for u in range(2):
                        g = 2 * i + u
                        stage_index(nc, act, i, first, u, idx, row_at, s_landed, s_idx)
                        if heads:
                            if not first:
                                act.wait_ge(s_sums, G * (g - 1))
                            ins = nc.scalar.copy(values[:, u, :, D:D + H], k.scores[:, at(g * G, G), :])
                            if last is not None:
                                ins = nc.scalar.copy(values[:, u, :, D + H:D + 2 * H], last[:, at(g * G, G), :])
                            ins.then_inc(s_extra, 1)
                        else:
                            act.wait_ge(s_landed[u], 16 * G * (i + 1))
                            if not first:
                                act.wait_ge(s_sums, G * (g - 1))
                            for j in range(G):
                                ins = nc.scalar.activation(values[:, u, j, 0:D], gathered[:, u, j, :], ACT.Copy,
                                                           scale=k.weight[:, at(g * G + j, 1)])
                            ins.then_inc(s_values, 1)
                act.wait_ge(s_zero, 2)
                rounds(act, IT, groups)

            @block.gpsimd
            def _(pool):
                gather_rounds(pool, k, s_idx, s_go, s_landed, idx, gathered, table,
                              lambda u, g: pool.wait_ge(s_values, g - 1))

            @block.tensor
            def _(pe):
                def groups(i, first):
                    for u in range(2):
                        g = 2 * i + u
                        pe.wait_ge(s_lane, g + 1)
                        pe.wait_ge(s_values, g + 1)
                        if heads:
                            pe.wait_ge(s_extra, g + 1)
                        for j in range(G):
                            if not first:
                                pe.wait_ge(s_added, G * (g - 2) + j + 1)
                            nc.tensor.matmul(ps_sums[:, G * u + j, 0:width], is_lane[:, u, j, :], values[:, u, j, :],
                                             start=True, stop=True).then_inc(s_sums, 1)
                pe.wait_ge(s_zero, 2)
                rounds(pe, IT, groups)

            @block.vector
            def _(dve):
                nc.vector.memset(sums[:, :, :], 0.0).then_inc(s_zero, 1)
                nc.vector.memset(values[:, :, :, width - 1:width], 1.0).then_inc(s_zero, 1)
                dve.wait_ge(s_zero, 2)

                def make(i, first, u):
                    g = 2 * i + u
                    if not first:
                        dve.wait_ge(s_sums, G * (g - 1))
                    for j in range(G):
                        ins = nc.vector.tensor_scalar(is_lane[:, u, j, :], k.lane[:, :], lane_of[:, at(g * G + j, 1)],
                                                      None, ALU.is_equal)
                    ins.then_inc(s_lane, 1)
                    if heads:
                        dve.wait_ge(s_landed[u], 16 * G * (i + 1))
                        nc.vector.tensor_tensor(
                            values[:, u, :, 0:D].rearrange("p j (h c) -> p j h c", h=H),
                            gathered[:, u, :, :].rearrange("p j (h c) -> p j h c", h=H),
                            k.scores[:, at(g * G, G), :].unsqueeze(3).to_broadcast([P, G, H, C]),
                            ALU.mult).then_inc(s_values, 1)

                def add(i, u, first):
                    g = 2 * i + u
                    tiles = tile_registers(nc, mybir.EngineType.DVE, tile_ids, g * G, G)
                    for j in range(G):
                        dve.wait_ge(s_sums, g * G + j + 1)
                        if not (first and j == 0):
                            dve.wait_ge(s_added, g * G + j)
                        to = tile_ap(sums, tiles[j])
                        nc.vector.tensor_tensor(to, to, ps_sums[:, G * u + j, 0:width], ALU.add).then_inc(s_added, 1)

                def groups(i, first):
                    make(i, first, 0)
                    if not first:
                        add(i - 1, 1, False)
                    make(i, first, 1)
                    add(i, 0, first)
                rounds(dve, IT, groups)
                add(IT - 1, 1, False)



@phase
def combine_loops_phase(nc, new_semaphore, k, sums):
    def sem(name):
        return new_semaphore(name)

    with ExitStack() as tmp:
        def sb(name, shape):
            return tmp.enter_context(nc.sbuf_tensor(name, shape, F32))

        own = sb("own_logit", [P, T, H])
        z = sb("own_z", [P, T, H])
        top = sb("top_logit", [P, T, H])
        old = sb("old_part", [P, T, H])
        new = sb("new_part", [P, T, H])
        s_step = sem("s_loop_step")
        s_less = sem("s_loop_less")
        s_exp = sem("s_loop_exp")
        weight, largest = sums[:, :, D:D + H], sums[:, :, D + H:D + 2 * H]
        rows = sums[:, :, 0:D].rearrange("p t (h c) -> p t h c", h=H)
        xl = k.xl[:, :, :].rearrange("p t (h c) -> p t h c", h=H)

        with nc.Block() as block:
            @block.vector
            def _(dve):
                step = Chain(dve, s_step)
                step(nc.vector.tensor_tensor(z[:, :, :], k.of_src[:, :, :], k.of_dst[:, :, :], ALU.add))
                step(nc.vector.scalar_tensor_tensor(own[:, :, :], z[:, :, :], 0.2, z[:, :, :], ALU.mult, ALU.max))
                step(nc.vector.tensor_scalar(z[:, :, :], weight, 0.5, -BIG, ALU.is_lt, ALU.mult))
                step(nc.vector.tensor_tensor(old[:, :, :], z[:, :, :], largest, ALU.add))
                step(nc.vector.tensor_tensor(top[:, :, :], old[:, :, :], own[:, :, :], ALU.max))
                step(nc.vector.tensor_tensor(old[:, :, :], old[:, :, :], top[:, :, :], ALU.subtract))
                step(nc.vector.tensor_tensor(new[:, :, :], own[:, :, :], top[:, :, :], ALU.subtract))
                dve.sem_inc(s_less, 1)
                dve.wait_ge(s_exp, 2)
                step(nc.vector.tensor_tensor(z[:, :, :], weight, old[:, :, :], ALU.mult))
                step(nc.vector.tensor_tensor(z[:, :, :], z[:, :, :], new[:, :, :], ALU.add))
                step(nc.vector.reciprocal(top[:, :, :], z[:, :, :]))
                step(nc.vector.tensor_tensor(old[:, :, :], old[:, :, :], top[:, :, :], ALU.mult))
                step(nc.vector.tensor_tensor(new[:, :, :], new[:, :, :], top[:, :, :], ALU.mult))
                step(nc.vector.tensor_tensor(xl, xl, new[:, :, :].unsqueeze(3).to_broadcast([P, T, H, C]), ALU.mult))
                step(nc.vector.tensor_tensor(rows, rows, old[:, :, :].unsqueeze(3).to_broadcast([P, T, H, C]), ALU.mult))
                step(nc.vector.tensor_tensor(k.xl[:, :, :], k.xl[:, :, :], sums[:, :, 0:D], ALU.add))
                step(nc.vector.tensor_tensor(k.xl[:, :, :], k.xl[:, :, :], k.b2[:, :].unsqueeze(1).to_broadcast([P, T, D]),
                                             ALU.add))

            @block.scalar
            def _(act):
                act.wait_ge(s_less, 1)
                nc.scalar.activation(old[:, :, :], old[:, :, :], ACT.Exp).then_inc(s_exp, 1)
                nc.scalar.activation(new[:, :, :], new[:, :, :], ACT.Exp).then_inc(s_exp, 1)


@phase
def norm_of_layer_phase(nc, new_semaphore, k):
    s_step = new_semaphore("s_norm2_step")
    s_scaled = new_semaphore("s_norm2_scaled")
    with nc.Block() as block:
        @block.scalar
        def _(act):
            def tiles(i, first):
                for u in range(2):
                    t = 2 * i + u
                    nc.scalar.activation(tile_ap(k.xl, t), tile_ap(k.xl, t), ACT.Identity, bias=k.shift[:, at(t, 1)],
                                         scale=k.rstd[:, at(t, 1)]).then_inc(s_scaled, 1)
            rounds(act, T // 2, tiles)

        @block.vector
        def _(dve):
            step = Chain(dve, s_step)
            step(nc.vector.tensor_tensor(k.x[:, :, :], k.x[:, :, :], k.beta[:, :].unsqueeze(1).to_broadcast([P, T, D]),
                                         ALU.add))
            dve.wait_ge(s_scaled, T)
            step(nc.vector.tensor_tensor(k.xl[:, :, :], k.xl[:, :, :], k.gamma[:, :].unsqueeze(1).to_broadcast([P, T, D]),
                                         ALU.mult))
            step(nc.vector.tensor_tensor(k.x[:, :, :], k.x[:, :, :], k.xl[:, :, :], ALU.add))


@phase
def logit_parts_phase(nc, new_semaphore, k):
    s_step = new_semaphore("s_parts_step")
    s_out = new_semaphore("s_of_src_out")
    with ExitStack() as tmp:
        left = tmp.enter_context(nc.sbuf_tensor("parts_left", [P, T, H], F32))
        with nc.Block() as block:
            @block.sync
            def _(sp):
                sp.dma_start(k.of_src_table.rearrange("(t p) h -> p t h", p=P), k.of_src[:, :, :]).then_inc(s_out, 16)
                sp.wait_ge(s_out, 16)

            @block.vector
            def _(dve):
                step = Chain(dve, s_step)
                step(nc.vector.tensor_copy(k.of_dst_parts[:, :, 0, :], k.of_dst[:, :, :]))
                step(nc.vector.tensor_tensor(left[:, :, :], k.of_dst[:, :, :], k.of_dst_parts[:, :, 0, :], ALU.subtract))
                step(nc.vector.tensor_copy(k.of_dst_parts[:, :, 1, :], left[:, :, :]))
                step(nc.vector.tensor_tensor(k.of_dst_parts[:, :, 2, :], left[:, :, :], k.of_dst_parts[:, :, 1, :],
                                             ALU.subtract))


def split_parts(nc, step, parts, t, value, left):
    def part(n):
        return parts[:, at(t, 1), n, :].rearrange("p o d -> p (o d)")
    step(nc.vector.tensor_copy(part(0), value))
    step(nc.vector.tensor_tensor(left, value, part(0), ALU.subtract))
    step(nc.vector.tensor_copy(part(1), left))
    return nc.vector.tensor_tensor(part(2), left, part(1), ALU.subtract)


A_PARTS = (0, 0, 0, 1, 1, 1, 2, 2)
W_PARTS = (0, 1, 2, 0, 1, 2, 0, 1)


@phase
def attribute_weights_phase(nc, new_semaphore, k, a):
    def sem(name):
        return new_semaphore(name)

    with ExitStack() as tmp:
        w = tmp.enter_context(nc.sbuf_tensor("w_attr_raw", [EA, HID], F32))
        left = tmp.enter_context(nc.sbuf_tensor("w_attr_left", [EA, HID], F32))
        parts = tmp.enter_context(nc.sbuf_tensor("w_attr_parts", [EA, 3, HID], BF16))
        s_w = sem("s_w_attr")
        s_step = sem("s_w_attr_step")
        s_split = sem("s_w_attr_split")
        s_stacked = sem("s_w_attr_stacked")
        s_rows = sem("s_w3")
        with nc.Block() as block:
            @block.sync
            def _(sp):
                sp.dma_start(w[:, :], a['L3_gnn_mW1'][2 * D:2 * D + EA, :]).then_inc(s_w, 16)
                for half in range(2):
                    sp.dma_start(k.w_node[:, :, half * HID:(half + 1) * HID],
                                 a['L3_gnn_mW1'][half * D:(half + 1) * D, :].rearrange("(b p) n -> p b n", p=P))\
                        .then_inc(s_rows, 16)
                sp.dma_start(k.b_m1[:, :], a['L3_gnn_mb1'].partition_broadcast(P)).then_inc(s_rows, 16)
                sp.wait_ge(s_split, 1)
                for n, part in enumerate(W_PARTS):
                    sp.dma_start(k.w_attr[n * EA:(n + 1) * EA, :], parts[:, part, :]).then_inc(s_stacked, 16)
                sp.wait_ge(s_stacked, 16 * len(W_PARTS))
                sp.wait_ge(s_rows, 48)

            @block.vector
            def _(dve):
                step = Chain(dve, s_step)
                dve.wait_ge(s_w, 16)
                step(nc.vector.tensor_copy(parts[:, 0, :], w[:, :]))
                step(nc.vector.tensor_tensor(left[:, :], w[:, :], parts[:, 0, :], ALU.subtract))
                step(nc.vector.tensor_copy(parts[:, 1, :], left[:, :]))
                step(nc.vector.tensor_tensor(parts[:, 2, :], left[:, :], parts[:, 1, :], ALU.subtract))
                dve.sem_inc(s_split, 1)


@phase
def message_phase(nc, new_semaphore, k, table, parts, sums):
    def sem(name):
        return new_semaphore(f"m_{name}")

    PAIRS = len(A_PARTS)
    with ExitStack() as tmp:
        def sb(name, shape, dt):
            return tmp.enter_context(nc.sbuf_tensor(f"m_{name}", shape, dt))

        raw = sb("raw", [P, 2, G, EA], F32)
        idx = sb("idx", [P, 2, G], I32)
        gathered = sb("gathered", [P, 2, G, HID], F32)
        hidden = k.x[:, 0:2 * G * HID // D, :].rearrange("p t d -> p (t d)")\
            .rearrange("p (u j f) -> p u j f", u=2, j=G)
        is_lane = sb("is_lane", [P, 2, G, P], F32)
        is_lane_b = sb("is_lane_b", [P, 2, G, P], BF16)
        lane_is = sb("lane_is", [P, 2, G, P], BF16)
        attr = sb("attr", [P, 2, G, PAIRS, EA], BF16)
        attr_turned = sb("attr_turned", [P, 2, G, P], BF16)
        left = sb("left", [P, 2, 2, G, EA], F32)
        ps_turn = tmp.enter_context(nc.psum_tensor("m_ps_turn", [P, 2, 2, G, P], BF16))
        ps_lane, ps_attr = ps_turn[:, :, 0, :, :], ps_turn[:, :, 1, :, :]
        ps_hidden = tmp.enter_context(nc.psum_tensor("m_ps_hidden", [P, 2, HID], F32))
        ps_sums = tmp.enter_context(nc.psum_tensor("m_ps_sums", [P, 2, HID], F32))
        s_raw = [sem(f"raw{u}") for u in range(2)]
        s_idx = sem("idx")
        s_go = sem("go")
        s_landed = [sem(f"landed{u}") for u in range(2)]
        s_zero = sem("zero")
        s_lane = sem("lane")
        s_lane_b = sem("lane_b")
        s_split = sem("split")
        s_split0 = sem("split_first")
        s_attr = sem("attr")
        s_turned = sem("turned")
        s_cols = sem("cols")
        s_ps_hidden = sem("ps_hidden")
        s_added = sem("hidden_added")
        s_hidden = sem("hidden")
        s_ps_sums = sem("ps_sums")
        s_sums = sem("sums")

        with nc.Block() as block:
            @block.sync
            def _(sp):
                def load(g, u, n):
                    if n >= 2:
                        sp.wait_ge(s_attr, g - 1)
                    sp.dma_start(raw[:, u, :, :], k.rec_b[at(g * G * P, G * P), 0:EA]
                                 .rearrange("(j p) r -> p j r", p=P)).then_inc(s_raw[u], 16)

                def groups(i, first):
                    if first:
                        load(0, 0, 0)
                    for u in range(2):
                        load(2 * i + u + 1, 1 - u, u + 1 if first else 2)
                rounds(sp, IT, groups)

            @block.gpsimd
            def _(pool):
                split = RoundChain(pool, s_split)

                def attributes(split, g, u, landed, n):
                    value = raw[:, u, :, :]
                    pool.wait_ge(s_raw[u], 16 * landed)
                    if n >= 2:
                        pool.wait_ge(s_turned, g - 1)
                    pool.sem_inc(s_go, 1)
                    for part in range(3):
                        pairs = [m for m in range(PAIRS) if A_PARTS[m] == part]
                        ins = nc.gpsimd.tensor_copy(attr[:, u, :, pairs[0]:pairs[-1] + 1, :],
                                                    value.unsqueeze(2).to_broadcast([P, G, len(pairs), EA]))
                        if part == 2:
                            ins.then_inc(s_attr, 1)
                            break
                        split(ins)
                        pool.sem_inc(s_go, 1)
                        split(nc.gpsimd.tensor_tensor(left[:, u, part, :, :], value, attr[:, u, :, pairs[0], :],
                                                      ALU.subtract))
                        pool.sem_inc(s_go, 1)
                        value = left[:, u, part, :, :]

                def groups(i, first):
                    split.start(i, first)
                    for u in range(2):
                        g = 2 * i + u
                        pool.wait_ge(s_idx, g + 1)
                        if not first:
                            pool.wait_ge(s_hidden, G * (g - 1))
                        pool.sem_inc(s_go, 1)
                        for j in range(G):
                            pool.indirect_dma_start(gathered[:, u, j, :], None, table,
                                                    bass.IndirectOffsetOnAxis(idx[:, u, j:j + 1], 0))\
                                .then_inc(s_landed[u], 16)
                        attributes(split, g + 1, 1 - u, i + 1 + u, u + 1 if first else 2)

                attributes(Chain(pool, s_split0), 0, 0, 1, 0)
                rounds(pool, IT, groups)

            @block.scalar
            def _(act):
                def narrow(g, u, n):
                    act.wait_ge(s_lane, g + 1)
                    if n >= 2:
                        act.wait_ge(s_turned, g - 1)
                    nc.scalar.copy(is_lane_b[:, u, :, :], is_lane[:, u, :, :]).then_inc(s_lane_b, 1)

                def columns(g, u, n):
                    act.wait_ge(s_turned, g + 1)
                    if n >= 2:
                        act.wait_ge(s_ps_hidden, G * (g - 1))
                    nc.scalar.copy(lane_is[:, u, :, :], ps_lane[:, u, :, :])
                    nc.scalar.copy(attr_turned[:, u, :, :], ps_attr[:, u, :, :]).then_inc(s_cols, 1)

                def groups(i, first):
                    if first:
                        narrow(0, 0, 0)
                        columns(0, 0, 0)
                    for u in range(2):
                        g = 2 * i + u
                        n = u + 1 if first else 2
                        stage_index(nc, act, i, first, u, idx, k.dst_at, s_landed, s_idx)
                        for j in range(G):
                            act.wait_ge(s_added, G * g + j + 1)
                            if not first:
                                act.wait_ge(s_ps_sums, G * (g - 2) + j + 1)
                            nc.scalar.activation(hidden[:, u, j, :], gathered[:, u, j, :], ACT.Relu).then_inc(s_hidden, 1)
                            if j == 1:
                                narrow(g + 1, 1 - u, n)
                            if j == 2:
                                columns(g + 1, 1 - u, n)
                rounds(act, IT, groups)

            @block.tensor
            def _(pe):
                def turn(g, u, n):
                    pe.wait_ge(s_lane_b, g + 1)
                    pe.wait_ge(s_attr, g + 1)
                    if n >= 2:
                        pe.wait_ge(s_cols, g - 1)
                    for j in range(G):
                        nc.tensor.transpose(ps_lane[:, u, j, :], is_lane_b[:, u, j, :], k.ident_b[:, :])
                        ins = nc.tensor.transpose(ps_attr[:, u, j, :], attr[:, u, j, :, :].rearrange("p n a -> p (n a)"),
                                                  k.ident_b[:, :])
                    ins.then_inc(s_turned, 1)

                def product(g, u, j, tile, first):
                    if not (first and u == 0 and j < 2):
                        pe.wait_ge(s_added, g * G + j - 1)
                    for part in range(3):
                        nc.tensor.matmul(ps_hidden[:, j % 2, :], lane_is[:, u, j, :], parts[:, at(tile, 1), part, :],
                                         start=(part == 0), stop=False)
                    nc.tensor.matmul(ps_hidden[:, j % 2, :], attr_turned[:, u, j, :], k.w_attr[:, :],
                                     start=False, stop=True).then_inc(s_ps_hidden, 1)

                def add(g, u, j, begin):
                    c = g * G + j
                    pe.wait_ge(s_hidden, c + 1)
                    if not (begin and j < 2):
                        pe.wait_ge(s_sums, c - 1)
                    nc.tensor.matmul(ps_sums[:, j % 2, :], is_lane[:, u, j, :], hidden[:, u, j, :], start=True,
                                     stop=True).then_inc(s_ps_sums, 1)

                def groups(i, first):
                    if first:
                        turn(0, 0, 0)
                    for u in range(2):
                        g = 2 * i + u
                        tiles = tile_registers(nc, mybir.EngineType.PE, k.tile_ib, g * G, G)
                        pe.wait_ge(s_cols, g + 1)
                        for j in range(G):
                            product(g, u, j, tiles[j], first)
                            if j >= 2:
                                add(g, u, j - 2, first and u == 0)
                            elif not (first and u == 0):
                                add(g - 1, 1 - u, j + 2, False)
                            if j == 2:
                                turn(g + 1, 1 - u, u + 1 if first else 2)
                rounds(pe, IT, groups)
                for j in range(2, G):
                    add(2 * IT - 1, 1, j, False)

            @block.vector
            def _(dve):
                nc.vector.memset(sums[:, :, :], 0.0).then_inc(s_zero, 1)
                dve.wait_ge(s_zero, 1)

                def lanes(g, u, n):
                    if n >= 2:
                        dve.wait_ge(s_ps_sums, G * (g - 1))
                        dve.wait_ge(s_lane_b, g - 1)
                    nc.vector.tensor_tensor(is_lane[:, u, :, :], k.lane[:, :].unsqueeze(1).to_broadcast([P, G, P]),
                                            k.lane_b[:, at(g * G, G)].unsqueeze(2).to_broadcast([P, G, P]),
                                            ALU.is_equal).then_inc(s_lane, 1)

                def add(g, j, tile, begin):
                    c = g * G + j
                    dve.wait_ge(s_ps_sums, c + 1)
                    if not (begin and j == 0):
                        dve.wait_ge(s_sums, c)
                    to = tile_ap(sums, tile)
                    nc.vector.tensor_tensor(to, to, ps_sums[:, j % 2, :], ALU.add).then_inc(s_sums, 1)

                def groups(i, first):
                    if first:
                        lanes(0, 0, 0)
                    for u in range(2):
                        g = 2 * i + u
                        begin = first and u == 0
                        if not begin:
                            before = tile_registers(nc, mybir.EngineType.DVE, k.tile_ib, g * G - 2, 2)
                        tiles = tile_registers(nc, mybir.EngineType.DVE, k.tile_ib, g * G, 2)
                        dve.wait_ge(s_landed[u], 16 * G * (i + 1))
                        for j in range(G):
                            dve.wait_ge(s_ps_hidden, G * g + j + 1)
                            nc.vector.tensor_tensor(gathered[:, u, j, :], gathered[:, u, j, :], ps_hidden[:, j % 2, :],
                                                    ALU.add).then_inc(s_added, 1)
                            if j >= 2:
                                add(g, j - 2, tiles[j - 2], begin)
                            elif not begin:
                                add(g - 1, j + 2, before[j], False)
                            if j == 1:
                                lanes(g + 1, 1 - u, u + 1 if first else 2)
                rounds(dve, IT, groups)
                tiles = tile_registers(nc, mybir.EngineType.DVE, k.tile_ib, NC - 2, 2)
                for j in range(2, G):
                    add(2 * IT - 1, j, tiles[j - 2], False)


@phase
def load_phase(nc, new_semaphore, name, pairs):
    s = new_semaphore(name)
    with nc.Block() as block:
        @block.sync
        def _(sp):
            for to, source in pairs:
                sp.dma_start(to, source).then_inc(s, 16)
            sp.wait_ge(s, 16 * len(pairs))


class Names:
    pass


_IN = ['x', 'src', 'dst', 'edge_attr_16', 'edge_weight', 'edge_weight1', 'L0_gnn_W', 'L0_gnn_bias', 'L1_gnn_Wq',
       'L1_gnn_bq', 'L1_gnn_Wk', 'L1_gnn_bk', 'L1_gnn_Wv', 'L1_gnn_bv', 'L1_gnn_Wo', 'L1_gnn_bo', 'L2_gnn_W',
       'L2_gnn_att_src', 'L2_gnn_att_dst', 'L2_gnn_bias', 'L2_gnn_gamma', 'L2_gnn_beta', 'L3_gnn_mW1', 'L3_gnn_mb1',
       'L3_gnn_mW2', 'L3_gnn_mb2', 'L3_gnn_uW1', 'L3_gnn_ub1', 'L3_gnn_uW2', 'L3_gnn_ub2']


def gnn_layers_kernel(nc, a, out):
    resting.clear()
    with ExitStack() as ctx:
        k = Names()
        k.x_in, k.src, k.dst = a['x'], a['src'], a['dst']
        k.edge_attr, k.edge_weight = a['edge_attr_16'], a['edge_weight']

        def table(name, width):
            return nc.dram_tensor(name, (NP, width), F32).ap()

        k.by_dst_src = nc.dram_tensor("by_dst_src", (E + P, 1), I32).ap()
        k.by_dst_dst = nc.dram_tensor("by_dst_dst", (E + P, 1), I32).ap()
        k.pairs = nc.dram_tensor("pairs_sorted", (E, 2), I32).ap()
        k.keys = nc.dram_tensor("keys_in_row", (NCB * P + 2,), F32).ap()
        k.rec_b = nc.dram_tensor("rec_b", ((NC + G) * P, RB), F32).ap()
        h_table, key_table, value_table = table("h_table", D), table("key_table", D), table("value_table", D)
        xl_table, h3_table, dst_table = table("xl_table", D), table("h3_table", D), table("dst_table", HID)
        k.of_src_table, x_table = table("of_src_table", H), table("x_table", D)

        def sb(name, shape, dt=F32, to=ctx):
            return to.enter_context(nc.sbuf_tensor(name, shape, dt))

        k.x = sb("x_nodes", [P, T, D])
        k.ident = sb("ident", [P, P])
        k.ident_b = sb("ident_b", [P, P], BF16)
        k.lane = sb("lane", [P, P])
        k.tile_ia = sb("tile_ia", [1, NC], I32)
        k.tile_ib = sb("tile_ib", [1, NC], I32)
        k.dst_at = sb("dst_at", [P, NC + G], I32)
        k.lane_b = sb("lane_b", [P, NC + G])
        k.weight = sb("weight", [P, NC])
        degree = sb("degree", [P, T])
        k.rstd = sb("rstd", [P, T])
        k.shift = sb("shift", [P, T])

        def normed(eng_step, t, u, rows):
            return nc.scalar.activation(rows[:, 0:D], tile_ap(k.x, t), ACT.Relu, bias=k.shift[:, at(t, 1)],
                                        scale=k.rstd[:, at(t, 1)])

        with ExitStack() as mid:
            k.scores = sb("scores", [P, NCB, H], F32, mid)
            k.new_node = sb("new_node", [P, BC * P + 1], F32, mid)
            k.src_at = sb("src_at", [P, NC + G], I32, mid)
            k.lane_a = sb("lane_a", [P, NC + G], F32, mid)
            k.w0, k.wo, k.w2 = (sb(n, [P, KC, D], F32, mid) for n in ("w0", "wo", "w2"))
            k.wqkv = sb("wqkv", [P, KC, 3 * D], F32, mid)
            k.b0, k.bo, k.b2, k.gamma, k.beta, k.att_src, k.att_dst = (
                sb(n, [P, D], F32, mid) for n in ("b0", "bo", "b2", "gamma", "beta", "att_src", "att_dst"))
            k.bqkv = sb("bqkv", [P, 3 * D], F32, mid)
            with ExitStack() as edges:
                def eb(name, shape, dt=F32):
                    return sb(name, shape, dt, edges)

                k.src_i, k.dst_i, k.next_i = (eb(n, [EP, EC], I32) for n in ("src_i", "dst_i", "next_i"))
                k.pos_b, k.fields_b = eb("pos_b", [EP, EC], I32), eb("fields_b", [EP, EC, RB])
                k.ones, k.before, k.minus = eb("ones", [P, P]), eb("before", [P, P]), eb("minus", [1, P], I32)
                k.tile_ids, k.chunk_ids, k.chunk_of_row = eb("tile_ids", [P, TR]), eb("chunk_ids", [1, NC]), eb("chunk_of_row", [CR, CQ])
                k.zeros_t, k.ends_b = eb("zeros_t", [P, TR]), eb("ends_b", [P, TR])
                k.node_of_row, k.start_of_row = eb("node_of_row", [CR, CQ]), eb("start_of_row", [CR, CQ], I32)
                k.disorder = eb("disorder", [1, 1], I32)
                setup_phase(nc, k)
                scatter_phase(nc, k, a)
                sort_by_dst_phase(nc, k)
                load_orders_phase(nc, k, h_table)

            with ExitStack() as layer:
                sums = sb("sums0", [P, T, D + 1], F32, layer)
                sum_phase(nc, k, "l0", h_table, sums, heads=False)

                def copy_rows(step, t, u, rows):
                    return nc.scalar.copy(rows, sums[:, at(t, 1), 0:D].rearrange("p o d -> p (o d)"))

                def keep_degree(step):
                    step(nc.vector.tensor_copy(degree[:, :], sums[:, :, D]))

                def add_relu(step, t, ps, slot, spare):
                    step(nc.vector.tensor_tensor(spare[:, 0, 0:D], ps, k.b0[:, :], ALU.add))
                    return nc.vector.scalar_tensor_tensor(tile_ap(k.x, t), spare[:, 0, 0:D], 0.0, tile_ap(k.x, t),
                                                          ALU.max, ALU.add)
                project_phase(nc, k, "p0", KC, D, k.w0, copy_rows, add_relu, setup=keep_degree)

            norm_stats(nc, k, "n1", k.x)
            with ExitStack() as layer:
                query = sb("query_parts", [P, T, 3, D], BF16, layer)

                def query_key_value(step, t, ps, slot, spare):
                    step(nc.vector.tensor_tensor(slot, ps, k.bqkv[:, :], ALU.add))
                    return split_parts(nc, step, query, t, slot[:, 0:D], spare[:, 0, 0:D])
                project_phase(nc, k, "p1", KC, 3 * D, k.wqkv, normed, query_key_value,
                              store=lambda t, slot: [(rows_of(key_table, t), slot[:, D:2 * D]),
                                                     (rows_of(value_table, t), slot[:, 2 * D:3 * D])])
                score_phase(nc, k, "s1", key_table, D, query)
            weights_of_edges_phase(nc, k, "m1", C ** -0.5)
            with ExitStack() as layer:
                sums1 = sb("sums1", [P, T, D + H], F32, layer)
                inverse = sb("inverse1", [P, T, H], F32, layer)
                sum_phase(nc, k, "l1", value_table, sums1, heads=True)

                def inverses(step):
                    step(nc.vector.tensor_scalar(inverse[:, :, :], sums1[:, :, D:D + H], 0.0, None, ALU.is_equal))
                    step(nc.vector.tensor_tensor(inverse[:, :, :], inverse[:, :, :], sums1[:, :, D:D + H], ALU.add))
                    step(nc.vector.reciprocal(inverse[:, :, :], inverse[:, :, :]))

                def divide(step, t, u, rows):
                    return nc.vector.tensor_tensor(
                        rows.rearrange("p (h c) -> p h c", h=H),
                        sums1[:, at(t, 1), 0:D].rearrange("p o (h c) -> p (o h) c", h=H),
                        inverse[:, at(t, 1), :].rearrange("p o h -> p (o h)").unsqueeze(2).to_broadcast([P, H, C]),
                        ALU.mult)

                def add_to_x(step, t, ps, slot, spare):
                    step(nc.vector.tensor_tensor(spare[:, 0, 0:D], ps, k.bo[:, :], ALU.add))
                    return nc.vector.tensor_tensor(tile_ap(k.x, t), tile_ap(k.x, t), spare[:, 0, 0:D], ALU.add)
                project_phase(nc, k, "p2", KC, D, k.wo, divide, add_to_x, prepare_on="dve", setup=inverses)

            norm_stats(nc, k, "n2", k.x)
            with ExitStack() as layer:
                k.xl = sb("xl", [P, T, D], F32, layer)
                k.of_src, k.of_dst = sb("of_src", [P, T, H], F32, layer), sb("of_dst", [P, T, H], F32, layer)
                k.of_dst_parts = sb("of_dst_parts", [P, T, 3, H], BF16, layer)

                def rows_and_logits(step, t, ps, slot, spare):
                    step(nc.vector.tensor_copy(slot[:, 0:D], ps))
                    step(nc.vector.tensor_copy(tile_ap(k.xl, t), ps))
                    step(nc.vector.tensor_tensor(spare[:, 0, 0:D], slot[:, 0:D], k.att_src[:, :], ALU.mult))
                    step(nc.vector.tensor_tensor(spare[:, 1, 0:D], slot[:, 0:D], k.att_dst[:, :], ALU.mult))
                    step(nc.vector.tensor_reduce(tile_ap(k.of_src, t), spare[:, 0, 0:D].rearrange("p (h c) -> p h c", h=H),
                                                 AX_X, ALU.add))
                    return nc.vector.tensor_reduce(tile_ap(k.of_dst, t),
                                                   spare[:, 1, 0:D].rearrange("p (h c) -> p h c", h=H), AX_X, ALU.add)
                project_phase(nc, k, "p3", KC, D, k.w2, normed, rows_and_logits,
                              store=lambda t, slot: [(rows_of(xl_table, t), slot[:, 0:D])])
                logit_parts_phase(nc, k)
                score_phase(nc, k, "s2", k.of_src_table, H, k.of_dst_parts)
                largest = sb("largest2", [P, NCB, H], F32, layer)
                weights_of_edges_phase(nc, k, "m2", 1.0, last=largest)
                sums2 = sb("sums2", [P, T, D + 2 * H], F32, layer)
                sum_phase(nc, k, "l2", xl_table, sums2, heads=True, last=largest)
                combine_loops_phase(nc, k, sums2)
                norm_stats(nc, k, "n3", k.xl)
                norm_of_layer_phase(nc, k)

        norm_stats(nc, k, "n4", k.x)
        with ExitStack() as layer:
            sums3 = sb("sums3", [P, T, HID], F32, layer)
            with ExitStack() as message:
                k.w_attr = sb("w_attr", [P, HID], BF16, message)
                parts = sb("src_parts", [P, T, 3, HID], BF16, message)
                with ExitStack() as weights:
                    k.w_node = sb("w_node", [P, KC, 2 * HID], F32, weights)
                    k.b_m1 = sb("b_m1", [P, HID], F32, weights)
                    attribute_weights_phase(nc, k, a)

                    def hidden_parts(step, t, ps, slot, spare):
                        step(nc.vector.tensor_copy(slot[:, 0:HID], ps[:, HID:2 * HID]))
                        step(nc.vector.tensor_tensor(spare[:, 0, :], ps[:, 0:HID], k.b_m1[:, :], ALU.add))
                        return split_parts(nc, step, parts, t, spare[:, 0, :], spare[:, 1, :])
                    project_phase(nc, k, "p4", KC, 2 * HID, k.w_node, normed, hidden_parts,
                                  keep=lambda t: rows_of(h3_table, t),
                                  store=lambda t, slot: [(rows_of(dst_table, t), slot[:, 0:HID])])
                load_phase(nc, "s_x_out", [(x_table.rearrange("(t p) d -> p t d", p=P), k.x[:, :, :])])
                message_phase(nc, k, dst_table, parts, sums3)

            h3 = sb("h3", [P, T, D], F32, layer)
            received = sb("received", [P, T, D], F32, layer)
            w_m2, w_u1 = sb("w_m2", [P, HID // P, D], F32, layer), sb("w_u1", [P, HID // P, HID], F32, layer)
            w_u2 = sb("w_u2", [P, HID // P, D], F32, layer)
            b_m2, b_u1, b_u2 = (sb(n, [P, w], F32, layer) for n, w in (("b_m2", D), ("b_u1", HID), ("b_u2", D)))
            load_phase(nc, "s_update_loads", [
                (k.x[:, :, :], x_table.rearrange("(t p) d -> p t d", p=P)),
                (h3[:, :, :], h3_table.rearrange("(t p) d -> p t d", p=P)),
                (w_m2[:, :, :], a['L3_gnn_mW2'].rearrange("(b p) n -> p b n", p=P)),
                (w_u1[:, :, :], a['L3_gnn_uW1'].rearrange("(b p) n -> p b n", p=P)),
                (w_u2[:, :, :], a['L3_gnn_uW2'].rearrange("(b p) n -> p b n", p=P)),
                (b_m2[:, :], a['L3_gnn_mb2'].partition_broadcast(P)), (b_u1[:, :], a['L3_gnn_ub1'].partition_broadcast(P)),
                (b_u2[:, :], a['L3_gnn_ub2'].partition_broadcast(P))])

            def copy_sums(step, t, u, rows):
                return nc.scalar.copy(rows, tile_ap(sums3, t))

            def messages(step, t, ps, slot, spare):
                return nc.vector.scalar_tensor_tensor(tile_ap(received, t), b_m2[:, :], degree[:, at(t, 1)], ps,
                                                      ALU.mult, ALU.add)
            project_phase(nc, k, "p5", HID // P, D, w_m2, copy_sums, messages)

            def node_and_received(step, t, u, rows):
                step(nc.scalar.copy(rows[:, 0:D], tile_ap(h3, t)))
                return nc.scalar.copy(rows[:, D:2 * D], tile_ap(received, t))

            def update_hidden(step, t, ps, slot, spare):
                step(nc.vector.tensor_tensor(spare[:, 0, :], ps, b_u1[:, :], ALU.add))
                return nc.vector.tensor_scalar(tile_ap(sums3, t), spare[:, 0, :], 0.0, None, ALU.max)
            project_phase(nc, k, "p6", HID // P, HID, w_u1, node_and_received, update_hidden)

            def update(step, t, ps, slot, spare):
                step(nc.vector.tensor_tensor(spare[:, 0, 0:D], ps, b_u2[:, :], ALU.add))
                step(nc.vector.tensor_tensor(spare[:, 1, 0:D], spare[:, 0, 0:D], tile_ap(h3, t), ALU.add))
                return nc.vector.tensor_tensor(tile_ap(k.x, t), tile_ap(k.x, t), spare[:, 1, 0:D], ALU.add)
            project_phase(nc, k, "p7", HID // P, D, w_u2, copy_sums, update)
            finish_x(nc, k, out)


def finish_x(nc, k, out):
    load_phase(nc, "s_out", [
        (out[0:(TR - 1) * P, :].rearrange("(t p) d -> p t d", p=P), k.x[:, 0:TR - 1, :]),
        (out[(TR - 1) * P:N, :], k.x[0:LAST, TR - 1, :])])


def kernel(**inputs):
    import numpy as _np
    import concourse.bacc as _bacc
    from concourse import mybir as _mybir
    from concourse.bass_utils import run_bass_kernel_spmd as _run

    nc = _bacc.Bacc("TRN2", target_bir_lowering=False, num_devices=1)
    arrays, args = {}, {}
    for name in _IN:
        v = _np.ascontiguousarray(inputs[name])
        arrays[f"in_{name}"] = v
        args[name] = nc.dram_tensor(f"in_{name}", v.shape, _mybir.dt.from_np(v.dtype), kind="ExternalInput").ap()
    out = nc.dram_tensor("x_out", (N, D), F32, kind="ExternalOutput").ap()
    gnn_layers_kernel(nc, args, out)
    r = _run(nc, [arrays], core_ids=[0])
    return r.results[0]["x_out"]
```
